# Optimizing a Trainium2 kernel written in Bass

```python
import numpy as np
import jax
import jax.numpy as jnp

def _softmax(x, axis=-1):
    return jax.nn.softmax(x, axis=axis)

def _gelu(x):
    return jax.nn.gelu(x, approximate=True)

def _silu(x):
    return jax.nn.silu(x)

def _sigmoid(x):
    return jax.nn.sigmoid(x)

def _layernorm(x, axis=-1, eps=1e-05):
    m = jnp.mean(x, axis=axis, keepdims=True)
    v = jnp.var(x, axis=axis, keepdims=True)
    return (x - m) / jnp.sqrt(v + eps)

def _scatter_add(tgt, idx, src, axis=0):
    return tgt.at[idx].add(src)

def _segment_sum(src, seg, n):
    return jax.ops.segment_sum(src, seg, n)
kernel_name = 'mk_xattn_ffn_d2_seqx_r4_6bf1f6'

def setup_inputs(seed: int=0):
    np.random.seed(seed)
    _w = jnp.asarray

    def _rec_inputs():
        import jax
        import jax.numpy as jnp
        _rk = jax.random.key(seed)
        x = -0.0002928 + 1 * jax.random.normal(jax.random.fold_in(_rk, 1), (16, 128, 512), jnp.float32)
        _lenS = 128 - jax.random.randint(jax.random.fold_in(_rk, 7), (16,), 0, max(1, 128 // 4) + 1, jnp.int32)
        _lenS2 = 128 - jax.random.randint(jax.random.fold_in(_rk, 8), (16,), 0, max(1, 128 // 4) + 1, jnp.int32)
        _ctx_2048P = jax.random.normal(jax.random.fold_in(_rk, 11), (16, 16, 512), jnp.float32)
        _ctx_2048c = jax.random.dirichlet(jax.random.fold_in(_rk, 511), 0.3 * jnp.ones((16,), jnp.float32), (16, 128))
        _ctx_2048t = jnp.einsum('bsk,bkd->bsd', _ctx_2048c, _ctx_2048P)
        _ctx_2048t = _ctx_2048t * jax.lax.rsqrt(jnp.mean(jnp.square(_ctx_2048t)) + 1e-12) * 0.953939
        ctx_2048 = -1.39393e-06 + 0.999914 * (_ctx_2048t + 0.3 * jax.random.normal(jax.random.fold_in(_rk, 611), (16, 128, 512), jnp.float32))
        return (x, ctx_2048)
    x, ctx_2048 = _rec_inputs()

    def _L0_xattn_setup():
        import jax, jax.numpy as jnp
        import numpy as np
        B, S, E, NH = (2, 256, 512, 16)
        DH = E // NH
        EPS = 1e-06

        def _mlstm_forward(q, k, v, Wi, bi, Wf, bf, ln_scale):
            b, s, e = q.shape
            nh = Wi.shape[1]
            dh = e // nh
            x = jnp.concatenate([q, k, v], axis=-1)
            ig = (x @ Wi + bi).transpose(0, 2, 1)[..., None]
            fg = (x @ Wf + bf).transpose(0, 2, 1)[..., None]
            split = lambda t: t.reshape(b, s, nh, dh).transpose(0, 2, 1, 3)
            qh, kh, vh = (split(q), split(k), split(v))
            log_f = jax.nn.log_sigmoid(fg)
            log_f_cum = jnp.concatenate([jnp.zeros((b, nh, 1, 1), q.dtype), jnp.cumsum(log_f, axis=2)], axis=2)
            fg_mat = log_f_cum - jnp.transpose(log_f_cum, (0, 1, 3, 2))
            ltr = jnp.tril(jnp.ones((s, s), dtype=bool))
            log_fg = jnp.where(ltr, fg_mat[:, :, 1:, 1:], -jnp.inf)
            log_D = log_fg + jnp.transpose(ig, (0, 1, 3, 2))
            max_log_D = jnp.max(log_D, axis=-1, keepdims=True)
            D = jnp.exp(log_D - max_log_D)
            qk = jnp.einsum('bhsd,bhtd->bhst', qh, kh) / jnp.sqrt(jnp.asarray(dh, q.dtype))
            C = qk * D
            normalizer = jnp.maximum(jnp.abs(C.sum(-1, keepdims=True)), jnp.exp(-max_log_D))
            Cn = C / (normalizer + EPS)
            h = jnp.einsum('bhst,bhtd->bhsd', Cn, vh)
            mu = h.mean(-1, keepdims=True)
            var = ((h - mu) ** 2).mean(-1, keepdims=True)
            hn = (h - mu) * jax.lax.rsqrt(var + EPS)
            hn = hn * ln_scale.reshape(1, nh, 1, dh)
            return hn.transpose(0, 2, 1, 3).reshape(b, s, e)
        key = jax.random.key(seed)
        ks = jax.random.split(key, 6)
        q = jax.random.normal(ks[0], (B, S, E), dtype=jnp.float32)
        k = jax.random.normal(ks[1], (B, S, E), dtype=jnp.float32)
        v = jax.random.normal(ks[2], (B, S, E), dtype=jnp.float32)
        Wi = jax.random.normal(ks[3], (3 * E, NH), dtype=jnp.float32) * 0.02
        bi = jax.random.normal(ks[4], (NH,), dtype=jnp.float32) * 0.1
        Wf = jax.random.normal(ks[5], (3 * E, NH), dtype=jnp.float32) * 0.02
        bf = jnp.linspace(3.0, 6.0, NH, dtype=jnp.float32)
        ln_scale = jnp.ones((E,), dtype=jnp.float32)
        return {'q': q, 'k': k, 'v': v, 'Wi': Wi, 'bi': bi, 'Wf': Wf, 'bf': bf, 'ln_scale': ln_scale}
    _L0_xattn_all = _L0_xattn_setup()
    _L0_xattn_in = {k: v for k, v in _L0_xattn_all.items() if k in ('Wi', 'bi', 'Wf', 'bf', 'ln_scale')}
    del _L0_xattn_all

    def _L0_ffn_setup():
        import jax, jax.numpy as jnp
        import numpy as np
        B, S, D = (4, 512, 512)
        E, F, K = (8, 256, 2)
        SF = 256
        EPS = 1e-06

        def _rmsnorm(x, w, eps=EPS):
            var = jnp.mean(x * x, axis=-1, keepdims=True)
            return x * jax.lax.rsqrt(var + eps) * w
        key = jax.random.key(seed)
        ks = jax.random.split(key, 9)
        g = lambda k, shape, scale: jax.random.normal(k, shape, jnp.float32) * scale
        return {'x': g(ks[0], (B, S, D), 1.0), 'rms_weight': jnp.ones((D,), jnp.float32), 'router_w': g(ks[1], (D, E), 0.02), 'w_gate': g(ks[2], (E, D, F), 0.02), 'w_up': g(ks[3], (E, D, F), 0.02), 'w_down': g(ks[4], (E, F, D), 0.02), 'sw_gate': g(ks[5], (D, SF), 0.02), 'sw_up': g(ks[6], (D, SF), 0.02), 'sw_down': g(ks[7], (SF, D), 0.02)}
    _L0_ffn_all = _L0_ffn_setup()
    _L0_ffn_in = {k: v for k, v in _L0_ffn_all.items() if k in ('rms_weight', 'router_w', 'w_gate', 'w_up', 'w_down', 'sw_gate', 'sw_up', 'sw_down')}
    del _L0_ffn_all

    def _L1_xattn_setup():
        import jax, jax.numpy as jnp
        import numpy as np
        DIM = 512
        H = 16
        D = 128
        INNER = H * D
        N_IMG = 257
        EPS = 1e-06

        def rms_norm(x, scale, eps=EPS):
            ms = jnp.mean(jnp.square(x), axis=-1, keepdims=True)
            return x * jax.lax.rsqrt(ms + eps) * scale

        def sdpa(q, k, v):
            scale = 1.0 / jnp.sqrt(jnp.asarray(D, q.dtype))
            scores = jnp.einsum('bshd,blhd->bhsl', q, k) * scale
            attn = jax.nn.softmax(scores, axis=-1)
            return jnp.einsum('bhsl,blhd->bshd', attn, v)
        key = jax.random.key(seed)
        ks = jax.random.split(key, 16)
        std = 1.0 / np.sqrt(DIM)
        inp = {'x': jax.random.normal(ks[0], (2, 1024, DIM), jnp.float32), 'context': jax.random.normal(ks[1], (2, 769, DIM), jnp.float32), 'q_w': jax.random.normal(ks[2], (DIM, INNER), jnp.float32) * std, 'q_b': jnp.zeros((INNER,), jnp.float32), 'k_w': jax.random.normal(ks[3], (DIM, INNER), jnp.float32) * std, 'k_b': jnp.zeros((INNER,), jnp.float32), 'v_w': jax.random.normal(ks[4], (DIM, INNER), jnp.float32) * std, 'v_b': jnp.zeros((INNER,), jnp.float32), 'ki_w': jax.random.normal(ks[5], (DIM, INNER), jnp.float32) * std, 'ki_b': jnp.zeros((INNER,), jnp.float32), 'vi_w': jax.random.normal(ks[6], (DIM, INNER), jnp.float32) * std, 'vi_b': jnp.zeros((INNER,), jnp.float32), 'o_w': jax.random.normal(ks[7], (INNER, DIM), jnp.float32) * std, 'o_b': jnp.zeros((DIM,), jnp.float32), 'nq_s': jnp.ones((INNER,), jnp.float32), 'nkt_s': jnp.ones((INNER,), jnp.float32), 'nki_s': jnp.ones((INNER,), jnp.float32)}
        return inp
    _L1_xattn_all = _L1_xattn_setup()
    _L1_xattn_in = {k: v for k, v in _L1_xattn_all.items() if k in ('q_w', 'q_b', 'k_w', 'k_b', 'v_w', 'v_b', 'ki_w', 'ki_b', 'vi_w', 'vi_b', 'o_w', 'o_b', 'nq_s', 'nkt_s', 'nki_s')}
    del _L1_xattn_all

    def _L1_ffn_setup():
        import jax, jax.numpy as jnp
        import numpy as np
        B, S, D_IN, D_OUT = (4, 512, 512, 512)
        EPS = 1e-10
        key = jax.random.key(seed)
        kx, kw, kb = jax.random.split(key, 3)
        x = jax.random.normal(kx, (B, S, D_IN), dtype=jnp.float32)
        weight = jax.random.normal(kw, (D_OUT, D_IN), dtype=jnp.float32) * 0.02
        bias = jax.random.normal(kb, (D_OUT,), dtype=jnp.float32) * 0.02
        return {'x': x, 'weight': weight, 'bias': bias}
    _L1_ffn_all = _L1_ffn_setup()
    _L1_ffn_in = {k: v for k, v in _L1_ffn_all.items() if k in ('weight', 'bias')}
    del _L1_ffn_all
    return {'x': x, 'ctx_2048': ctx_2048, 'L0_xattn_Wi': _L0_xattn_in['Wi'], 'L0_xattn_bi': _L0_xattn_in['bi'], 'L0_xattn_Wf': _L0_xattn_in['Wf'], 'L0_xattn_bf': _L0_xattn_in['bf'], 'L0_xattn_ln_scale': _L0_xattn_in['ln_scale'], 'L0_ffn_rms_weight': _L0_ffn_in['rms_weight'], 'L0_ffn_router_w': _L0_ffn_in['router_w'], 'L0_ffn_w_gate': _L0_ffn_in['w_gate'], 'L0_ffn_w_up': _L0_ffn_in['w_up'], 'L0_ffn_w_down': _L0_ffn_in['w_down'], 'L0_ffn_sw_gate': _L0_ffn_in['sw_gate'], 'L0_ffn_sw_up': _L0_ffn_in['sw_up'], 'L0_ffn_sw_down': _L0_ffn_in['sw_down'], 'L1_xattn_q_w': _L1_xattn_in['q_w'], 'L1_xattn_q_b': _L1_xattn_in['q_b'], 'L1_xattn_k_w': _L1_xattn_in['k_w'], 'L1_xattn_k_b': _L1_xattn_in['k_b'], 'L1_xattn_v_w': _L1_xattn_in['v_w'], 'L1_xattn_v_b': _L1_xattn_in['v_b'], 'L1_xattn_ki_w': _L1_xattn_in['ki_w'], 'L1_xattn_ki_b': _L1_xattn_in['ki_b'], 'L1_xattn_vi_w': _L1_xattn_in['vi_w'], 'L1_xattn_vi_b': _L1_xattn_in['vi_b'], 'L1_xattn_o_w': _L1_xattn_in['o_w'], 'L1_xattn_o_b': _L1_xattn_in['o_b'], 'L1_xattn_nq_s': _L1_xattn_in['nq_s'], 'L1_xattn_nkt_s': _L1_xattn_in['nkt_s'], 'L1_xattn_nki_s': _L1_xattn_in['nki_s'], 'L1_ffn_weight': _L1_ffn_in['weight'], 'L1_ffn_bias': _L1_ffn_in['bias']}

def reference(x, ctx_2048, L0_xattn_Wi, L0_xattn_bi, L0_xattn_Wf, L0_xattn_bf, L0_xattn_ln_scale, L0_ffn_rms_weight, L0_ffn_router_w, L0_ffn_w_gate, L0_ffn_w_up, L0_ffn_w_down, L0_ffn_sw_gate, L0_ffn_sw_up, L0_ffn_sw_down, L1_xattn_q_w, L1_xattn_q_b, L1_xattn_k_w, L1_xattn_k_b, L1_xattn_v_w, L1_xattn_v_b, L1_xattn_ki_w, L1_xattn_ki_b, L1_xattn_vi_w, L1_xattn_vi_b, L1_xattn_o_w, L1_xattn_o_b, L1_xattn_nq_s, L1_xattn_nkt_s, L1_xattn_nki_s, L1_ffn_weight, L1_ffn_bias):
    import jax
    import jax.numpy as jnp

    def _L0_xattn_ref(q, k, v, Wi, bi, Wf, bf, ln_scale):
        import jax, jax.numpy as jnp
        import numpy as np
        B, S, E, NH = (2, 256, 512, 16)
        DH = E // NH
        EPS = 1e-06

        def _mlstm_forward(q, k, v, Wi, bi, Wf, bf, ln_scale):
            b, s, e = q.shape
            nh = Wi.shape[1]
            dh = e // nh
            x = jnp.concatenate([q, k, v], axis=-1)
            ig = (x @ Wi + bi).transpose(0, 2, 1)[..., None]
            fg = (x @ Wf + bf).transpose(0, 2, 1)[..., None]
            split = lambda t: t.reshape(b, s, nh, dh).transpose(0, 2, 1, 3)
            qh, kh, vh = (split(q), split(k), split(v))
            log_f = jax.nn.log_sigmoid(fg)
            log_f_cum = jnp.concatenate([jnp.zeros((b, nh, 1, 1), q.dtype), jnp.cumsum(log_f, axis=2)], axis=2)
            fg_mat = log_f_cum - jnp.transpose(log_f_cum, (0, 1, 3, 2))
            ltr = jnp.tril(jnp.ones((s, s), dtype=bool))
            log_fg = jnp.where(ltr, fg_mat[:, :, 1:, 1:], -jnp.inf)
            log_D = log_fg + jnp.transpose(ig, (0, 1, 3, 2))
            max_log_D = jnp.max(log_D, axis=-1, keepdims=True)
            D = jnp.exp(log_D - max_log_D)
            qk = jnp.einsum('bhsd,bhtd->bhst', qh, kh) / jnp.sqrt(jnp.asarray(dh, q.dtype))
            C = qk * D
            normalizer = jnp.maximum(jnp.abs(C.sum(-1, keepdims=True)), jnp.exp(-max_log_D))
            Cn = C / (normalizer + EPS)
            h = jnp.einsum('bhst,bhtd->bhsd', Cn, vh)
            mu = h.mean(-1, keepdims=True)
            var = ((h - mu) ** 2).mean(-1, keepdims=True)
            hn = (h - mu) * jax.lax.rsqrt(var + EPS)
            hn = hn * ln_scale.reshape(1, nh, 1, dh)
            return hn.transpose(0, 2, 1, 3).reshape(b, s, e)
        return _mlstm_forward(q, k, v, Wi, bi, Wf, bf, ln_scale)

    def _L0_ffn_ref(x, rms_weight, router_w, w_gate, w_up, w_down, sw_gate, sw_up, sw_down):
        import jax, jax.numpy as jnp
        import numpy as np
        B, S, D = (4, 512, 512)
        E, F, K = (8, 256, 2)
        SF = 256
        EPS = 1e-06

        def _rmsnorm(x, w, eps=EPS):
            var = jnp.mean(x * x, axis=-1, keepdims=True)
            return x * jax.lax.rsqrt(var + eps) * w
        b, s, d = x.shape
        e = router_w.shape[1]
        h = _rmsnorm(x, rms_weight)
        ht = h.reshape(-1, d)
        t = ht.shape[0]
        logits = ht @ router_w
        probs = jax.nn.softmax(logits, axis=-1)
        topv, topi = jax.lax.top_k(probs, K)
        topv = topv / jnp.sum(topv, axis=-1, keepdims=True)
        w_dense = jnp.zeros((t, e), ht.dtype).at[jnp.arange(t)[:, None], topi].set(topv)
        g = jnp.einsum('td,edf->tef', ht, w_gate)
        u = jnp.einsum('td,edf->tef', ht, w_up)
        eo = jnp.einsum('tef,efd->ted', jax.nn.silu(g) * u, w_down)
        moe = jnp.einsum('te,ted->td', w_dense, eo)
        sh = jax.nn.silu(ht @ sw_gate) * (ht @ sw_up) @ sw_down
        return (moe + sh).reshape(b, s, d)

    def _L1_xattn_ref(x, context, q_w, q_b, k_w, k_b, v_w, v_b, ki_w, ki_b, vi_w, vi_b, o_w, o_b, nq_s, nkt_s, nki_s):
        import jax, jax.numpy as jnp
        import numpy as np
        DIM = 512
        H = 16
        D = 128
        INNER = H * D
        N_IMG = 257
        EPS = 1e-06

        def rms_norm(x, scale, eps=EPS):
            ms = jnp.mean(jnp.square(x), axis=-1, keepdims=True)
            return x * jax.lax.rsqrt(ms + eps) * scale

        def sdpa(q, k, v):
            scale = 1.0 / jnp.sqrt(jnp.asarray(D, q.dtype))
            scores = jnp.einsum('bshd,blhd->bhsl', q, k) * scale
            attn = jax.nn.softmax(scores, axis=-1)
            return jnp.einsum('bhsl,blhd->bshd', attn, v)
        B, S, _ = x.shape
        img_ctx = context[:, :N_IMG]
        txt_ctx = context[:, N_IMG:]
        q = rms_norm(x @ q_w + q_b, nq_s).reshape(B, S, H, D)
        k_txt = rms_norm(txt_ctx @ k_w + k_b, nkt_s).reshape(B, -1, H, D)
        v_txt = (txt_ctx @ v_w + v_b).reshape(B, -1, H, D)
        out_txt = sdpa(q, k_txt, v_txt)
        k_img = rms_norm(img_ctx @ ki_w + ki_b, nki_s).reshape(B, -1, H, D)
        v_img = (img_ctx @ vi_w + vi_b).reshape(B, -1, H, D)
        out_img = sdpa(q, k_img, v_img)
        out = (out_txt + out_img).reshape(B, S, INNER)
        return out @ o_w + o_b

    def _L1_ffn_ref(x, weight, bias):
        import jax, jax.numpy as jnp
        import numpy as np
        B, S, D_IN, D_OUT = (4, 512, 512, 512)
        EPS = 1e-10
        scale = jnp.mean(jnp.abs(weight))
        w_t = jnp.clip(jnp.round(weight / (scale + EPS)), -1.0, 1.0)
        w_ste = weight + jax.lax.stop_gradient(w_t * scale - weight)
        return jnp.einsum('bsi,oi->bso', x, w_ste) + bias
    x = x + _L0_xattn_ref(_layernorm(x, axis=-1), ctx_2048, ctx_2048, L0_xattn_Wi, L0_xattn_bi, L0_xattn_Wf, L0_xattn_bf, L0_xattn_ln_scale)
    x = x + _L0_ffn_ref(_layernorm(x, axis=-1), L0_ffn_rms_weight, L0_ffn_router_w, L0_ffn_w_gate, L0_ffn_w_up, L0_ffn_w_down, L0_ffn_sw_gate, L0_ffn_sw_up, L0_ffn_sw_down)
    x = x + _L1_xattn_ref(_layernorm(x, axis=-1), ctx_2048, L1_xattn_q_w, L1_xattn_q_b, L1_xattn_k_w, L1_xattn_k_b, L1_xattn_v_w, L1_xattn_v_b, L1_xattn_ki_w, L1_xattn_ki_b, L1_xattn_vi_w, L1_xattn_vi_b, L1_xattn_o_w, L1_xattn_o_b, L1_xattn_nq_s, L1_xattn_nkt_s, L1_xattn_nki_s)
    x = x + _L1_ffn_ref(_layernorm(x, axis=-1), L1_ffn_weight, L1_ffn_bias)
    return x

_drawn_inputs = setup_inputs


def setup_inputs(seed=0):
    import zlib

    import numpy as np

    out = dict(_drawn_inputs(seed))
    spreads = {'L0_xattn_ln_scale': (1.0, 0.2),
     'L0_ffn_rms_weight': (1.0, 0.6),
     'L1_xattn_q_b': (0.0, 1.722),
     'L1_xattn_k_b': (0.0, 0.1),
     'L1_xattn_v_b': (0.0, 0.1),
     'L1_xattn_ki_b': (0.0, 2.0),
     'L1_xattn_vi_b': (0.0, 0.1),
     'L1_xattn_o_b': (0.0, 0.537),
     'L1_xattn_nq_s': (1.0, 0.6),
     'L1_xattn_nkt_s': (1.0, 0.2),
     'L1_xattn_nki_s': (1.0, 0.6)}
    factors = {'L0_xattn_bi': 64.0,
     'L0_ffn_router_w': 4.812,
     'L0_ffn_w_gate': 4.253,
     'L0_ffn_w_up': 4.162,
     'L0_ffn_w_down': 4.161,
     'L0_ffn_sw_gate': 3.058,
     'L0_ffn_sw_up': 2.977,
     'L0_ffn_sw_down': 2.997,
     'L1_ffn_bias': 18.969}
    for name, (base, spread) in spreads.items():
        noise = np.random.default_rng([zlib.crc32(name.encode()), seed]).standard_normal(out[name].shape)
        drawn = base * np.exp(spread * noise) if base else spread * noise
        out[name] = jnp.asarray(drawn.astype(out[name].dtype))
    for name, factor in factors.items():
        out[name] = (out[name] * factor).astype(out[name].dtype)
    return out
```

```python
from contextlib import ExitStack

import numpy as np

import concourse.bass as bass
from concourse import mybir

F32 = mybir.dt.float32
F32R = mybir.dt.float32r
BF16 = mybir.dt.bfloat16
U32 = mybir.dt.uint32
ALU = mybir.AluOpType
ACT = mybir.ActivationFunctionType
AX = mybir.AxisListType.X

P = 128
B, S, D = 16, 128, 512
T = B * S
C = D // P
GB = 4
G = B // GB
N = GB * S
H0, DH0 = 16, 32
E, F = 8, 256
FC = F // P
H1, DH1 = 16, 128
INNER = H1 * DH1
FAR = 1e30
FIRST = 1


class Own:

    def __init__(self, eng, sem):
        self.eng, self.sem, self.base, self.done, self.i, self.per = eng, sem, 0, 0, 0, 0

    def enter(self, i, per):
        self.base, self.done, self.i, self.per = self.base + self.done, 0, i, per

    def leave(self, trips):
        assert self.done == self.per, (self.done, self.per)
        self.base, self.done, self.i, self.per = self.base + trips * self.per, 0, 0, 0

    def __call__(self, ins):
        ins.then_inc(self.sem, 1)
        self.done += 1
        self.eng.wait_ge(self.sem, self.i * self.per + (self.base + self.done))


class Phase:

    def __init__(self, nc, name):
        self.nc, self.name, self.stack, self.sems = nc, name, ExitStack(), []

    def __enter__(self):
        self.stack.__enter__()
        return self

    def __exit__(self, *a):
        self.stack.__exit__(*a)
        if self.sems:
            self.nc.clear_and_free_semaphores(self.sems)
            self.nc.all_engine_barrier()

    def sb(self, name, shape, dt=F32):
        return self.stack.enter_context(self.nc.sbuf_tensor(f"{self.name}_{name}", shape, dt))

    def sem(self, name):
        self.sems.append(self.nc.alloc_semaphore(name=f"{self.name}_{name}"))
        return self.sems[-1]

    def hold(self, eng, sem):
        eng.sem_inc(sem, 1)

    def block(self):
        return self.stack.enter_context(self.nc.Block())


def within(nc, v, hi):
    return nc.s_assert_within(v, 0, hi, skip_runtime_bounds_check_because="the loop's count bounds it")


def three_passes(nc, out, lead_l, trail_l, lead_r, trail_r, first, last):
    nc.tensor.matmul(out, lead_l, lead_r, start=first, stop=False)
    nc.tensor.matmul(out, lead_l, trail_r, start=False, stop=False)
    return nc.tensor.matmul(out, trail_l, lead_r, start=False, stop=last)


def setup(nc, K, x_dram):
    with Phase(nc, "setup") as ph:
        x_loaded, blank, made = ph.sem("x_loaded"), ph.sem("blank"), ph.sem("made")
        block = ph.block()

        @block.sync
        def _(sp):
            sp.dma_start(K.x[:], x_dram.rearrange("b s d -> s b d")).then_inc(x_loaded, 16)
            sp.wait_ge(x_loaded, 16)

        @block.gpsimd
        def _(pool):
            nc.gpsimd.memset(K.ident[:], 0.0).then_inc(blank, 1)
            nc.gpsimd.memset(K.eps5[:], 1e-5)
            nc.gpsimd.memset(K.eps6[:], 1e-6)
            nc.gpsimd.memset(K.ones[:], 1.0).then_inc(blank, 1)
            pool.wait_ge(blank, 2)
            nc.gpsimd.affine_select(out=K.ident[:], in_=K.ident[:], compare_op=ALU.not_equal, fill=1.0,
                                    base=0, pattern=[[-1, P]], channel_multiplier=1).then_inc(made, 1)
            pool.wait_ge(made, 1)


def mlstm(nc, K, ctx_dram, Wi, bi, Wf, bf, ln_scale):
    UNITS = C
    with Phase(nc, "mlstm") as ph:
        sb, sem = ph.sb, ph.sem
        ctx = sb("ctx", [P, GB, D])
        xn = sb("xn", [P, GB, D])
        xnT = sb("xnT", [P, C, N])
        ctxT = sb("ctxT", [P, C, N])
        ctx1 = sb("ctx1", [P, GB, H0, DH0 + 1])
        w_gate = sb("w_gate", [P, 3, C, 64])
        w_ctx = sb("w_ctx", [P, C, 64])
        bias_i = sb("bias_i", [H0, 1])
        bias_f = sb("bias_f", [64, 1])
        stats = sb("stats", [P, GB, 6])
        mv = sb("mv", [P, GB, 2])
        rstd = sb("rstd", [P, GB])
        keep = sb("keep", [H0, GB, S])
        pen = sb("pen", [H0, GB, S])
        f_abs = sb("f_abs", [64, N])
        f_min = sb("f_min", [64, N])
        logf = sb("logf", [H0, N])
        cumf = sb("cumf", [H0, N])
        arow = sb("arow", [H0, N])
        grow = sb("grow", [H0, N])
        mrow = sb("mrow", [H0, N])
        nat = sb("nat", [P, 2, GB, H0])
        sel = sb("sel", [H0, H0, P])
        far = sb("far", [P, GB, S], BF16)
        ident_b = sb("ident_b", [P, P], BF16)
        arg = sb("arg", [P, 2, GB, S])
        dec = sb("dec", [P, 2, GB, S])
        cmat = sb("cmat", [P, 4, GB, S])
        hraw = sb("hraw", [P, GB, H0, DH0 + 1])
        hc = sb("hc", [P, GB * H0, DH0])
        sq = sb("sq", [P, GB * H0, DH0])
        small = sb("small", [P, 6, GB * H0])
        lnb = sb("lnb", [P, D])

        loaded_w, loaded_ctx = sem("loaded_w"), sem("loaded_ctx")
        masks, own_dve, own_act, own_pool = sem("masks"), sem("own_dve"), sem("own_act"), sem("own_pool")
        wsum, stats_done, sd_done, xn_done = sem("wsum"), sem("stats_done"), sem("sd_done"), sem("xn_done")
        turned, xT_done, cT_done, ctx1_done = sem("turned"), sem("xT_done"), sem("cT_done"), sem("ctx1_done")
        gates, fa_done, sp_done, fmin_done = sem("gates"), sem("fa_done"), sem("sp_done"), sem("fmin_done")
        rows_done, m_done, em_done, nat_T, nat_done = (
            sem("rows_done"), sem("m_done"), sem("em_done"), sem("nat_T"), sem("nat_done"))
        qk, gb, arg_done, dec_done, c_done, pv, h_done = (
            sem("qk"), sem("gb"), sem("arg_done"), sem("dec_done"), sem("c_done"), sem("pv"), sem("h_done"))
        abs_done, hc_done, sq_done, var_done, std_done, y_done, res_done = (
            sem("abs_done"), sem("hc_done"), sem("sq_done"), sem("var_done"), sem("std_done"), sem("y_done"),
            sem("res_done"))
        held_dve, held_pe, held_pool = sem("held_dve"), sem("held_pe"), sem("held_pool")
        block = ph.block()
        ps = K.ps
        heads = ps[:, 2:4, 0:2 * 4 * (DH0 + 2)].rearrange("p k (b j e) -> p k b j e", b=2, j=4)

        @block.sync
        def _(sp):
            sp.wait_ge(masks, 1)
            for w, at in ((Wi, 0), (Wf, 32)):
                for part in range(3):
                    sp.dma_start(w_gate[:, part, :, at:at + H0],
                                 w[part * D:(part + 1) * D, :].rearrange("(c p) h -> p c h", p=P)
                                 ).then_inc(loaded_w, 16)
            sp.dma_start(bias_i[:], bi.rearrange("(h a) -> h a", a=1)).then_inc(loaded_w, 16)
            sp.dma_start(bias_f[32:32 + H0, :], bf.rearrange("(h a) -> h a", a=1)).then_inc(loaded_w, 16)
            sp.dma_start(lnb[:], ln_scale.partition_broadcast(P)).then_inc(loaded_w, 16)
            sp.dma_start(ctx[:], ctx_dram[0:GB].rearrange("b s d -> s b d")).then_inc(loaded_ctx, 16)
            with sp.Fori(1, G) as g:
                sp.wait_ge(turned, g * (2 * C))
                sp.wait_ge(ctx1_done, g)
                sp.dma_start(ctx[:], ctx_dram[bass.ds(g * GB, GB)].rearrange("b s d -> s b d")
                             ).then_inc(loaded_ctx, 16)

        @block.gpsimd
        def _(pool):
            for first in (res_done,):
                pool.sem_inc(first, FIRST)
            own = Own(pool, own_pool)
            nc.gpsimd.memset(w_gate[:], 0.0).then_inc(masks, 1)
            nc.gpsimd.memset(keep[:], 1.0)
            nc.gpsimd.memset(pen[:], 0.0)
            nc.gpsimd.memset(ctx1[:], 1.0)
            nc.gpsimd.memset(sel[:], 0.0)
            nc.gpsimd.memset(far[:], 0.0)
            own(nc.gpsimd.memset(ident_b[:], 0.0))
            nc.gpsimd.memset(keep[:, :, 0:1], 0.0)
            nc.gpsimd.memset(pen[:, :, 0:1], -FAR)
            nc.gpsimd.affine_select(out=sel[:], in_=sel[:], compare_op=ALU.not_equal, fill=1.0, base=0,
                                    pattern=[[-1, H0], [0, P]], channel_multiplier=1)
            nc.gpsimd.affine_select(out=far[:], in_=far[:], compare_op=ALU.is_ge, fill=FAR, base=0,
                                    pattern=[[0, GB], [1, S]], channel_multiplier=-1)
            nc.gpsimd.affine_select(out=ident_b[:], in_=ident_b[:], compare_op=ALU.not_equal, fill=1.0,
                                    base=0, pattern=[[-1, P]], channel_multiplier=1).then_inc(masks, 1)
            pool.wait_ge(loaded_w, 9 * 16)
            with pool.Fori(0, G) as g:
                own.enter(g, 1)
                pool.wait_ge(loaded_ctx, g * 16 + 16)
                pool.wait_ge(pv, FIRST + g * UNITS)
                pool.sem_inc(held_pool, 1)
                nc.gpsimd.tensor_scalar(ctx1[:, :, :, 0:DH0].rearrange("p b h e -> p (b h) e"),
                                        ctx[:].rearrange("p b (h e) -> p (b h) e", e=DH0), 1.0, None,
                                        ALU.mult).then_inc(ctx1_done, 1)
                pool.wait_ge(y_done, g + 1)
                out = hc[:].rearrange("p (b h) e -> p b (h e)", b=GB)
                own(nc.gpsimd.tensor_tensor(out, out, lnb[:].unsqueeze(1).broadcast_to([P, GB, D]), ALU.mult))
                xg = K.x[:, bass.ds(g * GB, GB), :]
                nc.gpsimd.tensor_tensor(xg, xg, out, ALU.add).then_inc(res_done, 1)
            own.leave(G)

        @block.scalar
        def _(act):
            for first in (h_done,):
                act.sem_inc(first, FIRST)
            own = Own(act, own_act)
            act.wait_ge(loaded_w, 9 * 16)
            with act.Fori(0, G) as g:
                own.enter(g, 2)
                act.wait_ge(stats_done, g + 1)
                nc.scalar.activation(rstd[:], mv[:, :, 1], ACT.Sqrt, bias=K.eps5[:, 0:1]).then_inc(sd_done, 1)
                for c in range(C):
                    act.wait_ge(turned, g * (2 * C) + c + 1)
                    nc.scalar.activation(ctxT[:, c, :], ps[:, c % 2, :], ACT.Copy).then_inc(cT_done, 1)
                act.wait_ge(fmin_done, g + 1)
                fa = f_abs[32:32 + H0, :]
                own(nc.scalar.activation(fa, ps[32:32 + H0, 2, :], ACT.Abs, bias=bias_f[32:32 + H0, :]))
                own(nc.scalar.activation(fa, fa, ACT.Exp, scale=-1.0))
                nc.scalar.activation(fa, fa, ACT.Ln, bias=1.0).then_inc(sp_done, 1)
                act.wait_ge(m_done, g + 1)
                nc.scalar.activation(mrow[:], mrow[:], ACT.Exp, scale=-1.0).then_inc(em_done, 1)
                act.wait_ge(nat_T, g + 1)
                nc.scalar.activation(nat[:], ps[:, 0, 0:2 * GB * H0].rearrange("p (k b h) -> p k b h", k=2, b=GB),
                                     ACT.Copy).then_inc(nat_done, 1)
                for c in range(UNITS):
                    for j in range(4):
                        n = 4 * c + j
                        act.wait_ge(arg_done, FIRST + g * H0 + n + 1)
                        act.wait_ge(c_done, FIRST + g * H0 + max(n - 1, 0))
                        nc.scalar.activation(dec[:, j % 2], arg[:, j % 2], ACT.Exp).then_inc(dec_done, 1)
                    act.wait_ge(pv, FIRST + g * UNITS + c + 1)
                    if c == 0:
                        act.wait_ge(hc_done, FIRST + g)
                    nc.scalar.activation(hraw[:, 0:2, 4 * c:4 * c + 4, :], heads[:, 0, :, :, 0:DH0 + 1], ACT.Copy)
                    nc.scalar.activation(hraw[:, 2:4, 4 * c:4 * c + 4, :], heads[:, 1, :, :, 0:DH0 + 1],
                                         ACT.Copy).then_inc(h_done, 1)
                act.wait_ge(h_done, FIRST + g * UNITS + UNITS)
                flat = hraw[:].rearrange("p b h e -> p (b h) e")
                nc.scalar.activation(small[:, 0], flat[:, :, DH0], ACT.Abs).then_inc(abs_done, 1)
                act.wait_ge(hc_done, FIRST + g + 1)
                nc.scalar.activation(sq[:], hc[:], ACT.Square).then_inc(sq_done, 1)
                act.wait_ge(var_done, g + 1)
                nc.scalar.activation(small[:, 4], small[:, 3], ACT.Sqrt, bias=K.eps6[:, 0:1]).then_inc(std_done, 1)
            own.leave(G)

        @block.vector
        def _(dve):
            for first in (c_done, hc_done, arg_done,):
                dve.sem_inc(first, FIRST)
            own = Own(dve, own_dve)
            dve.wait_ge(loaded_w, 9 * 16)
            nc.vector.tensor_tensor(w_ctx[:], w_gate[:, 1], w_gate[:, 2], ALU.add).then_inc(wsum, 1)
            dve.wait_ge(masks, 2)
            with dve.Fori(0, G) as g:
                own.enter(g, 17)
                for b in range(GB):
                    ins = nc.vector.bn_stats(stats[:, b, :], K.x[:, bass.ds(g * GB + b, 1), :].rearrange("p a d -> p (a d)"))
                own(ins)
                dve.sem_inc(held_dve, 1)
                for b in range(GB):
                    ins = nc.vector.bn_aggr(mv[:, b, :], stats[:, b, :])
                ins.then_inc(stats_done, 1)
                dve.wait_ge(sd_done, g + 1)
                own(nc.vector.reciprocal(rstd[:], rstd[:]))
                for b in range(GB):
                    ins = nc.vector.tensor_scalar(xn[:, b, :], K.x[:, bass.ds(g * GB + b, 1), :].rearrange("p a d -> p (a d)"),
                                                  mv[:, b, 0:1], rstd[:, b:b + 1], ALU.subtract, ALU.mult)
                ins.then_inc(xn_done, 1)
                for c in range(C):
                    dve.wait_ge(turned, g * (2 * C) + C + c + 1)
                    nc.vector.tensor_copy(xnT[:, c, :], ps[:, c % 2, :]).then_inc(xT_done, 1)
                dve.wait_ge(gates, g + 1)
                fm = f_min[32:32 + H0, :]
                nc.vector.tensor_scalar(fm, ps[32:32 + H0, 2, :], bias_f[32:32 + H0, :], 0.0, ALU.add, ALU.min).then_inc(fmin_done, 1)
                dve.wait_ge(sp_done, g + 1)
                own(nc.vector.tensor_tensor(logf[:], fm, f_abs[32:32 + H0, :], ALU.subtract))
                own(nc.vector.tensor_tensor_scan(cumf[:], keep[:].rearrange("p b s -> p (b s)"), logf[:], 0.0,
                                                 ALU.mult, ALU.add))
                own(nc.vector.scalar_tensor_tensor(arow[:], ps[0:H0, 2, :], bias_i[:], cumf[:], ALU.add, ALU.subtract))
                own(nc.vector.tensor_tensor_scan(grow[:], pen[:].rearrange("p b s -> p (b s)"), arow[:], 0.0,
                                                 ALU.add, ALU.max))
                nc.vector.tensor_tensor(mrow[:], cumf[:], grow[:], ALU.add).then_inc(m_done, 1)
                dve.wait_ge(nat_done, g + 1)

                def decayed(c, j):
                    n = 4 * c + j
                    if j == 0:
                        dve.wait_ge(qk, g * UNITS + c + 1)
                        dve.wait_ge(pv, FIRST + g * UNITS + c)
                    dve.wait_ge(dec_done, g * H0 + n + 1)
                    nc.vector.scalar_tensor_tensor(cmat[:, j].rearrange("p b s -> p (b s)"), ps[:, 4 + j, :],
                                                   DH0 ** -0.5, dec[:, j % 2].rearrange("p b s -> p (b s)"),
                                                   ALU.mult, ALU.mult).then_inc(c_done, 1)

                for c in range(UNITS):
                    for j in range(4):
                        n = 4 * c + j
                        dve.wait_ge(gb, g * H0 + n + 1)
                        nc.vector.tensor_tensor(arg[:, j % 2], nat[:, 0, :, n:n + 1].broadcast_to([P, GB, S]),
                                                ps[:, j % 2, :].rearrange("p (b s) -> p b s", b=GB),
                                                ALU.subtract).then_inc(arg_done, 1)
                        if j:
                            decayed(c, j - 1)
                    decayed(c, 3)
                dve.wait_ge(abs_done, g + 1)
                flat = hraw[:].rearrange("p b h e -> p (b h) e")
                own(nc.vector.tensor_tensor(small[:, 1], small[:, 0], nat[:, 1].rearrange("p b h -> p (b h)"), ALU.max))
                own(nc.vector.tensor_scalar(small[:, 1], small[:, 1], 1e-6, None, ALU.add))
                own(nc.vector.reciprocal(small[:, 1], small[:, 1]))
                own(nc.vector.tensor_reduce(small[:, 2], flat[:, :, 0:DH0], AX, ALU.add))
                own(nc.vector.tensor_scalar(small[:, 2], small[:, 2], 1.0 / DH0, None, ALU.mult))
                dve.wait_ge(res_done, FIRST + g)
                nc.vector.tensor_tensor(hc[:], flat[:, :, 0:DH0],
                                        small[:, 2].unsqueeze(2).broadcast_to([P, GB * H0, DH0]),
                                        ALU.subtract).then_inc(hc_done, 1)
                dve.wait_ge(sq_done, g + 1)
                own(nc.vector.tensor_reduce(small[:, 3], sq[:], AX, ALU.add))
                own(nc.vector.scalar_tensor_tensor(small[:, 3], small[:, 3], 1.0 / DH0, small[:, 1], ALU.mult, ALU.mult))
                own(nc.vector.tensor_tensor(small[:, 3], small[:, 3], small[:, 1], ALU.mult))
                own(nc.vector.tensor_copy(small[:, 5], small[:, 3]))
                nc.vector.tensor_copy(small[:, 2], small[:, 3]).then_inc(var_done, 1)
                dve.wait_ge(std_done, g + 1)
                own(nc.vector.reciprocal(small[:, 4], small[:, 4]))
                own(nc.vector.tensor_tensor(small[:, 5], small[:, 4], small[:, 1], ALU.mult))
                nc.vector.tensor_tensor(hc[:], hc[:], small[:, 5].unsqueeze(2).broadcast_to([P, GB * H0, DH0]),
                                        ALU.mult).then_inc(y_done, 1)
            own.leave(G)

        @block.tensor
        def _(pe):
            for first in (pv,):
                pe.sem_inc(first, FIRST)
            pe.wait_ge(masks, 2)
            pe.wait_ge(wsum, 1)
            with pe.Fori(0, G) as g:
                pe.wait_ge(loaded_ctx, g * 16 + 16)
                pe.wait_ge(arg_done, FIRST + g * H0)
                for k in range(2 * C):
                    c, src = k % C, (ctx if k < C else xn)
                    if k == C:
                        pe.wait_ge(xn_done, g + 1)
                    if k >= 2:
                        if k - 2 < C:
                            pe.wait_ge(cT_done, g * C + k - 1)
                        else:
                            pe.wait_ge(xT_done, g * C + k - 1 - C)
                    for b in range(GB):
                        ins = nc.tensor.transpose(ps[:, k % 2, b * S:(b + 1) * S], src[:, b, c * P:(c + 1) * P],
                                                  K.ident[:])
                    ins.then_inc(turned, 1)
                pe.wait_ge(xT_done, g * C + C)
                pe.wait_ge(h_done, FIRST + g * UNITS)
                for c in range(C):
                    nc.tensor.matmul(ps[0:64, 2, :], w_gate[:, 0, c, :], xnT[:, c, :], start=(c == 0), stop=False)
                for c in range(C):
                    ins = nc.tensor.matmul(ps[0:64, 2, :], w_ctx[:, c, :], ctxT[:, c, :], start=False, stop=(c == C - 1))
                ins.then_inc(gates, 1)
                pe.wait_ge(m_done, g + 1)
                pe.sem_inc(held_pe, 1)
                at = ps[:, 0, 0:2 * GB * H0].rearrange("p (k b h) -> p k b h", k=2, b=GB)
                for b in range(GB):
                    nc.tensor.transpose(at[:, 0, b, :], arow[:, b * S:(b + 1) * S], K.ident[0:H0, 0:H0])
                pe.wait_ge(em_done, g + 1)
                pe.sem_inc(held_pe, 1)
                for b in range(GB):
                    ins = nc.tensor.transpose(at[:, 1, b, :], mrow[:, b * S:(b + 1) * S], K.ident[0:H0, 0:H0])
                ins.then_inc(nat_T, 1)
                pe.wait_ge(nat_done, g + 1)
                pe.wait_ge(ctx1_done, g + 1)
                for c in range(UNITS):
                    pe.wait_ge(c_done, FIRST + g * H0 + 4 * c)
                    for b in range(GB):
                        for j in range(4):
                            r = slice(32 * j, 32 * j + 32)
                            ins = nc.tensor.matmul(ps[:, 4 + j, b * S:(b + 1) * S], ctxT[r, c, b * S:(b + 1) * S],
                                                   xnT[r, c, b * S:(b + 1) * S], start=True, stop=True)
                    ins.then_inc(qk, 1)
                    for j in range(4):
                        n = 4 * c + j
                        if n >= 2:
                            pe.wait_ge(arg_done, FIRST + g * H0 + n - 1)
                        nc.tensor.matmul(ps[:, j % 2, :], ident_b[:], far[:].rearrange("p b s -> p (b s)"),
                                         start=True, stop=False)
                        nc.tensor.matmul(ps[:, j % 2, :], sel[:, n, :], grow[:], start=False, stop=True).then_inc(gb, 1)
                    pe.wait_ge(h_done, FIRST + g * UNITS + c)
                    for j in range(4):
                        pe.wait_ge(c_done, FIRST + g * H0 + 4 * c + j + 1)
                        for b in range(GB):
                            ins = nc.tensor.matmul(heads[:, b // 2, b % 2, j, 0:DH0 + 1], cmat[:, j, b, :],
                                                   ctx1[:, b, 4 * c + j, :], start=True, stop=True)
                    ins.then_inc(pv, 1)



def turn(nc, K, name, lead, trail, ctx_dram=None, rms=None, logits=None, router=None):
    with Phase(nc, name) as ph:
        sb, sem = ph.sb, ph.sem
        norm = ctx_dram is None
        stage = sb("stage", [P, 2, GB, D])
        stats = sb("stats", [P, B, 6])
        mv = sb("mv", [P, B, 2])
        scale = sb("scale", [P, B])
        square = sb("square", [P, B])
        loaded = [sem("loaded0"), sem("loaded1")]
        staged, turned, lead_done, trail_done = sem("staged"), sem("turned"), sem("lead_done"), sem("trail_done")
        stats_done, std_done, ms_done, rms_done = sem("stats_done"), sem("std_done"), sem("ms_done"), sem("rms_done")
        plain_done, logit_mm, logit_done = sem("plain_done"), sem("logit_mm"), sem("logit_done")
        loaded_w, own_dve, held, held_act = sem("loaded_w"), sem("own_dve"), sem("held"), sem("held_act")
        if rms is not None:
            wcol = sb("wcol", [P, C])
            rw = sb("rw", [P, C, E])
            plain = sb("plain", [P, 2, C, N])
        block = ph.block()
        ps = K.ps

        @block.sync
        def _(sp):
            if rms is not None:
                sp.dma_start(wcol[:], rms.rearrange("(c p) -> p c", p=P), allow_slow_non_contiguous=True).then_inc(loaded_w, 16)
                sp.dma_start(rw[:], router.rearrange("(c p) e -> p c e", p=P)).then_inc(loaded_w, 16)
            if not norm:
                for q in range(2):
                    sp.dma_start(stage[:, q], ctx_dram[q * GB:(q + 1) * GB].rearrange("b s d -> s b d")
                                 ).then_inc(loaded[q], 16)
                for q in range(2):
                    sp.wait_ge(turned, (q + 1) * C)
                    sp.dma_start(stage[:, q], ctx_dram[(2 + q) * GB:(3 + q) * GB].rearrange("b s d -> s b d")
                                 ).then_inc(loaded[q], 16)

        @block.vector
        def _(dve):
            for first in (trail_done,):
                dve.sem_inc(first, FIRST)
            own = Own(dve, own_dve)
            if norm:
                with dve.Fori(0, G) as g:
                    for b in range(GB):
                        nc.vector.bn_stats(stats[:, bass.ds(g * GB + b, 1), :].rearrange("p a d -> p (a d)"),
                                           K.x[:, bass.ds(g * GB + b, 1), :].rearrange("p a d -> p (a d)")
                                           ).then_inc(held, 1)
                dve.wait_ge(held, B)
                for b in range(B):
                    ins = nc.vector.bn_aggr(mv[:, b, :], stats[:, b, :])
                ins.then_inc(stats_done, 1)
                dve.wait_ge(std_done, 1)
                own(nc.vector.reciprocal(scale[:], scale[:]))
                if rms is not None:
                    own(nc.vector.tensor_tensor(square[:], mv[:, :, 1], scale[:], ALU.mult))
                    nc.vector.tensor_tensor(square[:], square[:], scale[:], ALU.mult).then_inc(ms_done, 1)
                    dve.wait_ge(rms_done, 1)
                    own(nc.vector.reciprocal(square[:], square[:]))
                    own(nc.vector.tensor_tensor(scale[:], scale[:], square[:], ALU.mult))
            if rms is not None:
                dve.wait_ge(loaded_w, 32)
            with dve.Fori(0, G // 2) as i:
                if norm:
                    for q in range(2):
                        for b in range(GB):
                            g4 = (i * 2 + q) * GB + b
                            ins = nc.vector.tensor_scalar(
                                stage[:, q, b, :], K.x[:, bass.ds(g4, 1), :].rearrange("p a d -> p (a d)"),
                                mv[:, bass.ds(g4, 1), 0:1].rearrange("p a d -> p (a d)"), scale[:, bass.ds(g4, 1)],
                                ALU.subtract, ALU.mult)
                        ins.then_inc(staged, 1)
                for q in range(2):
                    cols = bass.ds((i * 2 + q) * N, N)
                    for c in range(C):
                        dve.wait_ge(lead_done, i * (2 * C) + q * C + c + 1)
                        src = ps[:, c + 4 * q, :] if rms is None else plain[:, q, c, :]
                        nc.vector.tensor_tensor(trail[:, c, cols], src, lead[:, c, cols].bitcast(F32),
                                                ALU.subtract).then_inc(trail_done, 1)

        @block.scalar
        def _(act):
            for first in (logit_done,):
                act.sem_inc(first, FIRST)
            if norm:
                act.wait_ge(stats_done, 1)
                nc.scalar.activation(scale[:], mv[:, :, 1], ACT.Sqrt, bias=K.eps5[:, 0:1]).then_inc(std_done, 1)
            if rms is not None:
                act.wait_ge(ms_done, 1)
                nc.scalar.activation(square[:], square[:], ACT.Sqrt, bias=K.eps6[:, 0:1]).then_inc(rms_done, 1)
                act.wait_ge(loaded_w, 32)
            with act.Fori(0, G // 2) as i:
                for q in range(2):
                    cols = bass.ds((i * 2 + q) * N, N)
                    for c in range(C):
                        act.wait_ge(turned, i * (2 * C) + q * C + c + 1)
                        if rms is None:
                            ph.hold(act, held_act)
                            nc.scalar.activation(lead[:, c, cols], ps[:, c + 4 * q, :], ACT.Copy).then_inc(lead_done, 1)
                        else:
                            act.wait_ge(logit_mm, FIRST + i * 2)
                            act.wait_ge(trail_done, FIRST + i * (2 * C))
                            nc.scalar.activation(plain[:, q, c, :], ps[:, c + 4 * q, :], ACT.Identity,
                                                 scale=wcol[:, c:c + 1]).then_inc(plain_done, 1)
                    if rms is not None:
                        act.wait_ge(logit_mm, FIRST + i * 2 + q + 1)
                        ph.hold(act, held_act)
                        nc.scalar.activation(logits[:, bass.ds((i * 2 + q) * GB, GB), :],
                                             ps[:, 4 * q, 0:GB * E].rearrange("p (b e) -> p b e", b=GB),
                                             ACT.Identity).then_inc(logit_done, 1)

        @block.gpsimd
        def _(pool):
            if rms is not None:
                with pool.Fori(0, G // 2) as i:
                    for q in range(2):
                        cols = bass.ds((i * 2 + q) * N, N)
                        for c in range(C):
                            pool.wait_ge(plain_done, i * (2 * C) + q * C + c + 1)
                            pool.sem_inc(held, 1)
                            nc.gpsimd.tensor_copy(lead[:, c, cols], plain[:, q, c, :]).then_inc(lead_done, 1)

        @block.tensor
        def _(pe):
            for first in (logit_mm,):
                pe.sem_inc(first, FIRST)
            with pe.Fori(0, G // 2) as i:
                pe.wait_ge(trail_done, FIRST + i * (2 * C))
                if rms is not None:
                    pe.wait_ge(logit_done, FIRST + i * 2)
                for q in range(2):
                    if norm:
                        pe.wait_ge(staged, i * 2 + q + 1)
                    else:
                        pe.wait_ge(loaded[q], i * 16 + 16)
                    for c in range(C):
                        for b in range(GB):
                            ins = nc.tensor.transpose(ps[:, c + 4 * q, b * S:(b + 1) * S],
                                                      stage[:, q, b, c * P:(c + 1) * P], K.ident[:])
                        ins.then_inc(turned, 1)
                    if rms is not None:
                        pe.wait_ge(plain_done, i * (2 * C) + (q + 1) * C)
                        pe.wait_ge(loaded_w, 32)
                        for b in range(GB):
                            for c in range(C):
                                ins = nc.tensor.matmul(ps[:, 4 * q, b * E:(b + 1) * E], plain[:, q, c, b * S:(b + 1) * S],
                                                       rw[:, c, :], start=(c == 0), stop=(c == C - 1))
                        ins.then_inc(logit_mm, 1)


def choose(nc, K, logits, wd):
    with Phase(nc, "choose") as ph:
        sb, sem = ph.sb, ph.sem
        top = sb("top", [P, B, 8])
        idx = sb("idx", [P, B, 8], U32)
        pos = sb("pos", [P, B, 2])
        row = sb("row", [P, B])
        part = sb("part", [P, B, E])
        part2 = sb("part2", [P, B, E])
        number = sb("number", [P, B, E])
        own_dve, shifted, exped, numbered = sem("own_dve"), sem("shifted"), sem("exped"), sem("numbered")
        block = ph.block()

        @block.gpsimd
        def _(pool):
            nc.gpsimd.iota(number[:], pattern=[[0, B], [1, E]], base=0, channel_multiplier=0,
                           allow_small_or_imprecise_dtypes=True).then_inc(numbered, 1)

        @block.scalar
        def _(act):
            act.wait_ge(shifted, 1)
            nc.scalar.activation(logits[:], logits[:], ACT.Exp).then_inc(exped, 1)

        @block.vector
        def _(dve):
            own = Own(dve, own_dve)
            wide = lambda v: v.unsqueeze(2).broadcast_to([P, B, E])
            own(nc.vector.tensor_reduce(row[:], logits[:], AX, ALU.max))
            nc.vector.tensor_tensor(logits[:], logits[:], wide(row[:]), ALU.subtract).then_inc(shifted, 1)
            dve.wait_ge(exped, 1)
            own(nc.vector.tensor_reduce(row[:], logits[:], AX, ALU.add))
            own(nc.vector.reciprocal(row[:], row[:]))
            own(nc.vector.tensor_tensor(logits[:], logits[:], wide(row[:]), ALU.mult))
            for b in range(B):
                ins = nc.vector.max(top[:, b, :], logits[:, b, :])
            own(ins)
            for b in range(B):
                ins = nc.vector.max_index(idx[:, b, :], top[:, b, :], logits[:, b, :])
            own(ins)
            own(nc.vector.tensor_copy(pos[:], idx[:, :, 0:2]))
            own(nc.vector.tensor_tensor(row[:], top[:, :, 0], top[:, :, 1], ALU.add))
            own(nc.vector.reciprocal(row[:], row[:]))
            dve.wait_ge(numbered, 1)
            nc.vector.tensor_tensor(part[:], number[:], wide(pos[:, :, 0]), ALU.is_equal)
            own(nc.vector.tensor_tensor(part2[:], number[:], wide(pos[:, :, 1]), ALU.is_equal))
            nc.vector.tensor_tensor(part[:], part[:], wide(top[:, :, 0]), ALU.mult)
            own(nc.vector.tensor_tensor(part2[:], part2[:], wide(top[:, :, 1]), ALU.mult))
            own(nc.vector.tensor_tensor(part[:], part[:], part2[:], ALU.add))
            own(nc.vector.tensor_tensor(wd[:, 0:E, :].rearrange("p e b -> p b e"), part[:], wide(row[:]), ALU.mult))
            own(nc.vector.memset(wd[:, E, :], 1.0))


def experts(nc, K, lead, trail, wd, routed, shared):
    CH = (2 * C * F + FC * D) // 512
    UP, DOWN = C * F, 2 * C * F
    with Phase(nc, "experts") as ph:
        sb, sem = ph.sb, ph.sem
        raw = sb("raw", [P, CH * 512])
        wl = sb("wl", [P, 2, CH * 512], F32R)
        wt = sb("wt", [P, 2, CH * 512], F32R)
        gated = sb("gated", [P, FC, N])
        hid = sb("hid", [P, FC, N])
        hl = sb("hl", [P, 2, FC, N], F32R)
        ht = sb("ht", [P, 2, FC, N], F32R)
        raw_loaded, wl_done, wt_done = sem("raw_loaded"), sem("wl_done"), sem("wt_done")
        gu, silu_done, hid_done, hl_done, ht_done = sem("gu"), sem("silu_done"), sem("hid_done"), sem("hl_done"), sem("ht_done")
        down, acc_done, held = sem("down"), sem("acc_done"), sem("held")
        block = ph.block()
        ps = K.ps

        @block.sync
        def _(sp):
            def load(gate_w, up_w, down_w):
                for w, at, n in ((gate_w, 0, UP), (up_w, UP, UP), (down_w, DOWN, FC * D)):
                    sp.dma_start(raw[:, at:at + n].rearrange("p (c f) -> p c f", f=w.shape[-1]),
                                 w.rearrange("(c p) f -> p c f", p=P)).then_inc(raw_loaded, 16)

            def load_expert(e):
                load(*(w[bass.ds(e, 1)].rearrange("e k f -> (e k) f") for w in routed))

            load_expert(0)
            with sp.Fori(0, E // 2 - 1) as i:
                sp.wait_ge(wt_done, i * (2 * CH) + CH)
                load_expert(i * 2 + 1)
                sp.wait_ge(wt_done, i * (2 * CH) + 2 * CH)
                load_expert(i * 2 + 2)
            sp.wait_ge(wt_done, CH * (E - 1))
            load_expert(E - 1)
            sp.wait_ge(wt_done, CH * E)
            load(*shared)

        def pieces(g):
            return range(2 * (g - 1), 2 * g) if g else ()

        @block.gpsimd
        def _(pool):
            def cut(e, p, k):
                pool.wait_ge(raw_loaded, (e + 1) * 48)
                pool.sem_inc(held, 1)
                nc.gpsimd.tensor_scalar(wl[:, p, k * 512:(k + 1) * 512], raw[:, k * 512:(k + 1) * 512], 1.0, None,
                                        ALU.mult).then_inc(wl_done, 1)

            def unit(i, u, following):
                p, g = divmod(u, G)
                for f in range(FC):
                    pool.wait_ge(hid_done, FIRST + i * 16 + 2 * u + f + 1)
                    pool.wait_ge(down, FIRST + i * 32 + max(4 * (u - 1), 0))
                    pool.sem_inc(held, 1)
                    nc.gpsimd.tensor_scalar(hl[:, u % 2, f, :], hid[:, f, :], 1.0, None, ALU.mult).then_inc(hl_done, 1)
                if following:
                    for k in pieces(g):
                        pool.wait_ge(down, FIRST + i * 32 + 16 * p)
                        cut(i * 2 + p + 1, 1 - p, k)

            for k in range(CH):
                cut(0, 0, k)
            with pool.Fori(0, E // 2) as i:
                for u in range(2 * G):
                    unit(i, u, True)
            for u in range(G):
                unit(E // 2, u, False)

        @block.scalar
        def _(act):
            nc.scalar.activation(K.scrap[:], K.ones[:, 0:1], ACT.Silu)

            def unit(i, u):
                for f in range(FC):
                    act.wait_ge(gu, i * 16 + 2 * u + f + 1)
                    act.wait_ge(hid_done, FIRST + i * 16 + max(2 * u + f - 1, 0))
                    nc.scalar.activation(gated[:, f, :], ps[:, 2 * f, :], ACT.Silu).then_inc(silu_done, 1)

            with act.Fori(0, E // 2) as i:
                for u in range(2 * G):
                    unit(i, u)
            for u in range(G):
                unit(E // 2, u)

        @block.vector
        def _(dve):
            for first in (hid_done, ht_done, acc_done,):
                dve.sem_inc(first, FIRST)
            def cut(e, p, k):
                dve.wait_ge(wl_done, e * CH + k + 1)
                cols = slice(k * 512, (k + 1) * 512)
                nc.vector.tensor_tensor(wt[:, p, cols], raw[:, cols], wl[:, p, cols].bitcast(F32),
                                        ALU.subtract).then_inc(wt_done, 1)

            def add(i, u):
                p, g = divmod(u, G)
                e = i * 2 + p
                for b in range(GB):
                    dve.wait_ge(down, FIRST + i * 32 + 4 * u + b + 1)
                    xb = K.x[:, g * GB + b, :]
                    nc.vector.scalar_tensor_tensor(
                        xb, ps[:, 4 + b, :], wd[:, bass.ds(e, 1), g * GB + b:g * GB + b + 1].rearrange("p a b -> p (a b)"),
                        xb, ALU.mult, ALU.add).then_inc(acc_done, 1)

            def unit(i, u, following):
                p, g = divmod(u, G)
                for f in range(FC):
                    dve.wait_ge(silu_done, i * 16 + 2 * u + f + 1)
                    dve.wait_ge(ht_done, FIRST + i * 16 + 2 * u)
                    nc.vector.tensor_tensor(hid[:, f, :], gated[:, f, :], ps[:, 2 * f + 1, :],
                                            ALU.mult).then_inc(hid_done, 1)
                for f in range(FC):
                    dve.wait_ge(hl_done, i * 16 + 2 * u + f + 1)
                    dve.wait_ge(hid_done, FIRST + i * 16 + 2 * u + f + 1)
                    dve.wait_ge(down, FIRST + i * 32 + max(4 * (u - 1), 0))
                    nc.vector.tensor_tensor(ht[:, u % 2, f, :], hid[:, f, :], hl[:, u % 2, f, :].bitcast(F32),
                                            ALU.subtract).then_inc(ht_done, 1)
                if following:
                    for k in pieces(g):
                        dve.wait_ge(down, FIRST + i * 32 + 16 * p)
                        cut(i * 2 + p + 1, 1 - p, k)
                if u:
                    add(i, u - 1)

            for k in range(CH):
                cut(0, 0, k)
            with dve.Fori(0, E // 2) as i:
                dve.wait_ge(acc_done, FIRST + i * 32)
                for u in range(2 * G):
                    if u == G:
                        dve.wait_ge(acc_done, FIRST + i * 32 + 4 * (G - 1))
                    unit(i, u, True)
                dve.wait_ge(acc_done, FIRST + i * 32 + 28)
                add(i, 2 * G - 1)
            dve.wait_ge(acc_done, FIRST + 16 * E)
            for u in range(G):
                unit(E // 2, u, False)
            add(E // 2, G - 1)

        @block.tensor
        def _(pe):
            for first in (down,):
                pe.sem_inc(first, FIRST)
            def up(i, u):
                p, g = divmod(u, G)
                cols = slice(g * N, (g + 1) * N)
                if g == 0:
                    pe.wait_ge(wt_done, (i * 2 + p + 1) * CH)
                for f in range(FC):
                    pe.wait_ge(hid_done, FIRST + i * 16 + max(2 * u + f - 1, 0))
                    for bank, at in ((2 * f, 0), (2 * f + 1, UP)):
                        for c in range(C):
                            w = slice(at + c * F + f * P, at + c * F + (f + 1) * P)
                            ins = three_passes(nc, ps[:, bank, :], wl[:, p, w], wt[:, p, w], lead[:, c, cols],
                                               trail[:, c, cols], c == 0, c == C - 1)
                    ins.then_inc(gu, 1)

            def down_product(i, u):
                p, g = divmod(u, G)
                pe.wait_ge(ht_done, FIRST + i * 16 + 2 * u + 2)
                for b in range(GB):
                    pe.wait_ge(acc_done, FIRST + i * 32 + max(4 * u - 3 + b, 0))
                    rows = slice(b * S, (b + 1) * S)
                    for f in range(FC):
                        w = slice(DOWN + f * D, DOWN + (f + 1) * D)
                        ins = three_passes(nc, ps[:, 4 + b, :], hl[:, u % 2, f, rows], ht[:, u % 2, f, rows],
                                           wl[:, p, w], wt[:, p, w], f == 0, f == FC - 1)
                    ins.then_inc(down, 1)

            with pe.Fori(0, E // 2) as i:
                for u in range(2 * G):
                    up(i, u)
                    if u:
                        down_product(i, u - 1)
                down_product(i, 2 * G - 1)
            for u in range(G):
                up(E // 2, u)
                if u:
                    down_product(E // 2, u - 1)
            down_product(E // 2, G - 1)


def project(nc, K, name, lead, trail, w_dram, b_dram, out_dram, rstd):
    W2 = 2 * P
    with Phase(nc, name) as ph:
        sb, sem = ph.sb, ph.sem
        raw = sb("raw", [P, C, W2])
        wl = sb("wl", [P, 2, C, W2], F32R)
        wt = sb("wt", [P, 2, C, W2], F32R)
        bias = sb("bias", [P, H1])
        head = sb("head", [P, 2, T])
        sq = sb("sq", [P, 2, N])
        total = sb("total", [P, T])
        raw_loaded, bias_loaded, wl_done, wt_done = sem("raw_loaded"), sem("bias_loaded"), sem("wl_done"), sem("wt_done")
        product, head_done, sq_done, acc_done, held = sem("product"), sem("head_done"), sem("sq_done"), sem("acc_done"), sem("held")
        stored = [sem("stored0"), sem("stored1")]
        sums, std_done, own_dve, blank = sem("sums"), sem("std_done"), sem("own_dve"), sem("blank")
        held_act, held_sp = sem("held_act"), sem("held_sp")
        block = ph.block()
        ps = K.ps
        UN = 4 * G

        @block.sync
        def _(sp):
            def load(pair):
                sp.dma_start(raw[:], w_dram[:, bass.ds(pair * W2, W2)].rearrange("(c p) n -> p c n", p=P)
                             ).then_inc(raw_loaded, 16)

            sp.dma_start(bias[:], b_dram.rearrange("(h p) -> p h", p=P), allow_slow_non_contiguous=True).then_inc(bias_loaded, 16)
            load(0)
            with sp.Fori(0, H1 // 4) as i:
                for p in range(2):
                    sp.wait_ge(wt_done, (i * 2 + p + 1) * 2)
                    ph.hold(sp, held_sp)
                    load(within(nc, (i * 2 + p + 1) & (H1 // 2 - 1), H1 // 2 - 1))
            sp.wait_ge(raw_loaded, 16 * (H1 // 2 + 1))

        def halves(p):
            return (lambda w: w[:, 2 * p:2 * p + 2, :])

        @block.gpsimd
        def _(pool):
            def cut(pair, p):
                pool.wait_ge(raw_loaded, (pair + 1) * 16)
                pool.sem_inc(held, 1)
                for k in range(2):
                    nc.gpsimd.tensor_scalar(halves(k)(wl[:, p]), halves(k)(raw[:]), 1.0, None, ALU.mult
                                            ).then_inc(wl_done, 1)

            nc.gpsimd.memset(total[:], 0.0).then_inc(blank, 1)
            cut(0, 0)
            with pool.Fori(0, H1 // 4) as i:
                for p in range(2):
                    pool.wait_ge(product, FIRST + i * UN + 8 * p)
                    cut(i * 2 + p + 1, 1 - p)

        @block.scalar
        def _(act):
            for first in (sq_done, stored[0], stored[1],):
                act.sem_inc(first, FIRST)
            act.wait_ge(bias_loaded, 16)
            with act.Fori(0, H1 // 4) as i:
                for n in range(UN):
                    hh, g = divmod(n, G)
                    b = bias[:, bass.ds(i * 4 + hh, 1)]
                    if g == 0:
                        act.wait_ge(stored[hh % 2], FIRST + (i * 2 + hh // 2) * 16)
                    act.wait_ge(product, FIRST + i * UN + n + 1)
                    ph.hold(act, held_act)
                    nc.scalar.activation(head[:, hh % 2, g * N:(g + 1) * N], ps[:, n % 8, :], ACT.Identity,
                                         bias=b).then_inc(head_done, 1)
                    act.wait_ge(acc_done, FIRST + i * UN + max(n - 1, 0))
                    ph.hold(act, held_act)
                    nc.scalar.activation(sq[:, n % 2, :], ps[:, n % 8, :], ACT.Square, bias=b).then_inc(sq_done, 1)
                    if g == G - 1:
                        act.wait_ge(head_done, i * UN + n + 1)
                        act.dma_start(out_dram[bass.ds(i * 4 + hh, 1)].rearrange("h p t -> (h p) t"),
                                      head[:, hh % 2, :]).then_inc(stored[hh % 2], 16)
            act.wait_ge(sums, 1)
            nc.scalar.activation(rstd[:], ps[:, 0, 0:B], ACT.Sqrt, scale=1.0 / INNER, bias=K.eps6[:, 0:1]
                                 ).then_inc(std_done, 1)
            for k in range(2):
                act.wait_ge(stored[k], FIRST + 16 * (H1 // 2))

        @block.vector
        def _(dve):
            for first in (acc_done,):
                dve.sem_inc(first, FIRST)
            def cut(pair, p):
                for k in range(2):
                    dve.wait_ge(wl_done, pair * 2 + k + 1)
                    nc.vector.tensor_tensor(halves(k)(wt[:, p]), halves(k)(raw[:]), halves(k)(wl[:, p]).bitcast(F32),
                                            ALU.subtract).then_inc(wt_done, 1)

            cut(0, 0)
            dve.wait_ge(blank, 1)
            with dve.Fori(0, H1 // 4) as i:
                for n in range(UN):
                    g = n % G
                    dve.wait_ge(sq_done, FIRST + i * UN + n + 1)
                    dve.wait_ge(acc_done, FIRST + i * UN + max(n - 3, 0))
                    t = total[:, g * N:(g + 1) * N]
                    nc.vector.tensor_tensor(t, t, sq[:, n % 2, :], ALU.add).then_inc(acc_done, 1)
                    if n % 8 == 1:
                        p = n // 8
                        dve.wait_ge(product, FIRST + i * UN + 8 * p)
                        cut(i * 2 + p + 1, 1 - p)
            dve.wait_ge(std_done, 1)
            Own(dve, own_dve)(nc.vector.reciprocal(rstd[:], rstd[:]))

        @block.tensor
        def _(pe):
            for first in (product,):
                pe.sem_inc(first, FIRST)
            with pe.Fori(0, H1 // 4) as i:
                for n in range(UN):
                    hh, g = divmod(n, G)
                    p = hh // 2
                    if n % 8 == 0:
                        pe.wait_ge(wt_done, (i * 2 + p + 1) * 2)
                    pe.wait_ge(sq_done, FIRST + i * UN + max(n - 7, 0))
                    w = slice((hh % 2) * P, (hh % 2 + 1) * P)
                    cols = slice(g * N, (g + 1) * N)
                    for c in range(C):
                        ins = three_passes(nc, ps[:, n % 8, :], wl[:, p, c, w], wt[:, p, c, w], lead[:, c, cols],
                                           trail[:, c, cols], c == 0, c == C - 1)
                    ins.then_inc(product, 1)
            pe.wait_ge(acc_done, FIRST + H1 * G)
            for b in range(B):
                ins = nc.tensor.matmul(ps[:, 0, b:b + 1], total[:, b * S:(b + 1) * S], K.ones[:, 0:1],
                                       start=True, stop=True)
            ins.then_inc(sums, 1)


def values(nc, K, lead, trail, w_dram, v_dram):
    with Phase(nc, "values") as ph:
        sb, sem = ph.sb, ph.sem
        raw = sb("raw", [P, C, N])
        wl = sb("wl", [P, 2, C, N], F32R)
        wt = sb("wt", [P, 2, C, N], F32R)
        out = sb("out", [P, 2, 4, GB, DH1])
        raw_loaded, wl_done, wt_done, held = sem("raw_loaded"), sem("wl_done"), sem("wt_done"), sem("held")
        product, even_done, odd_done = sem("product"), sem("even_done"), sem("odd_done")
        stored, held_sp = [sem("stored0"), sem("stored1")], sem("held_sp")
        block = ph.block()
        ps = K.ps
        QUADS = H1 // 4

        @block.sync
        def _(sp):
            for first in (stored[0], stored[1],):
                sp.sem_inc(first, FIRST)
            def load(quad):
                sp.dma_start(raw[:], w_dram[:, bass.ds(quad * N, N)].rearrange("(c p) n -> p c n", p=P)
                             ).then_inc(raw_loaded, 16)

            load(0)
            with sp.Fori(0, QUADS // 2) as i:
                for p in range(2):
                    sp.wait_ge(wt_done, (i * 2 + p + 1) * C)
                    ph.hold(sp, held_sp)
                    load(within(nc, (i * 2 + p + 1) & (QUADS - 1), QUADS - 1))
                    for k in range(G):
                        done = (i * 2 + p) * (B // 2) + (k + 1) * 2
                        sp.wait_ge(even_done, FIRST + done)
                        sp.wait_ge(odd_done, FIRST + done)
                        sp.dma_start(v_dram[bass.ds((i * 2 + p) * 4, 4), :, k * GB:(k + 1) * GB, :]
                                     .rearrange("h l b e -> l h (b e)"),
                                     out[:, k % 2].rearrange("p h b e -> p h (b e)")).then_inc(stored[k % 2], 16)
            for k in range(2):
                sp.wait_ge(stored[k], FIRST + 16 * 2 * QUADS)
            sp.wait_ge(raw_loaded, 16 * (QUADS + 1))

        @block.gpsimd
        def _(pool):
            def cut(quad, p):
                pool.wait_ge(raw_loaded, (quad + 1) * 16)
                pool.sem_inc(held, 1)
                for c in range(C):
                    nc.gpsimd.tensor_scalar(wl[:, p, c, :], raw[:, c, :], 1.0, None, ALU.mult).then_inc(wl_done, 1)

            cut(0, 0)
            with pool.Fori(0, QUADS // 2) as i:
                for p in range(2):
                    pool.wait_ge(product, FIRST + i * 2 * B + B * p)
                    cut(i * 2 + p + 1, 1 - p)

        def slot(b):
            return (lambda out: out[:, (b // GB) % 2, :, b % GB, :])

        @block.scalar
        def _(act):
            for first in (even_done,):
                act.sem_inc(first, FIRST)
            with act.Fori(0, QUADS // 2) as i:
                for n in range(2 * B):
                    p, b = divmod(n, B)
                    if b % 2 == 0:
                        if b % GB == 0:
                            act.wait_ge(stored[(b // GB) % 2], FIRST + ((i * 2 + p) * 2 + b // (2 * GB)) * 16)
                        act.wait_ge(product, FIRST + i * 2 * B + n + 1)
                        nc.scalar.activation(slot(b)(out), ps[:, n % 8, :].rearrange("p (h e) -> p h e", h=4),
                                             ACT.Copy).then_inc(even_done, 1)

        @block.vector
        def _(dve):
            for first in (odd_done,):
                dve.sem_inc(first, FIRST)
            def cut(quad, p, c):
                dve.wait_ge(wl_done, quad * C + c + 1)
                nc.vector.tensor_tensor(wt[:, p, c, :], raw[:, c, :], wl[:, p, c, :].bitcast(F32),
                                        ALU.subtract).then_inc(wt_done, 1)

            for c in range(C):
                cut(0, 0, c)
            with dve.Fori(0, QUADS // 2) as i:
                for n in range(2 * B):
                    p, b = divmod(n, B)
                    if b % 2 == 1:
                        if b % GB == 1:
                            dve.wait_ge(stored[(b // GB) % 2], FIRST + ((i * 2 + p) * 2 + b // (2 * GB)) * 16)
                        dve.wait_ge(product, FIRST + i * 2 * B + n + 1)
                        nc.vector.tensor_copy(slot(b)(out), ps[:, n % 8, :].rearrange("p (h e) -> p h e", h=4)
                                              ).then_inc(odd_done, 1)
                        if b in (3, 5, 7, 9):
                            cut(i * 2 + p + 1, 1 - p, (b - 3) // 2)

        @block.tensor
        def _(pe):
            for first in (product,):
                pe.sem_inc(first, FIRST)
            with pe.Fori(0, QUADS // 2) as i:
                for n in range(2 * B):
                    p, b = divmod(n, B)
                    if b == 0:
                        pe.wait_ge(wt_done, (i * 2 + p + 1) * C)
                    pe.wait_ge(odd_done if b % 2 else even_done, FIRST + i * B + max((n - 8) // 2 + 1, 0))
                    rows = slice(b * S, (b + 1) * S)
                    for c in range(C):
                        ins = three_passes(nc, ps[:, n % 8, :], lead[:, c, rows], trail[:, c, rows], wl[:, p, c, :],
                                           wt[:, p, c, :], c == 0, c == C - 1)
                    ins.then_inc(product, 1)


def attend(nc, K, q_dram, k_dram, v_dram, o_w, o_b, v_b, nq, nk, rq, rk):
    QUADS = H1 // 4
    IT = G * QUADS
    with Phase(nc, "attend") as ph:
        sb, sem = ph.sb, ph.sem
        wol = sb("wol", [P, H1, D], F32R)
        wot = sb("wot", [P, H1, D], F32R)
        q = sb("q", [P, 4, N])
        k = sb("k", [P, 4, N])
        v = sb("v", [P, 4, GB, DH1])
        kcol = sb("kcol", [P, H1])
        qcol = sb("qcol", [P, H1])
        vbias = sb("vbias", [P, H1])
        obias = sb("obias", [P, D])
        rkb = sb("rkb", [P, T])
        kn = sb("kn", [P, 2, N])
        prob = sb("prob", [P, 2, GB, S])
        probT = sb("probT", [P, 2, N])
        ol = sb("ol", [P, 4, N], F32R)
        ot = sb("ot", [P, 4, N], F32R)
        row = sb("row", [P, 2, 4, GB])
        raw = q
        ring = [sem(f"ring{j}") for j in range(4)]
        cols_loaded, raw_loaded, wol_done, wot_done = sem("cols_loaded"), sem("raw_loaded"), sem("wol_done"), sem("wot_done")
        bias_done, spread, rkb_done, col_done = sem("bias_done"), sem("spread"), sem("rkb_done"), sem("col_done")
        kn_done, scores, max_done, exp_done, sum_done, prob_done = (
            sem("kn_done"), sem("scores"), sem("max_done"), sem("exp_done"), sem("sum_done"), sem("prob_done"))
        prob_T, probT_done, mixed, ol_done, ot_done, final, acc_done = (
            sem("prob_T"), sem("probT_done"), sem("mixed"), sem("ol_done"), sem("ot_done"), sem("final"), sem("acc_done"))
        own_dve, row_done, held_sp, held_act = sem("own_dve"), sem("row_done"), sem("held_sp"), sem("held_act")
        block = ph.block()
        ps = K.ps

        @block.sync
        def _(sp):
            for t, d in ((kcol, nk), (qcol, nq), (vbias, v_b)):
                sp.dma_start(t[:], d.rearrange("(h p) -> p h", p=P), allow_slow_non_contiguous=True).then_inc(cols_loaded, 16)
            sp.dma_start(obias[:], o_b.partition_broadcast(P)).then_inc(cols_loaded, 16)
            with sp.Fori(0, QUADS) as i:
                sp.wait_ge(wot_done, FIRST + i * 4)
                sp.dma_start(raw[:], o_w[bass.ds(i * 4 * P, 4 * P), :].rearrange("(h p) d -> p h d", p=P)
                             ).then_inc(raw_loaded, 16)
            sp.wait_ge(wot_done, FIRST + H1)

            def load(g, quad, j):
                h = quad * 4 + j
                cols = bass.ds(g * N, N)
                sp.dma_start(q[:, j, :], q_dram[bass.ds(h, 1), :, cols].rearrange("h p t -> (h p) t")).then_inc(ring[j], 16)
                sp.dma_start(k[:, j, :], k_dram[bass.ds(h, 1), :, cols].rearrange("h p t -> (h p) t")).then_inc(ring[j], 16)
                sp.dma_start(v[:, j].rearrange("p b e -> p (b e)"),
                             v_dram[bass.ds(h, 1), :, bass.ds(g * GB, GB), :].rearrange("h l b e -> (h l) (b e)")
                             ).then_inc(ring[j], 16)

            for j in range(4):
                load(0, 0, j)
            with sp.Fori(1, IT) as it:
                for j in range(4):
                    sp.wait_ge(mixed, (it - 1) * 4 + j + 1)
                    ph.hold(sp, held_sp)
                    load(within(nc, it >> 2, G - 1), within(nc, it & 3, QUADS - 1), j)

        @block.gpsimd
        def _(pool):
            pool.wait_ge(cols_loaded, 64)
            with pool.Fori(0, G) as g:
                xg = K.x[:, bass.ds(g * GB, GB), :]
                nc.gpsimd.tensor_tensor(xg, xg, obias[:].unsqueeze(1).broadcast_to([P, GB, D]), ALU.add
                                        ).then_inc(bias_done, 1)

        @block.scalar
        def _(act):
            for first in (exp_done, probT_done,):
                act.sem_inc(first, FIRST)
            with act.Fori(0, QUADS) as i:
                act.wait_ge(raw_loaded, (i + 1) * 16)
                ph.hold(act, held_act)
                for j in range(4):
                    nc.scalar.activation(wol[:, bass.ds(i * 4 + j, 1), :].rearrange("p a d -> p (a d)"), raw[:, j, :],
                                         ACT.Copy).then_inc(wol_done, 1)
            act.wait_ge(cols_loaded, 64)
            for g in range(G):
                act.wait_ge(spread, g + 1)
                nc.scalar.activation(rkb[:, g * N:(g + 1) * N], ps[:, g, :], ACT.Copy).then_inc(rkb_done, 1)
            nc.scalar.activation(K.scrap[:], K.ones[:, 0:1], ACT.Exp)

            def softmax(it, g, j):
                n = it * 4 + j
                act.wait_ge(max_done, n + 1)
                ph.hold(act, held_act)
                for b in range(GB):
                    ins = nc.scalar.activation(prob[:, j % 2, b, :], ps[:, j % 2, b * S:(b + 1) * S], ACT.Exp,
                                               bias=row[:, j % 2, 1, b:b + 1], scale=rq[:, bass.ds(g * GB + b, 1)],
                                               accum_out=row[:, j % 2, 2, b:b + 1])
                ins.then_inc(exp_done, 1)

            def turned(it, j):
                act.wait_ge(prob_T, it * 4 + j + 1)
                nc.scalar.activation(probT[:, j % 2, :], ps[:, 2 + j % 2, :], ACT.Copy).then_inc(probT_done, 1)

            def head(it, quad, j):
                act.wait_ge(mixed, it * 4 + j + 1)
                if j == 0:
                    act.wait_ge(final, FIRST + it * GB)
                ph.hold(act, held_act)
                nc.scalar.activation(ol[:, j, :], ps[:, 4 + j % 2, :], ACT.Identity,
                                     bias=vbias[:, bass.ds(quad * 4 + j, 1)]).then_inc(ol_done, 1)

            with act.Fori(0, IT) as it:
                g, quad = within(nc, it >> 2, G - 1), within(nc, it & 3, QUADS - 1)
                softmax(it, g, 0)
                softmax(it, g, 1)
                turned(it, 0)
                for j in range(2, 4):
                    softmax(it, g, j)
                    turned(it, j - 1)
                    head(it, quad, j - 2)
                turned(it, 3)
                head(it, quad, 2)
                head(it, quad, 3)

        @block.vector
        def _(dve):
            for first in (wot_done, acc_done, ot_done,):
                dve.sem_inc(first, FIRST)
            own = Own(dve, own_dve)
            with dve.Fori(0, QUADS) as i:
                for j in range(4):
                    dve.wait_ge(wol_done, i * 4 + j + 1)
                    at = bass.ds(i * 4 + j, 1)
                    nc.vector.tensor_tensor(wot[:, at, :].rearrange("p a d -> p (a d)"), raw[:, j, :],
                                            wol[:, at, :].rearrange("p a d -> p (a d)").bitcast(F32),
                                            ALU.subtract).then_inc(wot_done, 1)
            dve.wait_ge(cols_loaded, 64)
            own(nc.vector.scalar_tensor_tensor(kcol[:], kcol[:], DH1 ** -0.5, qcol[:], ALU.mult, ALU.mult))
            dve.wait_ge(rkb_done, G)
            dve.wait_ge(bias_done, G)

            def keys(it, g, quad, j):
                dve.wait_ge(ring[j], (it + 1) * 48)
                nc.vector.scalar_tensor_tensor(kn[:, j % 2, :], k[:, j, :], kcol[:, bass.ds(quad * 4 + j, 1)],
                                               rkb[:, bass.ds(g * N, N)], ALU.mult, ALU.mult).then_inc(kn_done, 1)

            def peak(it, g, j):
                n = it * 4 + j
                dve.wait_ge(scores, n + 1)
                r = row[:, j % 2]
                nc.vector.tensor_reduce(r[:, 0], ps[:, j % 2, :].rearrange("p (b s) -> p b s", b=GB), AX, ALU.max
                                        ).then_inc(row_done, 1)
                dve.wait_ge(row_done, n + 1)
                nc.vector.scalar_tensor_tensor(r[:, 1], r[:, 0], -1.0, rq[:, bass.ds(g * GB, GB)], ALU.mult, ALU.mult
                                               ).then_inc(max_done, 1)

            def divide(it, j):
                n = it * 4 + j
                dve.wait_ge(exp_done, FIRST + n + 1)
                r = row[:, j % 2]
                nc.vector.reciprocal(r[:, 3], r[:, 2]).then_inc(sum_done, 1)
                dve.wait_ge(sum_done, n + 1)
                nc.vector.tensor_tensor(prob[:, j % 2], prob[:, j % 2], r[:, 3].unsqueeze(2).broadcast_to([P, GB, S]),
                                        ALU.mult).then_inc(prob_done, 1)

            def rest(it, quad, j):
                dve.wait_ge(ol_done, it * 4 + j + 1)
                nc.vector.scalar_tensor_tensor(ot[:, j, :], ps[:, 4 + j % 2, :], vbias[:, bass.ds(quad * 4 + j, 1)],
                                               ol[:, j, :].bitcast(F32), ALU.add, ALU.subtract).then_inc(ot_done, 1)

            with dve.Fori(0, IT) as it:
                g, quad = within(nc, it >> 2, G - 1), within(nc, it & 3, QUADS - 1)
                keys(it, g, quad, 0)
                keys(it, g, quad, 1)
                peak(it, g, 0)
                keys(it, g, quad, 2)
                peak(it, g, 1)
                keys(it, g, quad, 3)
                divide(it, 0)
                divide(it, 1)
                for j in range(2, 4):
                    peak(it, g, j)
                    divide(it, j)
                    rest(it, quad, j - 2)
                rest(it, quad, 2)
                rest(it, quad, 3)
                dve.wait_ge(acc_done, FIRST + it * GB)
                for b in range(GB):
                    dve.wait_ge(final, FIRST + it * GB + b + 1)
                    xb = K.x[:, bass.ds(g * GB + b, 1), :].rearrange("p a d -> p (a d)")
                    nc.vector.tensor_tensor(xb, xb, ps[:, 6 + b % 2, :], ALU.add).then_inc(acc_done, 1)

        @block.tensor
        def _(pe):
            for first in (final,):
                pe.sem_inc(first, FIRST)
            for g in range(G):
                for b in range(GB):
                    ins = nc.tensor.matmul(ps[:, g, b * S:(b + 1) * S],
                                           rk[:, g * GB + b:g * GB + b + 1].broadcast_to([P, P]), K.ident[:],
                                           start=True, stop=True)
                ins.then_inc(spread, 1)
            pe.wait_ge(rkb_done, G)
            pe.wait_ge(wot_done, FIRST + H1)

            def score(it, j):
                pe.wait_ge(kn_done, it * 4 + j + 1)
                if j >= 2:
                    pe.wait_ge(exp_done, FIRST + it * 4 + j - 1)
                else:
                    pe.wait_ge(exp_done, FIRST + it * 4)
                for b in range(GB):
                    s = slice(b * S, (b + 1) * S)
                    ins = nc.tensor.matmul(ps[:, j % 2, s], q[:, j, s], kn[:, j % 2, s], start=True, stop=True)
                ins.then_inc(scores, 1)

            def turn_prob(it, j):
                pe.wait_ge(prob_done, it * 4 + j + 1)
                if j >= 2:
                    pe.wait_ge(probT_done, FIRST + it * 4 + j - 1)
                else:
                    pe.wait_ge(probT_done, FIRST + it * 4)
                for b in range(GB):
                    ins = nc.tensor.transpose(ps[:, 2 + j % 2, b * S:(b + 1) * S], prob[:, j % 2, b, :], K.ident[:])
                ins.then_inc(prob_T, 1)

            def mix(it, j):
                pe.wait_ge(probT_done, FIRST + it * 4 + j + 1)
                if j >= 2:
                    pe.wait_ge(ot_done, FIRST + it * 4 + j - 1)
                else:
                    pe.wait_ge(ot_done, FIRST + it * 4)
                for b in range(GB):
                    s = slice(b * S, (b + 1) * S)
                    ins = nc.tensor.matmul(ps[:, 4 + j % 2, s], v[:, j, b, :], probT[:, j % 2, s], start=True, stop=True)
                ins.then_inc(mixed, 1)

            with pe.Fori(0, IT) as it:
                quad = within(nc, it & 3, QUADS - 1)
                score(it, 0)
                score(it, 1)
                turn_prob(it, 0)
                for j in range(2, 4):
                    score(it, j)
                    turn_prob(it, j - 1)
                    mix(it, j - 2)
                turn_prob(it, 3)
                mix(it, 2)
                mix(it, 3)
                pe.wait_ge(ot_done, FIRST + it * 4 + 4)
                for b in range(GB):
                    if b >= 2:
                        pe.wait_ge(acc_done, FIRST + it * GB + b - 1)
                    else:
                        pe.wait_ge(acc_done, FIRST + it * GB)
                    rows = slice(b * S, (b + 1) * S)
                    for j in range(4):
                        w = bass.ds(quad * 4 + j, 1)
                        ins = three_passes(nc, ps[:, 6 + b % 2, :], ol[:, j, rows], ot[:, j, rows],
                                           wol[:, w, :].rearrange("p a d -> p (a d)"),
                                           wot[:, w, :].rearrange("p a d -> p (a d)"), j == 0, j == 3)
                    ins.then_inc(final, 1)


def ternary(nc, K, lead, trail, w_dram, b_dram, out):
    with Phase(nc, "ternary") as ph:
        sb, sem = ph.sb, ph.sem
        w = sb("w", [P, C, D])
        size = sb("size", [P, C, D])
        low = sb("low", [P, C, D])
        tern = sb("tern", [P, C, D])
        ternT = sb("ternT", [P, C, D], F32R)
        bias = sb("bias", [P, D])
        rows = sb("rows", [P, 1])
        scale = sb("scale", [P, 1])
        edge = sb("edge", [P, 2])
        loaded, abs_done, sums, own_dve, tern_done, turned, copied = (
            sem("loaded"), sem("abs_done"), sem("sums"), sem("own_dve"), sem("tern_done"), sem("turned"), sem("copied"))
        bias_done, product, y_done, stored = sem("bias_done"), sem("product"), sem("y_done"), sem("stored")
        block = ph.block()
        ps = K.ps

        @block.sync
        def _(sp):
            sp.dma_start(w[:], w_dram.rearrange("(c p) i -> p c i", p=P)).then_inc(loaded, 16)
            sp.dma_start(bias[:], b_dram.partition_broadcast(P)).then_inc(loaded, 16)
            with sp.Fori(0, G) as g:
                sp.wait_ge(y_done, (g + 1) * GB)
                at = bass.ds(g * GB, GB)
                sp.dma_start(out[at].rearrange("b s d -> s b d"), K.x[:, at, :]).then_inc(stored, 16)
            sp.wait_ge(stored, 16 * G)

        @block.gpsimd
        def _(pool):
            pool.wait_ge(loaded, 32)
            with pool.Fori(0, G) as g:
                xg = K.x[:, bass.ds(g * GB, GB), :]
                nc.gpsimd.tensor_tensor(xg, xg, bias[:].unsqueeze(1).broadcast_to([P, GB, D]), ALU.add
                                        ).then_inc(bias_done, 1)

        @block.scalar
        def _(act):
            act.wait_ge(loaded, 32)
            nc.scalar.activation(size[:], w[:], ACT.Abs, accum_out=rows[:]).then_inc(abs_done, 1)
            for c in range(C):
                act.wait_ge(turned, c + 1)
                nc.scalar.activation(ternT[:, c, :], ps[:, c, :], ACT.Copy).then_inc(copied, 1)

        @block.vector
        def _(dve):
            own = Own(dve, own_dve)
            dve.wait_ge(sums, 1)
            own(nc.vector.tensor_scalar(scale[:], ps[:, 4, 0:1], 1.0 / (D * D), None, ALU.mult))
            nc.vector.tensor_scalar(edge[:, 0:1], scale[:], 1e-10, 0.5, ALU.add, ALU.mult)
            own(nc.vector.tensor_scalar(edge[:, 1:2], scale[:], 1e-10, -0.5, ALU.add, ALU.mult))
            flat = lambda t: t[:].rearrange("p c d -> p (c d)")
            own(nc.vector.tensor_scalar(flat(low), flat(w), edge[:, 1:2], None, ALU.is_lt))
            nc.vector.scalar_tensor_tensor(flat(tern), flat(w), edge[:, 0:1], flat(low), ALU.is_gt, ALU.subtract
                                           ).then_inc(tern_done, 1)
            with dve.Fori(0, G) as g:
                dve.wait_ge(bias_done, g + 1)
                for b in range(GB):
                    dve.wait_ge(product, g * GB + b + 1)
                    xb = K.x[:, bass.ds(g * GB + b, 1), :].rearrange("p a d -> p (a d)")
                    nc.vector.scalar_tensor_tensor(xb, ps[:, b, :], scale[:, 0:1], xb, ALU.mult, ALU.add
                                                   ).then_inc(y_done, 1)

        @block.tensor
        def _(pe):
            pe.wait_ge(abs_done, 1)
            nc.tensor.matmul(ps[:, 4, 0:1], K.ones[:], rows[:], start=True, stop=True).then_inc(sums, 1)
            pe.wait_ge(tern_done, 1)
            for c in range(C):
                for o in range(C):
                    ins = nc.tensor.transpose(ps[:, c, o * P:(o + 1) * P], tern[:, o, c * P:(c + 1) * P], K.ident[:])
                ins.then_inc(turned, 1)
            pe.wait_ge(copied, C)
            for b in range(B):
                if b >= GB:
                    pe.wait_ge(y_done, b - GB + 1)
                r = slice(b * S, (b + 1) * S)
                for c in range(C):
                    nc.tensor.matmul(ps[:, b % GB, :], lead[:, c, r], ternT[:, c, :], start=(c == 0), stop=False)
                    ins = nc.tensor.matmul(ps[:, b % GB, :], trail[:, c, r], ternT[:, c, :], start=False,
                                           stop=(c == C - 1))
                ins.then_inc(product, 1)


class Kept:
    pass


def operands(ph):
    return ph.sb("lead", [P, C, T], F32R), ph.sb("trail", [P, C, T], F32R)


def two_layers(nc, a, out):
    q_dram = nc.dram_tensor("q_heads", [H1, P, T], F32).ap()
    k_dram = nc.dram_tensor("k_heads", [H1, P, T], F32).ap()
    v_dram = nc.dram_tensor("v_heads", [H1, S, B, DH1], F32).ap()
    with ExitStack() as stack:
        kept = lambda name, shape: stack.enter_context(nc.sbuf_tensor(name, shape, F32))
        K = Kept()
        K.x = kept("x_kept", [P, B, D])
        K.ident, K.ones = kept("ident", [P, P]), kept("ones", [P, P])
        K.eps5, K.eps6 = kept("eps5", [P, 1]), kept("eps6", [P, 1])
        K.scrap = kept("scrap", [P, 1])
        rq, rk = kept("rq", [P, B]), kept("rk", [P, B])
        K.ps = stack.enter_context(nc.psum_tensor("banks", [P, 8, 512], F32))
        setup(nc, K, a["x"])
        with Phase(nc, "of_ctx") as ph:
            lead, trail = operands(ph)
            turn(nc, K, "turn_ctx", lead, trail, ctx_dram=a["ctx_2048"])
            project(nc, K, "keys", lead, trail, a["L1_xattn_ki_w"], a["L1_xattn_ki_b"], k_dram, rk)
            values(nc, K, lead, trail, a["L1_xattn_vi_w"], v_dram)
        mlstm(nc, K, a["ctx_2048"], a["L0_xattn_Wi"], a["L0_xattn_bi"], a["L0_xattn_Wf"], a["L0_xattn_bf"],
              a["L0_xattn_ln_scale"])
        with Phase(nc, "of_x1") as ph:
            lead, trail = operands(ph)
            logits, wd = ph.sb("logits", [P, B, E]), ph.sb("wd", [P, E + 1, B])
            turn(nc, K, "turn_x1", lead, trail, rms=a["L0_ffn_rms_weight"], logits=logits,
                 router=a["L0_ffn_router_w"])
            choose(nc, K, logits, wd)
            experts(nc, K, lead, trail, wd, [a[f"L0_ffn_w_{n}"] for n in ("gate", "up", "down")],
                    [a[f"L0_ffn_sw_{n}"] for n in ("gate", "up", "down")])
        with Phase(nc, "of_x2") as ph:
            lead, trail = operands(ph)
            turn(nc, K, "turn_x2", lead, trail)
            project(nc, K, "queries", lead, trail, a["L1_xattn_q_w"], a["L1_xattn_q_b"], q_dram, rq)
        attend(nc, K, q_dram, k_dram, v_dram, a["L1_xattn_o_w"], a["L1_xattn_o_b"], a["L1_xattn_vi_b"],
               a["L1_xattn_nq_s"], a["L1_xattn_nki_s"], rq, rk)
        with Phase(nc, "of_x3") as ph:
            lead, trail = operands(ph)
            turn(nc, K, "turn_x3", lead, trail)
            ternary(nc, K, lead, trail, a["L1_ffn_weight"], a["L1_ffn_bias"], out)


_INS = ['x', 'ctx_2048', 'L0_xattn_Wi', 'L0_xattn_bi', 'L0_xattn_Wf', 'L0_xattn_bf', 'L0_xattn_ln_scale',
        'L0_ffn_rms_weight', 'L0_ffn_router_w', 'L0_ffn_w_gate', 'L0_ffn_w_up', 'L0_ffn_w_down',
        'L0_ffn_sw_gate', 'L0_ffn_sw_up', 'L0_ffn_sw_down', 'L1_xattn_q_w', 'L1_xattn_q_b',
        'L1_xattn_ki_w', 'L1_xattn_ki_b', 'L1_xattn_vi_w', 'L1_xattn_vi_b', 'L1_xattn_o_w', 'L1_xattn_o_b',
        'L1_xattn_nq_s', 'L1_xattn_nki_s', 'L1_ffn_weight', 'L1_ffn_bias']


def kernel(**inputs):
    import concourse.bacc as bacc
    from concourse.bass_utils import run_bass_kernel_spmd

    nc = bacc.Bacc("TRN2", target_bir_lowering=False, num_devices=1)
    arrays, args = {}, {}
    for name in _INS:
        v = np.ascontiguousarray(inputs[name])
        arrays[f"in_{name}"] = v
        args[name] = nc.dram_tensor(f"in_{name}", v.shape, mybir.dt.from_np(v.dtype), kind="ExternalInput").ap()
    out = nc.dram_tensor("out", (B, S, D), F32, kind="ExternalOutput").ap()
    two_layers(nc, args, out)
    return run_bass_kernel_spmd(nc, [arrays], core_ids=[0]).results[0]["out"]
```

```python
from contextlib import ExitStack

import numpy as np

import concourse.bass as bass
from concourse import mybir

F32 = mybir.dt.float32
F32R = mybir.dt.float32r
BF16 = mybir.dt.bfloat16
U32 = mybir.dt.uint32
ALU = mybir.AluOpType
ACT = mybir.ActivationFunctionType
AX = mybir.AxisListType.X

P = 128
B, S, D = 16, 128, 512
T = B * S
C = D // P
GB = 4
G = B // GB
N = GB * S
H0, DH0 = 16, 32
E, F = 8, 256
FC = F // P
H1, DH1 = 16, 128
INNER = H1 * DH1
FAR = 1e30
FIRST = 1


class Own:

    def __init__(self, eng, sem):
        self.eng, self.sem, self.base, self.done, self.i, self.per = eng, sem, 0, 0, 0, 0

    def enter(self, i, per):
        self.base, self.done, self.i, self.per = self.base + self.done, 0, i, per

    def leave(self, trips):
        assert self.done == self.per, (self.done, self.per)
        self.base, self.done, self.i, self.per = self.base + trips * self.per, 0, 0, 0

    def __call__(self, ins):
        ins.then_inc(self.sem, 1)
        self.done += 1
        self.eng.wait_ge(self.sem, self.i * self.per + (self.base + self.done))


class Phase:

    def __init__(self, nc, name):
        self.nc, self.name, self.stack, self.sems = nc, name, ExitStack(), []

    def __enter__(self):
        self.stack.__enter__()
        return self

    def __exit__(self, *a):
        self.stack.__exit__(*a)
        if self.sems:
            self.nc.clear_and_free_semaphores(self.sems)
            self.nc.all_engine_barrier()

    def sb(self, name, shape, dt=F32):
        return self.stack.enter_context(self.nc.sbuf_tensor(f"{self.name}_{name}", shape, dt))

    def sem(self, name):
        self.sems.append(self.nc.alloc_semaphore(name=f"{self.name}_{name}"))
        return self.sems[-1]

    def hold(self, eng, sem):
        eng.sem_inc(sem, 1)

    def block(self):
        return self.stack.enter_context(self.nc.Block())


def within(nc, v, hi):
    return nc.s_assert_within(v, 0, hi, skip_runtime_bounds_check_because="the loop's count bounds it")


def three_passes(nc, out, lead_l, trail_l, lead_r, trail_r, first, last):
    nc.tensor.matmul(out, lead_l, lead_r, start=first, stop=False)
    nc.tensor.matmul(out, lead_l, trail_r, start=False, stop=False)
    return nc.tensor.matmul(out, trail_l, lead_r, start=False, stop=last)


def setup(nc, K, x_dram):
    with Phase(nc, "setup") as ph:
        x_loaded, blank, made = ph.sem("x_loaded"), ph.sem("blank"), ph.sem("made")
        block = ph.block()

        @block.sync
        def _(sp):
            sp.dma_start(K.x[:], x_dram.rearrange("b s d -> s b d")).then_inc(x_loaded, 16)
            sp.wait_ge(x_loaded, 16)

        @block.gpsimd
        def _(pool):
            nc.gpsimd.memset(K.ident[:], 0.0).then_inc(blank, 1)
            nc.gpsimd.memset(K.eps5[:], 1e-5)
            nc.gpsimd.memset(K.eps6[:], 1e-6)
            nc.gpsimd.memset(K.ones[:], 1.0).then_inc(blank, 1)
            pool.wait_ge(blank, 2)
            nc.gpsimd.affine_select(out=K.ident[:], in_=K.ident[:], compare_op=ALU.not_equal, fill=1.0,
                                    base=0, pattern=[[-1, P]], channel_multiplier=1).then_inc(made, 1)
            pool.wait_ge(made, 1)


class Gates:
    pass


def gates(nc, K, M, ctx_dram, Wi, bi, Wf, bf):
    with Phase(nc, "gates") as ph:
        sb, sem = ph.sb, ph.sem
        ctx = sb("ctx", [P, GB, D])
        xn = sb("xn", [P, GB, D])
        w_gate = sb("w_gate", [P, 3, C, 64])
        w_ctx = sb("w_ctx", [P, C, 64])
        bias = sb("bias", [64, 1])
        stats = sb("stats", [P, B, 6])
        mv = sb("mv", [P, B, 2])
        rstd = sb("rstd", [P, B])
        keep = sb("keep", [32, GB, S])
        pen = sb("pen", [32, GB, S])
        f_abs = sb("f_abs", [64, N])
        f_min = sb("f_min", [64, N])
        logf = sb("logf", [32, N])
        cumf = sb("cumf", [32, N])
        arow = sb("arow", [32, T])
        grow = sb("grow", [32, T])
        mrow = sb("mrow", [32, T])

        loaded_w, loaded_ctx = sem("loaded_w"), sem("loaded_ctx")
        masks, own_dve, own_act, own_pool = sem("masks"), sem("own_dve"), sem("own_act"), sem("own_pool")
        wsum, stats_done, sd_done, xn_done = sem("wsum"), sem("stats_done"), sem("sd_done"), sem("xn_done")
        turned, xT_done, cT_done = sem("turned"), sem("xT_done"), sem("cT_done")
        gates_done, sp_done, fmin_done = sem("gates_done"), sem("sp_done"), sem("fmin_done")
        a_done, m_done, em_done, nat_T, nat_done = sem("a_done"), sem("m_done"), sem("em_done"), sem("nat_T"), sem("nat_done")
        g_lead, g_trail = sem("g_lead"), sem("g_trail")
        held_act = sem("held_act")
        block = ph.block()
        ps = K.ps

        @block.sync
        def _(sp):
            sp.dma_start(ctx[:], ctx_dram[0:GB].rearrange("b s d -> s b d")).then_inc(loaded_ctx, 16)
            sp.wait_ge(masks, 1)
            for w, at in ((Wi, 0), (Wf, 32)):
                for part in range(3):
                    sp.dma_start(w_gate[:, part, :, at:at + H0],
                                 w[part * D:(part + 1) * D, :].rearrange("(c p) h -> p c h", p=P)
                                 ).then_inc(loaded_w, 16)
            sp.dma_start(bias[0:H0, :], bi.rearrange("(h a) -> h a", a=1)).then_inc(loaded_w, 16)
            sp.dma_start(bias[32:32 + H0, :], bf.rearrange("(h a) -> h a", a=1)).then_inc(loaded_w, 16)
            with sp.Fori(1, G) as g:
                sp.wait_ge(turned, FIRST + (g - 1) * (2 * C) + C)
                sp.dma_start(ctx[:], ctx_dram[bass.ds(g * GB, GB)].rearrange("b s d -> s b d")
                             ).then_inc(loaded_ctx, 16)

        @block.gpsimd
        def _(pool):
            own = Own(pool, own_pool)
            nc.gpsimd.memset(w_gate[:], 0.0)
            nc.gpsimd.memset(bias[:], 0.0).then_inc(masks, 1)
            nc.gpsimd.memset(keep[:], 1.0)
            own(nc.gpsimd.memset(pen[:], 0.0))
            nc.gpsimd.memset(keep[:, :, 0:1], 0.0)
            nc.gpsimd.memset(pen[:, :, 0:1], -FAR).then_inc(masks, 1)
            pool.wait_ge(masks, 2)

        @block.scalar
        def _(act):
            own = Own(act, own_act)
            act.wait_ge(stats_done, 1)
            nc.scalar.activation(rstd[:], mv[:, :, 1], ACT.Sqrt, bias=K.eps5[:, 0:1]).then_inc(sd_done, 1)
            act.wait_ge(loaded_w, 8 * 16)
            with act.Fori(0, G) as g:
                own.enter(g, 2)
                for c in range(C):
                    act.wait_ge(turned, FIRST + g * (2 * C) + c + 1)
                    ph.hold(act, held_act)
                    nc.scalar.activation(M.ctxT[:, c, bass.ds(g * N, N)], ps[:, c, :], ACT.Copy).then_inc(cT_done, 1)
                act.wait_ge(fmin_done, g + 1)
                fa = f_abs[32:64, :]
                own(nc.scalar.activation(fa, ps[32:64, 6, :], ACT.Abs, bias=bias[32:64, :]))
                own(nc.scalar.activation(fa, fa, ACT.Exp, scale=-1.0))
                nc.scalar.activation(fa, fa, ACT.Ln, bias=1.0).then_inc(sp_done, 1)
            own.leave(G)
            act.wait_ge(m_done, G)
            nc.scalar.activation(mrow[:], mrow[:], ACT.Exp, scale=-1.0).then_inc(em_done, 1)
            nc.scalar.activation(M.g[0:32, :], grow[:], ACT.Copy).then_inc(g_lead, 1)
            for kind in range(2):
                act.wait_ge(nat_T, kind + 1)
                nc.scalar.activation(M.nat[:, kind].rearrange("p g b h -> p (g b) h"),
                                     ps[:, kind, :].rearrange("p (n h) -> p n h", h=32)[:, :, 0:H0],
                                     ACT.Copy).then_inc(nat_done, 1)
            act.wait_ge(g_trail, 1)
            act.wait_ge(nat_done, 2)

        @block.vector
        def _(dve):
            own = Own(dve, own_dve)
            for b in range(B):
                ins = nc.vector.bn_stats(stats[:, b, :], K.x[:, b, :])
            own(ins)
            for b in range(B):
                ins = nc.vector.bn_aggr(mv[:, b, :], stats[:, b, :])
            ins.then_inc(stats_done, 1)
            dve.wait_ge(sd_done, 1)
            own(nc.vector.reciprocal(rstd[:], rstd[:]))

            def normalise(g):
                for b in range(GB):
                    at = g * GB + b
                    ins = nc.vector.tensor_scalar(xn[:, b, :], K.x[:, bass.ds(at, 1), :].rearrange("p a d -> p (a d)"),
                                                  mv[:, bass.ds(at, 1), 0:1].rearrange("p a d -> p (a d)"),
                                                  rstd[:, bass.ds(at, 1)], ALU.subtract, ALU.mult)
                ins.then_inc(xn_done, 1)

            normalise(0)
            dve.wait_ge(loaded_w, 8 * 16)
            nc.vector.tensor_tensor(w_ctx[:], w_gate[:, 1], w_gate[:, 2], ALU.add).then_inc(wsum, 1)
            dve.wait_ge(masks, 2)
            with dve.Fori(0, G) as g:
                own.enter(g, 4)
                cols = bass.ds(g * N, N)
                for c in range(C):
                    dve.wait_ge(turned, FIRST + g * (2 * C) + C + c + 1)
                    nc.vector.tensor_copy(M.xnT[:, c, cols], ps[:, 4 + c % 2, :]).then_inc(xT_done, 1)
                normalise(within(nc, (g + 1) & (G - 1), G - 1))
                dve.wait_ge(gates_done, g + 1)
                fm = f_min[32:64, :]
                nc.vector.tensor_scalar(fm, ps[32:64, 6, :], bias[32:64, :], 0.0, ALU.add, ALU.min).then_inc(fmin_done, 1)
                dve.wait_ge(sp_done, g + 1)
                own(nc.vector.tensor_tensor(logf[:], fm, f_abs[32:64, :], ALU.subtract))
                own(nc.vector.tensor_tensor_scan(cumf[:], keep[:].rearrange("p b s -> p (b s)"), logf[:], 0.0,
                                                 ALU.mult, ALU.add))
                own(nc.vector.scalar_tensor_tensor(arow[:, cols], ps[0:32, 6, :], bias[0:32, :], cumf[:], ALU.add,
                                                   ALU.subtract))
                own(nc.vector.tensor_tensor_scan(grow[:, cols], pen[:].rearrange("p b s -> p (b s)"), arow[:, cols], 0.0,
                                                 ALU.add, ALU.max))
                nc.vector.tensor_tensor(mrow[:, cols], cumf[:], grow[:, cols], ALU.add).then_inc(m_done, 1)
            own.leave(G)
            dve.wait_ge(g_lead, 1)
            nc.vector.tensor_tensor(M.g[32:64, :], grow[:], M.g[0:32, :].bitcast(F32), ALU.subtract).then_inc(g_trail, 1)

        @block.tensor
        def _(pe):
            pe.sem_inc(turned, FIRST)
            pe.wait_ge(wsum, 1)
            with pe.Fori(0, G) as g:
                cols = bass.ds(g * N, N)
                pe.wait_ge(loaded_ctx, g * 16 + 16)
                for k in range(2 * C):
                    c, src = k % C, (ctx if k < C else xn)
                    if k == C:
                        pe.wait_ge(xn_done, g + 1)
                    if k >= C + 2:
                        pe.wait_ge(xT_done, g * C + c - 1)
                    for b in range(GB):
                        ins = nc.tensor.transpose(ps[:, k if k < C else C + c % 2, b * S:(b + 1) * S],
                                                  src[:, b, c * P:(c + 1) * P], K.ident[:])
                    ins.then_inc(turned, 1)
                pe.wait_ge(cT_done, g * C + C)
                for c in range(C):
                    nc.tensor.matmul(ps[0:64, 6, :], w_ctx[:, c, :], M.ctxT[:, c, cols], start=(c == 0), stop=False)
                pe.wait_ge(xT_done, g * C + C)
                for c in range(C):
                    ins = nc.tensor.matmul(ps[0:64, 6, :], w_gate[:, 0, c, :], M.xnT[:, c, cols], start=False,
                                           stop=(c == C - 1))
                ins.then_inc(gates_done, 1)
            pe.wait_ge(m_done, G)
            for kind, row in ((0, arow), (1, mrow)):
                if kind:
                    pe.wait_ge(em_done, 1)
                for b in range(B):
                    ins = nc.tensor.transpose(ps[:, kind, b * 32:(b + 1) * 32], row[:, b * S:(b + 1) * S],
                                              K.ident[0:32, 0:32])
                ins.then_inc(nat_T, 1)


def heads(nc, K, M, ctx_dram, ln_scale):
    PER = H0
    PAIRS = PER // 2
    RING = 4
    with Phase(nc, "heads") as ph:
        sb, sem = ph.sb, ph.sem
        ctx = sb("ctx", [P, GB, D])
        ctx1 = sb("ctx1", [P, 2, GB, H0, DH0 + 1])
        kT = sb("kT", [P, C, N])
        qz = sb("qz", [P, 2, 4, N])
        ident2 = sb("ident2", [64, H0])
        pick = sb("pick", [64, H0], F32R)
        far = sb("far", [P, GB, S], BF16)
        ident_b = sb("ident_b", [P, P], BF16)
        arg = sb("arg", [P, 2, GB, S])
        dec = sb("dec", [P, 2, GB, S])
        cmat = sb("cmat", [P, RING, GB, S])
        hraw = sb("hraw", [P, 2, GB, H0, DH0 + 1])
        sq = sb("sq", [P, GB * H0, DH0])
        small = sb("small", [P, 6, GB * H0])
        lnb = sb("lnb", [P, D])

        loaded_w, loaded_ctx, masks, pick_done = sem("loaded_w"), sem("loaded_ctx"), sem("masks"), sem("pick_done")
        own_dve, own_pool, ctx1_done, kT_done, qz_done = sem("own_dve"), sem("own_pool"), sem("ctx1_done"), sem("kT_done"), sem("qz_done")
        qk, gb, arg_done, dec_done, c_done, pv, h_done = (
            sem("qk"), sem("gb"), sem("arg_done"), sem("dec_done"), sem("c_done"), sem("pv"), sem("h_done"))
        abs_done, mean_done, centred, sq_done, var_done, std_done, fac_done, norm_done, res_done = (
            sem("abs_done"), sem("mean_done"), sem("centred"), sem("sq_done"), sem("var_done"), sem("std_done"),
            sem("fac_done"), sem("norm_done"), sem("res_done"))
        held_act, held_pool, held_pe, held_sp, held_dve = (
            sem("held_act"), sem("held_pool"), sem("held_pe"), sem("held_sp"), sem("held_dve"))

        def after(g, n):
            if n < PER:
                return g, n
            return ((g + 1) % G if isinstance(g, int) else within(nc, (g + 1) & (G - 1), G - 1)), n - PER

        def half(g):
            return g % 2 if isinstance(g, int) else within(nc, g & 1, 1)

        def raw_heads(g):
            return hraw[:, bass.ds(half(g), 1)].rearrange("p a b h e -> p (a b h) e")

        block = ph.block()
        ps = K.ps

        @block.sync
        def _(sp):
            sp.dma_start(lnb[:], ln_scale.partition_broadcast(P)).then_inc(loaded_w, 16)

            def load(g):
                sp.dma_start(ctx[:], ctx_dram[bass.ds(g * GB, GB)].rearrange("b s d -> s b d")).then_inc(loaded_ctx, 16)

            load(0)
            with sp.Fori(0, G) as g:
                sp.wait_ge(ctx1_done, g + 1)
                ph.hold(sp, held_sp)
                load(within(nc, (g + 1) & (G - 1), G - 1))
            sp.wait_ge(loaded_ctx, 16 * (G + 1))
            sp.wait_ge(loaded_w, 16)

        def shift(eng, g):
            h = raw_heads(g)[:, :, 0:DH0]
            eng.tensor_tensor(h, h, small[:, 2].unsqueeze(2).broadcast_to([P, GB * H0, DH0]), ALU.subtract
                              ).then_inc(centred, 1)

        @block.gpsimd
        def _(pool):
            pool.sem_inc(norm_done, FIRST)
            pool.sem_inc(res_done, FIRST)
            own = Own(pool, own_pool)
            nc.gpsimd.memset(qz[:], 0.0)
            nc.gpsimd.memset(ctx1[:], 1.0)
            nc.gpsimd.memset(ident2[:], 0.0)
            nc.gpsimd.memset(far[:], 0.0)
            own(nc.gpsimd.memset(ident_b[:], 0.0))
            nc.gpsimd.affine_select(out=far[:], in_=far[:], compare_op=ALU.is_ge, fill=FAR, base=0,
                                    pattern=[[0, GB], [1, S]], channel_multiplier=-1)
            nc.gpsimd.affine_select(out=ident_b[:], in_=ident_b[:], compare_op=ALU.not_equal, fill=1.0,
                                    base=0, pattern=[[-1, P]], channel_multiplier=1)
            own(nc.gpsimd.affine_select(out=ident2[:], in_=ident2[:], compare_op=ALU.not_equal, fill=1.0,
                                        base=0, pattern=[[-1, H0]], channel_multiplier=1))
            nc.gpsimd.affine_select(out=ident2[:], in_=ident2[:], compare_op=ALU.not_equal, fill=1.0,
                                    base=-32, pattern=[[-1, H0]], channel_multiplier=1).then_inc(masks, 1)

            def values(g, count):
                pool.wait_ge(loaded_ctx, (count + 1) * 16)
                ph.hold(pool, held_pool)
                nc.gpsimd.tensor_copy(ctx1[:, bass.ds(half(g), 1), :, :, 0:DH0].rearrange("p a b h e -> p (a b h) e"),
                                      ctx[:].rearrange("p b (h e) -> p (b h) e", e=DH0)).then_inc(ctx1_done, 1)

            pool.wait_ge(loaded_w, 16)
            values(0, 0)
            values(1, 1)
            with pool.Fori(1, G) as g:
                own.enter(g - 1, 1)
                pool.wait_ge(pv, g * PER)
                values(after(g, PER)[0], g + 1)
                pool.wait_ge(mean_done, g)
                ph.hold(pool, held_pool)
                shift(nc.gpsimd, g - 1)
                pool.wait_ge(fac_done, g)
                ph.hold(pool, held_pool)
                nc.gpsimd.tensor_tensor(sq[:], raw_heads(g - 1)[:, :, 0:DH0],
                                        small[:, 5].unsqueeze(2).broadcast_to([P, GB * H0, DH0]),
                                        ALU.mult).then_inc(norm_done, 1)
                pool.wait_ge(norm_done, FIRST + g)
                ph.hold(pool, held_pool)
                out = sq[:].rearrange("p (b h) e -> p b (h e)", b=GB)
                own(nc.gpsimd.tensor_tensor(out, out, lnb[:].unsqueeze(1).broadcast_to([P, GB, D]), ALU.mult))
                xg = K.x[:, bass.ds((g - 1) * GB, GB), :]
                nc.gpsimd.tensor_tensor(xg, xg, out, ALU.add).then_inc(res_done, 1)
            own.leave(G - 1)

        @block.scalar
        def _(act):
            act.wait_ge(masks, 1)
            nc.scalar.activation(pick[:], ident2[:], ACT.Copy).then_inc(pick_done, 1)

            def keys(g, c):
                nc.scalar.activation(kT[:, c, :], M.ctxT[:, c, bass.ds(g * N, N)], ACT.Copy).then_inc(kT_done, 1)

            def query(g, h):
                c, j = divmod(h, 4)
                r = slice(32 * j, 32 * j + 32)
                nc.scalar.activation(qz[r, c % 2, j, :], M.xnT[r, c, bass.ds(g * N, N)], ACT.Copy).then_inc(qz_done, 1)

            for c in range(C):
                keys(0, c)
            for h in range(8):
                query(0, h)
            nc.scalar.activation(K.scrap[:], K.ones[:, 0:1], ACT.Exp)

            def exp(g, n, first):
                act.wait_ge(arg_done, g * PER + n + 1)
                if not (first and n < 2):
                    act.wait_ge(c_done, g * PER + n - 1)
                nc.scalar.activation(dec[:, n % 2], arg[:, n % 2], ACT.Exp).then_inc(dec_done, 1)

            def pair(g, k):
                act.wait_ge(pv, g * PER + 2 * k + 2)
                if k == 0 and not (isinstance(g, int) and g == 0):
                    act.wait_ge(norm_done, FIRST + g - 1)
                ph.hold(act, held_act)
                nc.scalar.activation(hraw[:, bass.ds(half(g), 1), :, 2 * k:2 * k + 2, :].rearrange("p a b j e -> p (a b) j e"),
                                     ps[:, 2 + k % 2, 0:GB * 2 * (DH0 + 1)].rearrange("p (b j e) -> p b j e", b=GB, j=2),
                                     ACT.Copy).then_inc(h_done, 1)

            def row_sums(g):
                act.wait_ge(h_done, (g + 1) * PAIRS)
                ph.hold(act, held_act)
                nc.scalar.activation(small[:, 0], raw_heads(g)[:, :, DH0], ACT.Abs).then_inc(abs_done, 1)

            def square(g):
                act.wait_ge(centred, g + 1)
                act.wait_ge(res_done, FIRST + g)
                ph.hold(act, held_act)
                nc.scalar.activation(sq[:], raw_heads(g)[:, :, 0:DH0], ACT.Square).then_inc(sq_done, 1)

            def deviation(g):
                act.wait_ge(var_done, g + 1)
                nc.scalar.activation(small[:, 4], small[:, 3], ACT.Sqrt, bias=K.eps6[:, 0:1]).then_inc(std_done, 1)

            def body(g, first):
                for n in range(PER):
                    exp(g, n + 2, first)
                    if n % 2 == 0:
                        if n:
                            pair(g, n // 2 - 1)
                        elif not first:
                            pair(g - 1, PAIRS - 1)
                    if n % 4 == 2:
                        act.wait_ge(qk, g * PAIRS + (n // 4) * 2 + 2)
                        ph.hold(act, held_act)
                        keys(after(g, PER)[0], n // 4)
                    if n or not first:
                        act.wait_ge(qk, g * PAIRS + (n - 1) // 4 * 2 + 2)
                        ph.hold(act, held_act)
                        query(*after(g, n + 7))
                    if not first:
                        if n == 1:
                            row_sums(g - 1)
                        if n == 9:
                            square(g - 1)
                        if n == 12:
                            deviation(g - 1)

            exp(0, 0, True)
            exp(0, 1, True)
            body(0, True)
            with act.Fori(1, G) as g:
                body(g, False)
            pair(G - 1, PAIRS - 1)
            row_sums(G - 1)
            square(G - 1)
            deviation(G - 1)

        @block.vector
        def _(dve):
            own = Own(dve, own_dve)

            def argument(g, n):
                g1, h = after(g, n)
                dve.wait_ge(gb, g * PER + n + 1)
                nc.vector.tensor_tensor(arg[:, n % 2], M.nat[:, 0, bass.ds(g1, 1), :, h:h + 1].rearrange("p a b h -> p (a b) h")
                                        .broadcast_to([P, GB, S]),
                                        ps[:, n % 2, :].rearrange("p (b s) -> p b s", b=GB),
                                        ALU.subtract).then_inc(arg_done, 1)

            def decayed(g, n, first):
                if n % 2 == 0:
                    dve.wait_ge(qk, g * PAIRS + n // 2 + 1)
                dve.wait_ge(dec_done, g * PER + n + 1)
                if not (first and n < RING):
                    dve.wait_ge(pv, g * PER + n - RING + 1)
                nc.vector.scalar_tensor_tensor(cmat[:, n % RING].rearrange("p b s -> p (b s)"), ps[:, 4 + n % 4, :],
                                               DH0 ** -0.5, dec[:, n % 2].rearrange("p b s -> p (b s)"),
                                               ALU.mult, ALU.mult).then_inc(c_done, 1)

            def divisor(g):
                dve.wait_ge(abs_done, g + 1)
                own(nc.vector.tensor_tensor(small[:, 1], small[:, 0],
                                            M.nat[:, 1, bass.ds(g, 1)].rearrange("p a b h -> p (a b h)"), ALU.max))
                own(nc.vector.tensor_scalar(small[:, 1], small[:, 1], 1e-6, None, ALU.add))
                own(nc.vector.reciprocal(small[:, 1], small[:, 1]))

            def mean(g):
                own(nc.vector.tensor_reduce(small[:, 2], raw_heads(g)[:, :, 0:DH0], AX, ALU.add))
                nc.vector.tensor_scalar(small[:, 2], small[:, 2], 1.0 / DH0, None, ALU.mult).then_inc(mean_done, 1)

            def variance(g):
                dve.wait_ge(sq_done, g + 1)
                own(nc.vector.tensor_reduce(small[:, 3], sq[:], AX, ALU.add))
                own(nc.vector.scalar_tensor_tensor(small[:, 3], small[:, 3], 1.0 / DH0, small[:, 1], ALU.mult, ALU.mult))
                nc.vector.tensor_tensor(small[:, 3], small[:, 3], small[:, 1], ALU.mult).then_inc(var_done, 1)

            def factor(g):
                dve.wait_ge(std_done, g + 1)
                own(nc.vector.reciprocal(small[:, 4], small[:, 4]))
                nc.vector.tensor_tensor(small[:, 5], small[:, 4], small[:, 1], ALU.mult).then_inc(fac_done, 1)

            def body(g, first):
                for n in range(PER):
                    argument(g, n + 2)
                    decayed(g, n + 1, first)
                    if not first:
                        for at, step in ((2, divisor), (3, mean), (10, variance), (13, factor)):
                            if n == at:
                                step(g - 1)

            argument(0, 0)
            argument(0, 1)
            decayed(0, 0, True)
            body(0, True)
            with dve.Fori(1, G) as g:
                own.enter(g - 1, 7)
                body(g, False)
            own.leave(G - 1)
            last = G - 1
            divisor(last)
            mean(last)
            dve.wait_ge(mean_done, G)
            shift(nc.vector, last)
            variance(last)
            factor(last)
            dve.wait_ge(fac_done, G)
            for b in range(GB):
                r = slice(b * H0, (b + 1) * H0)
                ins = nc.vector.tensor_tensor(sq[:, r, :], raw_heads(last)[:, r, 0:DH0],
                                              small[:, 5, r].unsqueeze(2).broadcast_to([P, H0, DH0]), ALU.mult)
            own(ins)
            out = sq[:].rearrange("p (b h) e -> p b (h e)", b=GB)
            own(nc.vector.tensor_tensor(out, out, lnb[:].unsqueeze(1).broadcast_to([P, GB, D]), ALU.mult))
            xg = K.x[:, last * GB:, :]
            own(nc.vector.tensor_tensor(xg, xg, out, ALU.add))

        @block.tensor
        def _(pe):
            pe.wait_ge(masks, 1)
            pe.wait_ge(pick_done, 1)

            def maxima(g, n, first):
                g1, h = after(g, n)
                if not (first and n < 2):
                    pe.wait_ge(arg_done, g * PER + n - 1)
                nc.tensor.matmul(ps[:, n % 2, :], ident_b[:], far[:].rearrange("p b s -> p (b s)"),
                                 start=True, stop=False)
                nc.tensor.matmul(ps[:, n % 2, :], pick[:, h:h + 1].broadcast_to([64, P]), M.g[:, bass.ds(g1 * N, N)],
                                 start=False, stop=True).then_inc(gb, 1)

            def scores(g, n, first):
                g1, h = after(g, n)
                c = h // 4
                if h % 4 == 0:
                    pe.wait_ge(kT_done, (g * C + c + 1) if n < PER else (g * C + C + 1))
                    pe.wait_ge(qz_done, g * PER + n + 4)
                if not (first and n < 4):
                    pe.wait_ge(c_done, g * PER + n - 2)
                for b in range(GB):
                    for j in (h % 4, h % 4 + 1):
                        ins = nc.tensor.matmul(ps[:, 4 + j, b * S:(b + 1) * S], kT[:, c, b * S:(b + 1) * S],
                                               qz[:, c % 2, j, b * S:(b + 1) * S], start=True, stop=True)
                ins.then_inc(qk, 1)

            def outputs(g, n, first):
                if n == 0:
                    pe.wait_ge(ctx1_done, g + 1)
                if n % 2 == 0 and not (first and n < 4):
                    pe.wait_ge(h_done, g * PAIRS + n // 2 - 1)
                pe.wait_ge(c_done, g * PER + n + 1)
                for b in range(GB):
                    at = (b * 2 + n % 2) * (DH0 + 1)
                    ins = nc.tensor.matmul(ps[:, 2 + n // 2 % 2, at:at + DH0 + 1], cmat[:, n % RING, b, :],
                                           ctx1[:, bass.ds(half(g), 1), b, n, :].rearrange("p a e -> p (a e)"),
                                           start=True, stop=True)
                ins.then_inc(pv, 1)

            def body(g, first):
                for n in range(PER):
                    maxima(g, n + 2, first)
                    if n % 2 == 0:
                        scores(g, n + 2, first)
                    outputs(g, n, first)

            maxima(0, 0, True)
            scores(0, 0, True)
            maxima(0, 1, True)
            body(0, True)
            with pe.Fori(1, G) as g:
                body(g, False)


def mlstm(nc, K, ctx_dram, Wi, bi, Wf, bf, ln_scale):
    with Phase(nc, "mlstm") as ph:
        M = Gates()
        M.xcT = ph.sb("xcT", [P, 2, C, T])
        M.xnT, M.ctxT = M.xcT[:, 0], M.xcT[:, 1]
        M.nat = ph.sb("nat", [P, 2, G, GB, H0])
        M.g = ph.sb("g", [64, T], F32R)
        gates(nc, K, M, ctx_dram, Wi, bi, Wf, bf)
        heads(nc, K, M, ctx_dram, ln_scale)


def turn(nc, K, name, lead, trail, ctx_dram=None, rms=None, logits=None, router=None):
    with Phase(nc, name) as ph:
        sb, sem = ph.sb, ph.sem
        norm = ctx_dram is None
        stage = sb("stage", [P, 2, GB, D])
        stats = sb("stats", [P, B, 6])
        mv = sb("mv", [P, B, 2])
        scale = sb("scale", [P, B])
        square = sb("square", [P, B])
        loaded = [sem("loaded0"), sem("loaded1")]
        staged, turned, lead_done, trail_done = sem("staged"), sem("turned"), sem("lead_done"), sem("trail_done")
        stats_done, std_done, ms_done, rms_done = sem("stats_done"), sem("std_done"), sem("ms_done"), sem("rms_done")
        plain_done, logit_mm, logit_done = sem("plain_done"), sem("logit_mm"), sem("logit_done")
        loaded_w, own_dve, held, held_act = sem("loaded_w"), sem("own_dve"), sem("held"), sem("held_act")
        if rms is not None:
            wcol = sb("wcol", [P, C])
            rw = sb("rw", [P, C, E])
            plain = sb("plain", [P, 2, C, N])
        block = ph.block()
        ps = K.ps

        @block.sync
        def _(sp):
            if rms is not None:
                sp.dma_start(wcol[:], rms.rearrange("(c p) -> p c", p=P), allow_slow_non_contiguous=True).then_inc(loaded_w, 16)
                sp.dma_start(rw[:], router.rearrange("(c p) e -> p c e", p=P)).then_inc(loaded_w, 16)
            if not norm:
                for q in range(2):
                    sp.dma_start(stage[:, q], ctx_dram[q * GB:(q + 1) * GB].rearrange("b s d -> s b d")
                                 ).then_inc(loaded[q], 16)
                for q in range(2):
                    sp.wait_ge(turned, (q + 1) * C)
                    sp.dma_start(stage[:, q], ctx_dram[(2 + q) * GB:(3 + q) * GB].rearrange("b s d -> s b d")
                                 ).then_inc(loaded[q], 16)

        @block.vector
        def _(dve):
            for first in (trail_done,):
                dve.sem_inc(first, FIRST)
            own = Own(dve, own_dve)
            if norm:
                with dve.Fori(0, G) as g:
                    for b in range(GB):
                        nc.vector.bn_stats(stats[:, bass.ds(g * GB + b, 1), :].rearrange("p a d -> p (a d)"),
                                           K.x[:, bass.ds(g * GB + b, 1), :].rearrange("p a d -> p (a d)")
                                           ).then_inc(held, 1)
                dve.wait_ge(held, B)
                for b in range(B):
                    ins = nc.vector.bn_aggr(mv[:, b, :], stats[:, b, :])
                ins.then_inc(stats_done, 1)
                dve.wait_ge(std_done, 1)
                own(nc.vector.reciprocal(scale[:], scale[:]))
                if rms is not None:
                    own(nc.vector.tensor_tensor(square[:], mv[:, :, 1], scale[:], ALU.mult))
                    nc.vector.tensor_tensor(square[:], square[:], scale[:], ALU.mult).then_inc(ms_done, 1)
                    dve.wait_ge(rms_done, 1)
                    own(nc.vector.reciprocal(square[:], square[:]))
                    own(nc.vector.tensor_tensor(scale[:], scale[:], square[:], ALU.mult))
            if rms is not None:
                dve.wait_ge(loaded_w, 32)
            with dve.Fori(0, G // 2) as i:
                if norm:
                    for q in range(2):
                        for b in range(GB):
                            g4 = (i * 2 + q) * GB + b
                            ins = nc.vector.tensor_scalar(
                                stage[:, q, b, :], K.x[:, bass.ds(g4, 1), :].rearrange("p a d -> p (a d)"),
                                mv[:, bass.ds(g4, 1), 0:1].rearrange("p a d -> p (a d)"), scale[:, bass.ds(g4, 1)],
                                ALU.subtract, ALU.mult)
                        ins.then_inc(staged, 1)
                for q in range(2):
                    cols = bass.ds((i * 2 + q) * N, N)
                    for c in range(C):
                        dve.wait_ge(lead_done, i * (2 * C) + q * C + c + 1)
                        src = ps[:, c + 4 * q, :] if rms is None else plain[:, q, c, :]
                        nc.vector.tensor_tensor(trail[:, c, cols], src, lead[:, c, cols].bitcast(F32),
                                                ALU.subtract).then_inc(trail_done, 1)

        @block.scalar
        def _(act):
            for first in (logit_done,):
                act.sem_inc(first, FIRST)
            if norm:
                act.wait_ge(stats_done, 1)
                nc.scalar.activation(scale[:], mv[:, :, 1], ACT.Sqrt, bias=K.eps5[:, 0:1]).then_inc(std_done, 1)
            if rms is not None:
                act.wait_ge(ms_done, 1)
                nc.scalar.activation(square[:], square[:], ACT.Sqrt, bias=K.eps6[:, 0:1]).then_inc(rms_done, 1)
                act.wait_ge(loaded_w, 32)
            with act.Fori(0, G // 2) as i:
                for q in range(2):
                    cols = bass.ds((i * 2 + q) * N, N)
                    for c in range(C):
                        act.wait_ge(turned, i * (2 * C) + q * C + c + 1)
                        if rms is None:
                            ph.hold(act, held_act)
                            nc.scalar.activation(lead[:, c, cols], ps[:, c + 4 * q, :], ACT.Copy).then_inc(lead_done, 1)
                        else:
                            act.wait_ge(logit_mm, FIRST + i * 2)
                            act.wait_ge(trail_done, FIRST + i * (2 * C))
                            nc.scalar.activation(plain[:, q, c, :], ps[:, c + 4 * q, :], ACT.Identity,
                                                 scale=wcol[:, c:c + 1]).then_inc(plain_done, 1)
                    if rms is not None:
                        act.wait_ge(logit_mm, FIRST + i * 2 + q + 1)
                        ph.hold(act, held_act)
                        nc.scalar.activation(logits[:, bass.ds((i * 2 + q) * GB, GB), :],
                                             ps[:, 4 * q, 0:GB * E].rearrange("p (b e) -> p b e", b=GB),
                                             ACT.Identity).then_inc(logit_done, 1)

        @block.gpsimd
        def _(pool):
            if rms is not None:
                with pool.Fori(0, G // 2) as i:
                    for q in range(2):
                        cols = bass.ds((i * 2 + q) * N, N)
                        for c in range(C):
                            pool.wait_ge(plain_done, i * (2 * C) + q * C + c + 1)
                            pool.sem_inc(held, 1)
                            nc.gpsimd.tensor_copy(lead[:, c, cols], plain[:, q, c, :]).then_inc(lead_done, 1)

        @block.tensor
        def _(pe):
            for first in (logit_mm,):
                pe.sem_inc(first, FIRST)
            with pe.Fori(0, G // 2) as i:
                pe.wait_ge(trail_done, FIRST + i * (2 * C))
                if rms is not None:
                    pe.wait_ge(logit_done, FIRST + i * 2)
                for q in range(2):
                    if norm:
                        pe.wait_ge(staged, i * 2 + q + 1)
                    else:
                        pe.wait_ge(loaded[q], i * 16 + 16)
                    for c in range(C):
                        for b in range(GB):
                            ins = nc.tensor.transpose(ps[:, c + 4 * q, b * S:(b + 1) * S],
                                                      stage[:, q, b, c * P:(c + 1) * P], K.ident[:])
                        ins.then_inc(turned, 1)
                    if rms is not None:
                        pe.wait_ge(plain_done, i * (2 * C) + (q + 1) * C)
                        pe.wait_ge(loaded_w, 32)
                        for b in range(GB):
                            for c in range(C):
                                ins = nc.tensor.matmul(ps[:, 4 * q, b * E:(b + 1) * E], plain[:, q, c, b * S:(b + 1) * S],
                                                       rw[:, c, :], start=(c == 0), stop=(c == C - 1))
                        ins.then_inc(logit_mm, 1)


def choose(nc, K, logits, wd):
    with Phase(nc, "choose") as ph:
        sb, sem = ph.sb, ph.sem
        top = sb("top", [P, B, 8])
        idx = sb("idx", [P, B, 8], U32)
        pos = sb("pos", [P, B, 2])
        row = sb("row", [P, B])
        part = sb("part", [P, B, E])
        part2 = sb("part2", [P, B, E])
        number = sb("number", [P, B, E])
        own_dve, shifted, exped, numbered = sem("own_dve"), sem("shifted"), sem("exped"), sem("numbered")
        block = ph.block()

        @block.gpsimd
        def _(pool):
            nc.gpsimd.iota(number[:], pattern=[[0, B], [1, E]], base=0, channel_multiplier=0,
                           allow_small_or_imprecise_dtypes=True).then_inc(numbered, 1)

        @block.scalar
        def _(act):
            act.wait_ge(shifted, 1)
            nc.scalar.activation(logits[:], logits[:], ACT.Exp).then_inc(exped, 1)

        @block.vector
        def _(dve):
            own = Own(dve, own_dve)
            wide = lambda v: v.unsqueeze(2).broadcast_to([P, B, E])
            own(nc.vector.tensor_reduce(row[:], logits[:], AX, ALU.max))
            nc.vector.tensor_tensor(logits[:], logits[:], wide(row[:]), ALU.subtract).then_inc(shifted, 1)
            dve.wait_ge(exped, 1)
            own(nc.vector.tensor_reduce(row[:], logits[:], AX, ALU.add))
            own(nc.vector.reciprocal(row[:], row[:]))
            own(nc.vector.tensor_tensor(logits[:], logits[:], wide(row[:]), ALU.mult))
            for b in range(B):
                ins = nc.vector.max(top[:, b, :], logits[:, b, :])
            own(ins)
            for b in range(B):
                ins = nc.vector.max_index(idx[:, b, :], top[:, b, :], logits[:, b, :])
            own(ins)
            own(nc.vector.tensor_copy(pos[:], idx[:, :, 0:2]))
            own(nc.vector.tensor_tensor(row[:], top[:, :, 0], top[:, :, 1], ALU.add))
            own(nc.vector.reciprocal(row[:], row[:]))
            dve.wait_ge(numbered, 1)
            nc.vector.tensor_tensor(part[:], number[:], wide(pos[:, :, 0]), ALU.is_equal)
            own(nc.vector.tensor_tensor(part2[:], number[:], wide(pos[:, :, 1]), ALU.is_equal))
            nc.vector.tensor_tensor(part[:], part[:], wide(top[:, :, 0]), ALU.mult)
            own(nc.vector.tensor_tensor(part2[:], part2[:], wide(top[:, :, 1]), ALU.mult))
            own(nc.vector.tensor_tensor(part[:], part[:], part2[:], ALU.add))
            own(nc.vector.tensor_tensor(wd[:, 0:E, :].rearrange("p e b -> p b e"), part[:], wide(row[:]), ALU.mult))
            own(nc.vector.memset(wd[:, E, :], 1.0))


def experts(nc, K, lead, trail, wd, routed, shared):
    CH = (2 * C * F + FC * D) // 512
    UP, DOWN = C * F, 2 * C * F
    with Phase(nc, "experts") as ph:
        sb, sem = ph.sb, ph.sem
        raw = sb("raw", [P, CH * 512])
        wl = sb("wl", [P, 2, CH * 512], F32R)
        wt = sb("wt", [P, 2, CH * 512], F32R)
        gated = sb("gated", [P, FC, N])
        hid = sb("hid", [P, FC, N])
        hl = sb("hl", [P, 2, FC, N], F32R)
        ht = sb("ht", [P, 2, FC, N], F32R)
        raw_loaded, wl_done, wt_done = sem("raw_loaded"), sem("wl_done"), sem("wt_done")
        gu, silu_done, hid_done, hl_done, ht_done = sem("gu"), sem("silu_done"), sem("hid_done"), sem("hl_done"), sem("ht_done")
        down, acc_done, held = sem("down"), sem("acc_done"), sem("held")
        block = ph.block()
        ps = K.ps

        @block.sync
        def _(sp):
            def load(gate_w, up_w, down_w):
                for w, at, n in ((gate_w, 0, UP), (up_w, UP, UP), (down_w, DOWN, FC * D)):
                    sp.dma_start(raw[:, at:at + n].rearrange("p (c f) -> p c f", f=w.shape[-1]),
                                 w.rearrange("(c p) f -> p c f", p=P)).then_inc(raw_loaded, 16)

            def load_expert(e):
                load(*(w[bass.ds(e, 1)].rearrange("e k f -> (e k) f") for w in routed))

            load_expert(0)
            with sp.Fori(0, E // 2 - 1) as i:
                sp.wait_ge(wt_done, i * (2 * CH) + CH)
                load_expert(i * 2 + 1)
                sp.wait_ge(wt_done, i * (2 * CH) + 2 * CH)
                load_expert(i * 2 + 2)
            sp.wait_ge(wt_done, CH * (E - 1))
            load_expert(E - 1)
            sp.wait_ge(wt_done, CH * E)
            load(*shared)

        def pieces(g):
            return range(2 * (g - 1), 2 * g) if g else ()

        @block.gpsimd
        def _(pool):
            def cut(e, p, k):
                pool.wait_ge(raw_loaded, (e + 1) * 48)
                pool.sem_inc(held, 1)
                nc.gpsimd.tensor_scalar(wl[:, p, k * 512:(k + 1) * 512], raw[:, k * 512:(k + 1) * 512], 1.0, None,
                                        ALU.mult).then_inc(wl_done, 1)

            def unit(i, u, following):
                p, g = divmod(u, G)
                for f in range(FC):
                    pool.wait_ge(hid_done, FIRST + i * 16 + 2 * u + f + 1)
                    pool.wait_ge(down, FIRST + i * 32 + max(4 * (u - 1), 0))
                    pool.sem_inc(held, 1)
                    nc.gpsimd.tensor_scalar(hl[:, u % 2, f, :], hid[:, f, :], 1.0, None, ALU.mult).then_inc(hl_done, 1)
                if following:
                    for k in pieces(g):
                        pool.wait_ge(down, FIRST + i * 32 + 16 * p)
                        cut(i * 2 + p + 1, 1 - p, k)

            for k in range(CH):
                cut(0, 0, k)
            with pool.Fori(0, E // 2) as i:
                for u in range(2 * G):
                    unit(i, u, True)
            for u in range(G):
                unit(E // 2, u, False)

        @block.scalar
        def _(act):
            nc.scalar.activation(K.scrap[:], K.ones[:, 0:1], ACT.Silu)

            def unit(i, u):
                for f in range(FC):
                    act.wait_ge(gu, i * 16 + 2 * u + f + 1)
                    act.wait_ge(hid_done, FIRST + i * 16 + max(2 * u + f - 1, 0))
                    nc.scalar.activation(gated[:, f, :], ps[:, 2 * f, :], ACT.Silu).then_inc(silu_done, 1)

            with act.Fori(0, E // 2) as i:
                for u in range(2 * G):
                    unit(i, u)
            for u in range(G):
                unit(E // 2, u)

        @block.vector
        def _(dve):
            for first in (hid_done, ht_done, acc_done,):
                dve.sem_inc(first, FIRST)
            def cut(e, p, k):
                dve.wait_ge(wl_done, e * CH + k + 1)
                cols = slice(k * 512, (k + 1) * 512)
                nc.vector.tensor_tensor(wt[:, p, cols], raw[:, cols], wl[:, p, cols].bitcast(F32),
                                        ALU.subtract).then_inc(wt_done, 1)

            def add(i, u):
                p, g = divmod(u, G)
                e = i * 2 + p
                for b in range(GB):
                    dve.wait_ge(down, FIRST + i * 32 + 4 * u + b + 1)
                    xb = K.x[:, g * GB + b, :]
                    nc.vector.scalar_tensor_tensor(
                        xb, ps[:, 4 + b, :], wd[:, bass.ds(e, 1), g * GB + b:g * GB + b + 1].rearrange("p a b -> p (a b)"),
                        xb, ALU.mult, ALU.add).then_inc(acc_done, 1)

            def unit(i, u, following):
                p, g = divmod(u, G)
                for f in range(FC):
                    dve.wait_ge(silu_done, i * 16 + 2 * u + f + 1)
                    dve.wait_ge(ht_done, FIRST + i * 16 + 2 * u)
                    nc.vector.tensor_tensor(hid[:, f, :], gated[:, f, :], ps[:, 2 * f + 1, :],
                                            ALU.mult).then_inc(hid_done, 1)
                for f in range(FC):
                    dve.wait_ge(hl_done, i * 16 + 2 * u + f + 1)
                    dve.wait_ge(hid_done, FIRST + i * 16 + 2 * u + f + 1)
                    dve.wait_ge(down, FIRST + i * 32 + max(4 * (u - 1), 0))
                    nc.vector.tensor_tensor(ht[:, u % 2, f, :], hid[:, f, :], hl[:, u % 2, f, :].bitcast(F32),
                                            ALU.subtract).then_inc(ht_done, 1)
                if following:
                    for k in pieces(g):
                        dve.wait_ge(down, FIRST + i * 32 + 16 * p)
                        cut(i * 2 + p + 1, 1 - p, k)
                if u:
                    add(i, u - 1)

            for k in range(CH):
                cut(0, 0, k)
            with dve.Fori(0, E // 2) as i:
                dve.wait_ge(acc_done, FIRST + i * 32)
                for u in range(2 * G):
                    if u == G:
                        dve.wait_ge(acc_done, FIRST + i * 32 + 4 * (G - 1))
                    unit(i, u, True)
                dve.wait_ge(acc_done, FIRST + i * 32 + 28)
                add(i, 2 * G - 1)
            dve.wait_ge(acc_done, FIRST + 16 * E)
            for u in range(G):
                unit(E // 2, u, False)
            add(E // 2, G - 1)

        @block.tensor
        def _(pe):
            for first in (down,):
                pe.sem_inc(first, FIRST)
            def up(i, u):
                p, g = divmod(u, G)
                cols = slice(g * N, (g + 1) * N)
                if g == 0:
                    pe.wait_ge(wt_done, (i * 2 + p + 1) * CH)
                for f in range(FC):
                    pe.wait_ge(hid_done, FIRST + i * 16 + max(2 * u + f - 1, 0))
                    for bank, at in ((2 * f, 0), (2 * f + 1, UP)):
                        for c in range(C):
                            w = slice(at + c * F + f * P, at + c * F + (f + 1) * P)
                            ins = three_passes(nc, ps[:, bank, :], wl[:, p, w], wt[:, p, w], lead[:, c, cols],
                                               trail[:, c, cols], c == 0, c == C - 1)
                    ins.then_inc(gu, 1)

            def down_product(i, u):
                p, g = divmod(u, G)
                pe.wait_ge(ht_done, FIRST + i * 16 + 2 * u + 2)
                for b in range(GB):
                    pe.wait_ge(acc_done, FIRST + i * 32 + max(4 * u - 3 + b, 0))
                    rows = slice(b * S, (b + 1) * S)
                    for f in range(FC):
                        w = slice(DOWN + f * D, DOWN + (f + 1) * D)
                        ins = three_passes(nc, ps[:, 4 + b, :], hl[:, u % 2, f, rows], ht[:, u % 2, f, rows],
                                           wl[:, p, w], wt[:, p, w], f == 0, f == FC - 1)
                    ins.then_inc(down, 1)

            with pe.Fori(0, E // 2) as i:
                for u in range(2 * G):
                    up(i, u)
                    if u:
                        down_product(i, u - 1)
                down_product(i, 2 * G - 1)
            for u in range(G):
                up(E // 2, u)
                if u:
                    down_product(E // 2, u - 1)
            down_product(E // 2, G - 1)


def project(nc, K, name, lead, trail, w_dram, b_dram, out_dram, rstd):
    W2 = 2 * P
    with Phase(nc, name) as ph:
        sb, sem = ph.sb, ph.sem
        raw = sb("raw", [P, C, W2])
        wl = sb("wl", [P, 2, C, W2], F32R)
        wt = sb("wt", [P, 2, C, W2], F32R)
        bias = sb("bias", [P, H1])
        head = sb("head", [P, 2, T])
        sq = sb("sq", [P, 2, N])
        total = sb("total", [P, T])
        raw_loaded, bias_loaded, wl_done, wt_done = sem("raw_loaded"), sem("bias_loaded"), sem("wl_done"), sem("wt_done")
        product, head_done, sq_done, acc_done, held = sem("product"), sem("head_done"), sem("sq_done"), sem("acc_done"), sem("held")
        stored = [sem("stored0"), sem("stored1")]
        sums, std_done, own_dve, blank = sem("sums"), sem("std_done"), sem("own_dve"), sem("blank")
        held_act, held_sp = sem("held_act"), sem("held_sp")
        block = ph.block()
        ps = K.ps
        UN = 4 * G

        @block.sync
        def _(sp):
            def load(pair):
                sp.dma_start(raw[:], w_dram[:, bass.ds(pair * W2, W2)].rearrange("(c p) n -> p c n", p=P)
                             ).then_inc(raw_loaded, 16)

            sp.dma_start(bias[:], b_dram.rearrange("(h p) -> p h", p=P), allow_slow_non_contiguous=True).then_inc(bias_loaded, 16)
            load(0)
            with sp.Fori(0, H1 // 4) as i:
                for p in range(2):
                    sp.wait_ge(wt_done, (i * 2 + p + 1) * 2)
                    ph.hold(sp, held_sp)
                    load(within(nc, (i * 2 + p + 1) & (H1 // 2 - 1), H1 // 2 - 1))
            sp.wait_ge(raw_loaded, 16 * (H1 // 2 + 1))

        def halves(p):
            return (lambda w: w[:, 2 * p:2 * p + 2, :])

        @block.gpsimd
        def _(pool):
            def cut(pair, p):
                pool.wait_ge(raw_loaded, (pair + 1) * 16)
                pool.sem_inc(held, 1)
                for k in range(2):
                    nc.gpsimd.tensor_scalar(halves(k)(wl[:, p]), halves(k)(raw[:]), 1.0, None, ALU.mult
                                            ).then_inc(wl_done, 1)

            nc.gpsimd.memset(total[:], 0.0).then_inc(blank, 1)
            cut(0, 0)
            with pool.Fori(0, H1 // 4) as i:
                for p in range(2):
                    pool.wait_ge(product, FIRST + i * UN + 8 * p)
                    cut(i * 2 + p + 1, 1 - p)

        @block.scalar
        def _(act):
            for first in (sq_done, stored[0], stored[1],):
                act.sem_inc(first, FIRST)
            act.wait_ge(bias_loaded, 16)
            with act.Fori(0, H1 // 4) as i:
                for n in range(UN):
                    hh, g = divmod(n, G)
                    b = bias[:, bass.ds(i * 4 + hh, 1)]
                    if g == 0:
                        act.wait_ge(stored[hh % 2], FIRST + (i * 2 + hh // 2) * 16)
                    act.wait_ge(product, FIRST + i * UN + n + 1)
                    ph.hold(act, held_act)
                    nc.scalar.activation(head[:, hh % 2, g * N:(g + 1) * N], ps[:, n % 8, :], ACT.Identity,
                                         bias=b).then_inc(head_done, 1)
                    act.wait_ge(acc_done, FIRST + i * UN + max(n - 1, 0))
                    ph.hold(act, held_act)
                    nc.scalar.activation(sq[:, n % 2, :], ps[:, n % 8, :], ACT.Square, bias=b).then_inc(sq_done, 1)
                    if g == G - 1:
                        act.wait_ge(head_done, i * UN + n + 1)
                        act.dma_start(out_dram[bass.ds(i * 4 + hh, 1)].rearrange("h p t -> (h p) t"),
                                      head[:, hh % 2, :]).then_inc(stored[hh % 2], 16)
            act.wait_ge(sums, 1)
            nc.scalar.activation(rstd[:], ps[:, 0, 0:B], ACT.Sqrt, scale=1.0 / INNER, bias=K.eps6[:, 0:1]
                                 ).then_inc(std_done, 1)
            for k in range(2):
                act.wait_ge(stored[k], FIRST + 16 * (H1 // 2))

        @block.vector
        def _(dve):
            for first in (acc_done,):
                dve.sem_inc(first, FIRST)
            def cut(pair, p):
                for k in range(2):
                    dve.wait_ge(wl_done, pair * 2 + k + 1)
                    nc.vector.tensor_tensor(halves(k)(wt[:, p]), halves(k)(raw[:]), halves(k)(wl[:, p]).bitcast(F32),
                                            ALU.subtract).then_inc(wt_done, 1)

            cut(0, 0)
            dve.wait_ge(blank, 1)
            with dve.Fori(0, H1 // 4) as i:
                for n in range(UN):
                    g = n % G
                    dve.wait_ge(sq_done, FIRST + i * UN + n + 1)
                    dve.wait_ge(acc_done, FIRST + i * UN + max(n - 3, 0))
                    t = total[:, g * N:(g + 1) * N]
                    nc.vector.tensor_tensor(t, t, sq[:, n % 2, :], ALU.add).then_inc(acc_done, 1)
                    if n % 8 == 1:
                        p = n // 8
                        dve.wait_ge(product, FIRST + i * UN + 8 * p)
                        cut(i * 2 + p + 1, 1 - p)
            dve.wait_ge(std_done, 1)
            Own(dve, own_dve)(nc.vector.reciprocal(rstd[:], rstd[:]))

        @block.tensor
        def _(pe):
            for first in (product,):
                pe.sem_inc(first, FIRST)
            with pe.Fori(0, H1 // 4) as i:
                for n in range(UN):
                    hh, g = divmod(n, G)
                    p = hh // 2
                    if n % 8 == 0:
                        pe.wait_ge(wt_done, (i * 2 + p + 1) * 2)
                    pe.wait_ge(sq_done, FIRST + i * UN + max(n - 7, 0))
                    w = slice((hh % 2) * P, (hh % 2 + 1) * P)
                    cols = slice(g * N, (g + 1) * N)
                    for c in range(C):
                        ins = three_passes(nc, ps[:, n % 8, :], wl[:, p, c, w], wt[:, p, c, w], lead[:, c, cols],
                                           trail[:, c, cols], c == 0, c == C - 1)
                    ins.then_inc(product, 1)
            pe.wait_ge(acc_done, FIRST + H1 * G)
            for b in range(B):
                ins = nc.tensor.matmul(ps[:, 0, b:b + 1], total[:, b * S:(b + 1) * S], K.ones[:, 0:1],
                                       start=True, stop=True)
            ins.then_inc(sums, 1)


def values(nc, K, lead, trail, w_dram, v_dram):
    with Phase(nc, "values") as ph:
        sb, sem = ph.sb, ph.sem
        raw = sb("raw", [P, C, N])
        wl = sb("wl", [P, 2, C, N], F32R)
        wt = sb("wt", [P, 2, C, N], F32R)
        out = sb("out", [P, 2, 4, GB, DH1])
        raw_loaded, wl_done, wt_done, held = sem("raw_loaded"), sem("wl_done"), sem("wt_done"), sem("held")
        product, even_done, odd_done = sem("product"), sem("even_done"), sem("odd_done")
        stored, held_sp = [sem("stored0"), sem("stored1")], sem("held_sp")
        block = ph.block()
        ps = K.ps
        QUADS = H1 // 4

        @block.sync
        def _(sp):
            for first in (stored[0], stored[1],):
                sp.sem_inc(first, FIRST)
            def load(quad):
                sp.dma_start(raw[:], w_dram[:, bass.ds(quad * N, N)].rearrange("(c p) n -> p c n", p=P)
                             ).then_inc(raw_loaded, 16)

            load(0)
            with sp.Fori(0, QUADS // 2) as i:
                for p in range(2):
                    sp.wait_ge(wt_done, (i * 2 + p + 1) * C)
                    ph.hold(sp, held_sp)
                    load(within(nc, (i * 2 + p + 1) & (QUADS - 1), QUADS - 1))
                    for k in range(G):
                        done = (i * 2 + p) * (B // 2) + (k + 1) * 2
                        sp.wait_ge(even_done, FIRST + done)
                        sp.wait_ge(odd_done, FIRST + done)
                        sp.dma_start(v_dram[bass.ds((i * 2 + p) * 4, 4), :, k * GB:(k + 1) * GB, :]
                                     .rearrange("h l b e -> l h (b e)"),
                                     out[:, k % 2].rearrange("p h b e -> p h (b e)")).then_inc(stored[k % 2], 16)
            for k in range(2):
                sp.wait_ge(stored[k], FIRST + 16 * 2 * QUADS)
            sp.wait_ge(raw_loaded, 16 * (QUADS + 1))

        @block.gpsimd
        def _(pool):
            def cut(quad, p):
                pool.wait_ge(raw_loaded, (quad + 1) * 16)
                pool.sem_inc(held, 1)
                for c in range(C):
                    nc.gpsimd.tensor_scalar(wl[:, p, c, :], raw[:, c, :], 1.0, None, ALU.mult).then_inc(wl_done, 1)

            cut(0, 0)
            with pool.Fori(0, QUADS // 2) as i:
                for p in range(2):
                    pool.wait_ge(product, FIRST + i * 2 * B + B * p)
                    cut(i * 2 + p + 1, 1 - p)

        def slot(b):
            return (lambda out: out[:, (b // GB) % 2, :, b % GB, :])

        @block.scalar
        def _(act):
            for first in (even_done,):
                act.sem_inc(first, FIRST)
            with act.Fori(0, QUADS // 2) as i:
                for n in range(2 * B):
                    p, b = divmod(n, B)
                    if b % 2 == 0:
                        if b % GB == 0:
                            act.wait_ge(stored[(b // GB) % 2], FIRST + ((i * 2 + p) * 2 + b // (2 * GB)) * 16)
                        act.wait_ge(product, FIRST + i * 2 * B + n + 1)
                        nc.scalar.activation(slot(b)(out), ps[:, n % 8, :].rearrange("p (h e) -> p h e", h=4),
                                             ACT.Copy).then_inc(even_done, 1)

        @block.vector
        def _(dve):
            for first in (odd_done,):
                dve.sem_inc(first, FIRST)
            def cut(quad, p, c):
                dve.wait_ge(wl_done, quad * C + c + 1)
                nc.vector.tensor_tensor(wt[:, p, c, :], raw[:, c, :], wl[:, p, c, :].bitcast(F32),
                                        ALU.subtract).then_inc(wt_done, 1)

            for c in range(C):
                cut(0, 0, c)
            with dve.Fori(0, QUADS // 2) as i:
                for n in range(2 * B):
                    p, b = divmod(n, B)
                    if b % 2 == 1:
                        if b % GB == 1:
                            dve.wait_ge(stored[(b // GB) % 2], FIRST + ((i * 2 + p) * 2 + b // (2 * GB)) * 16)
                        dve.wait_ge(product, FIRST + i * 2 * B + n + 1)
                        nc.vector.tensor_copy(slot(b)(out), ps[:, n % 8, :].rearrange("p (h e) -> p h e", h=4)
                                              ).then_inc(odd_done, 1)
                        if b in (3, 5, 7, 9):
                            cut(i * 2 + p + 1, 1 - p, (b - 3) // 2)

        @block.tensor
        def _(pe):
            for first in (product,):
                pe.sem_inc(first, FIRST)
            with pe.Fori(0, QUADS // 2) as i:
                for n in range(2 * B):
                    p, b = divmod(n, B)
                    if b == 0:
                        pe.wait_ge(wt_done, (i * 2 + p + 1) * C)
                    pe.wait_ge(odd_done if b % 2 else even_done, FIRST + i * B + max((n - 8) // 2 + 1, 0))
                    rows = slice(b * S, (b + 1) * S)
                    for c in range(C):
                        ins = three_passes(nc, ps[:, n % 8, :], lead[:, c, rows], trail[:, c, rows], wl[:, p, c, :],
                                           wt[:, p, c, :], c == 0, c == C - 1)
                    ins.then_inc(product, 1)


def attend(nc, K, q_dram, k_dram, v_dram, o_w, o_b, v_b, nq, nk, rq, rk):
    QUADS = H1 // 4
    IT = G * QUADS
    with Phase(nc, "attend") as ph:
        sb, sem = ph.sb, ph.sem
        wol = sb("wol", [P, H1, D], F32R)
        wot = sb("wot", [P, H1, D], F32R)
        q = sb("q", [P, 4, N])
        k = sb("k", [P, 4, N])
        v = sb("v", [P, 4, GB, DH1])
        kcol = sb("kcol", [P, H1])
        qcol = sb("qcol", [P, H1])
        vbias = sb("vbias", [P, H1])
        obias = sb("obias", [P, D])
        rkb = sb("rkb", [P, T])
        kn = sb("kn", [P, 2, N])
        prob = sb("prob", [P, 2, GB, S])
        probT = sb("probT", [P, 2, N])
        ol = sb("ol", [P, 2, 4, N], F32R)
        ot = sb("ot", [P, 2, 4, N], F32R)
        row = sb("row", [P, 2, 4, GB])
        raw = q
        qk_ring = [sem(f"qk_ring{j}") for j in range(4)]
        v_ring = [sem(f"v_ring{j}") for j in range(4)]
        cols_loaded, raw_loaded, wol_done, wot_done = sem("cols_loaded"), sem("raw_loaded"), sem("wol_done"), sem("wot_done")
        bias_done, spread, rkb_done, col_done = sem("bias_done"), sem("spread"), sem("rkb_done"), sem("col_done")
        kn_done, scores, max_done, exp_done, sum_done, prob_done = (
            sem("kn_done"), sem("scores"), sem("max_done"), sem("exp_done"), sem("sum_done"), sem("prob_done"))
        prob_T, probT_done, mixed, ol_done, ot_done, final, acc_done = (
            sem("prob_T"), sem("probT_done"), sem("mixed"), sem("ol_done"), sem("ot_done"), sem("final"), sem("acc_done"))
        own_dve, row_done, held_sp, held_act = sem("own_dve"), sem("row_done"), sem("held_sp"), sem("held_act")

        def group(it):
            return it >> 2 if isinstance(it, int) else within(nc, it >> 2, G - 1)

        def quad_of(it):
            return it & 3 if isinstance(it, int) else within(nc, it & 3, QUADS - 1)

        def blocks(eng, body):
            body(0, 0, True, False)
            body(1, 1, False, False)
            with eng.Fori(1, IT // 2 - 1) as i:
                body(i * 2, 0, False, False)
                body(i * 2 + 1, 1, False, False)
            body(IT - 2, 0, False, False)
            body(IT - 1, 1, False, True)

        block = ph.block()
        ps = K.ps

        @block.sync
        def _(sp):
            for t, d in ((kcol, nk), (qcol, nq), (vbias, v_b)):
                sp.dma_start(t[:], d.rearrange("(h p) -> p h", p=P), allow_slow_non_contiguous=True).then_inc(cols_loaded, 16)
            sp.dma_start(obias[:], o_b.partition_broadcast(P)).then_inc(cols_loaded, 16)
            with sp.Fori(0, QUADS) as i:
                sp.wait_ge(wot_done, FIRST + i * 4)
                sp.dma_start(raw[:], o_w[bass.ds(i * 4 * P, 4 * P), :].rearrange("(h p) d -> p h d", p=P)
                             ).then_inc(raw_loaded, 16)
            sp.wait_ge(wot_done, FIRST + H1)

            def load_qk(it, j):
                g, h = group(it), quad_of(it) * 4 + j
                cols = bass.ds(g * N, N)
                sp.dma_start(q[:, j, :], q_dram[bass.ds(h, 1), :, cols].rearrange("h p t -> (h p) t")).then_inc(qk_ring[j], 16)
                sp.dma_start(k[:, j, :], k_dram[bass.ds(h, 1), :, cols].rearrange("h p t -> (h p) t")).then_inc(qk_ring[j], 16)

            def load_v(it, j):
                g, h = group(it), quad_of(it) * 4 + j
                sp.dma_start(v[:, j].rearrange("p b e -> p (b e)"),
                             v_dram[bass.ds(h, 1), :, bass.ds(g * GB, GB), :].rearrange("h l b e -> (h l) (b e)")
                             ).then_inc(v_ring[j], 16)

            for j in range(4):
                load_qk(0, j)
                load_v(0, j)
            with sp.Fori(1, IT) as it:
                for what, j in (("qk", 0), ("qk", 1), ("qk", 2), ("v", 0), ("qk", 3), ("v", 1), ("v", 2), ("v", 3)):
                    if what == "qk":
                        sp.wait_ge(scores, (it - 1) * 4 + j + 1)
                        ph.hold(sp, held_sp)
                        load_qk(it, j)
                    else:
                        sp.wait_ge(mixed, (it - 1) * 4 + j + 1)
                        ph.hold(sp, held_sp)
                        load_v(it, j)

        @block.gpsimd
        def _(pool):
            pool.wait_ge(cols_loaded, 64)
            with pool.Fori(0, G) as g:
                xg = K.x[:, bass.ds(g * GB, GB), :]
                nc.gpsimd.tensor_tensor(xg, xg, obias[:].unsqueeze(1).broadcast_to([P, GB, D]), ALU.add
                                        ).then_inc(bias_done, 1)

        @block.scalar
        def _(act):
            for first in (exp_done, probT_done,):
                act.sem_inc(first, FIRST)
            with act.Fori(0, QUADS) as i:
                act.wait_ge(raw_loaded, (i + 1) * 16)
                ph.hold(act, held_act)
                for j in range(4):
                    nc.scalar.activation(wol[:, bass.ds(i * 4 + j, 1), :].rearrange("p a d -> p (a d)"), raw[:, j, :],
                                         ACT.Copy).then_inc(wol_done, 1)
            act.wait_ge(cols_loaded, 64)
            for g in range(G):
                act.wait_ge(spread, g + 1)
                nc.scalar.activation(rkb[:, g * N:(g + 1) * N], ps[:, g, :], ACT.Copy).then_inc(rkb_done, 1)
            nc.scalar.activation(K.scrap[:], K.ones[:, 0:1], ACT.Exp)

            def softmax(it, j):
                n, g = it * 4 + j, group(it)
                act.wait_ge(max_done, n + 1)
                ph.hold(act, held_act)
                for b in range(GB):
                    ins = nc.scalar.activation(prob[:, j % 2, b, :], ps[:, j % 2, b * S:(b + 1) * S], ACT.Exp,
                                               bias=row[:, j % 2, 1, b:b + 1], scale=rq[:, bass.ds(g * GB + b, 1)],
                                               accum_out=row[:, j % 2, 2, b:b + 1])
                ins.then_inc(exp_done, 1)

            def turned(it, j):
                act.wait_ge(prob_T, it * 4 + j + 1)
                nc.scalar.activation(probT[:, j % 2, :], ps[:, 2 + j % 2, :], ACT.Copy).then_inc(probT_done, 1)

            def head(it, par, j):
                act.wait_ge(mixed, it * 4 + j + 1)
                ph.hold(act, held_act)
                nc.scalar.activation(ol[:, par, j, :], ps[:, 4 + j % 2, :], ACT.Identity,
                                     bias=vbias[:, bass.ds(quad_of(it) * 4 + j, 1)]).then_inc(ol_done, 1)

            def body(it, par, first, last):
                for j in range(4):
                    if j == 0 and not first:
                        head(it - 1, 1 - par, 2)
                        head(it - 1, 1 - par, 3)
                    if j >= 2:
                        head(it, par, j - 2)
                    if j < 3:
                        softmax(it, j + 1)
                    elif not last:
                        softmax(it + 1, 0)
                    turned(it, j)

            softmax(0, 0)
            blocks(act, body)
            head(IT - 1, 1, 2)
            head(IT - 1, 1, 3)

        @block.vector
        def _(dve):
            for first in (wot_done, acc_done, ot_done,):
                dve.sem_inc(first, FIRST)
            own = Own(dve, own_dve)
            with dve.Fori(0, QUADS) as i:
                for j in range(4):
                    dve.wait_ge(wol_done, i * 4 + j + 1)
                    at = bass.ds(i * 4 + j, 1)
                    nc.vector.tensor_tensor(wot[:, at, :].rearrange("p a d -> p (a d)"), raw[:, j, :],
                                            wol[:, at, :].rearrange("p a d -> p (a d)").bitcast(F32),
                                            ALU.subtract).then_inc(wot_done, 1)
            dve.wait_ge(cols_loaded, 64)
            own(nc.vector.scalar_tensor_tensor(kcol[:], kcol[:], DH1 ** -0.5, qcol[:], ALU.mult, ALU.mult))
            dve.wait_ge(rkb_done, G)
            dve.wait_ge(bias_done, G)

            def keys(it, j):
                dve.wait_ge(qk_ring[j], (it + 1) * 32)
                nc.vector.scalar_tensor_tensor(kn[:, j % 2, :], k[:, j, :], kcol[:, bass.ds(quad_of(it) * 4 + j, 1)],
                                               rkb[:, bass.ds(group(it) * N, N)], ALU.mult, ALU.mult).then_inc(kn_done, 1)

            def peak(it, j):
                n = it * 4 + j
                dve.wait_ge(scores, n + 1)
                r = row[:, j % 2]
                nc.vector.tensor_reduce(r[:, 0], ps[:, j % 2, :].rearrange("p (b s) -> p b s", b=GB), AX, ALU.max
                                        ).then_inc(row_done, 1)
                dve.wait_ge(row_done, n + 1)
                nc.vector.scalar_tensor_tensor(r[:, 1], r[:, 0], -1.0, rq[:, bass.ds(group(it) * GB, GB)], ALU.mult,
                                               ALU.mult).then_inc(max_done, 1)

            def divide(it, j):
                n = it * 4 + j
                dve.wait_ge(exp_done, FIRST + n + 1)
                r = row[:, j % 2]
                nc.vector.reciprocal(r[:, 3], r[:, 2]).then_inc(sum_done, 1)
                dve.wait_ge(sum_done, n + 1)
                nc.vector.tensor_tensor(prob[:, j % 2], prob[:, j % 2], r[:, 3].unsqueeze(2).broadcast_to([P, GB, S]),
                                        ALU.mult).then_inc(prob_done, 1)

            def rest(it, par, j):
                dve.wait_ge(ol_done, it * 4 + j + 1)
                nc.vector.scalar_tensor_tensor(ot[:, par, j, :], ps[:, 4 + j % 2, :], vbias[:, bass.ds(quad_of(it) * 4 + j, 1)],
                                               ol[:, par, j, :].bitcast(F32), ALU.add, ALU.subtract).then_inc(ot_done, 1)

            def add(it, b):
                dve.wait_ge(final, FIRST + it * GB + b + 1)
                dve.wait_ge(acc_done, FIRST + it * GB + b)
                xb = K.x[:, bass.ds(group(it) * GB + b, 1), :].rearrange("p a d -> p (a d)")
                nc.vector.tensor_tensor(xb, xb, ps[:, 6 + b % 2, :], ALU.add).then_inc(acc_done, 1)

            def body(it, par, first, last):
                for j in range(4):
                    if j == 0 and not first:
                        rest(it - 1, 1 - par, 2)
                        rest(it - 1, 1 - par, 3)
                    if j >= 2:
                        rest(it, par, j - 2)
                    if j < 3:
                        peak(it, j + 1)
                    elif not last:
                        peak(it + 1, 0)
                    if j < 2:
                        keys(it, j + 2)
                    elif not last:
                        keys(it + 1, j - 2)
                    if not first:
                        if j:
                            add(it - 1, j - 1)
                    if j < 3:
                        divide(it, j + 1)
                    elif not last:
                        divide(it + 1, 0)
                    if j == 3 and not first:
                        add(it - 1, 3)

            keys(0, 0)
            keys(0, 1)
            peak(0, 0)
            divide(0, 0)
            blocks(dve, body)
            rest(IT - 1, 1, 2)
            rest(IT - 1, 1, 3)
            for b in range(GB):
                add(IT - 1, b)

        @block.tensor
        def _(pe):
            for first in (final,):
                pe.sem_inc(first, FIRST)
            for g in range(G):
                for b in range(GB):
                    ins = nc.tensor.matmul(ps[:, g, b * S:(b + 1) * S],
                                           rk[:, g * GB + b:g * GB + b + 1].broadcast_to([P, P]), K.ident[:],
                                           start=True, stop=True)
                ins.then_inc(spread, 1)
            pe.wait_ge(rkb_done, G)
            pe.wait_ge(wot_done, FIRST + H1)

            def n_before(it, j):
                return not isinstance(it, int) or it * 4 + j >= 2

            def score(it, j):
                pe.wait_ge(kn_done, it * 4 + j + 1)
                if n_before(it, j):
                    pe.wait_ge(exp_done, FIRST + it * 4 + j - 1)
                for b in range(GB):
                    s = slice(b * S, (b + 1) * S)
                    ins = nc.tensor.matmul(ps[:, j % 2, s], q[:, j, s], kn[:, j % 2, s], start=True, stop=True)
                ins.then_inc(scores, 1)

            def turn_prob(it, j):
                pe.wait_ge(prob_done, it * 4 + j + 1)
                if n_before(it, j):
                    pe.wait_ge(probT_done, FIRST + it * 4 + j - 1)
                for b in range(GB):
                    ins = nc.tensor.transpose(ps[:, 2 + j % 2, b * S:(b + 1) * S], prob[:, j % 2, b, :], K.ident[:])
                ins.then_inc(prob_T, 1)

            def mix(it, j):
                pe.wait_ge(probT_done, FIRST + it * 4 + j + 1)
                pe.wait_ge(v_ring[j], (it + 1) * 16)
                if n_before(it, j):
                    pe.wait_ge(ot_done, FIRST + it * 4 + j - 1)
                for b in range(GB):
                    s = slice(b * S, (b + 1) * S)
                    ins = nc.tensor.matmul(ps[:, 4 + j % 2, s], v[:, j, b, :], probT[:, j % 2, s], start=True, stop=True)
                ins.then_inc(mixed, 1)

            def output(it, par, b):
                if b == 0:
                    pe.wait_ge(ot_done, FIRST + it * 4 + 4)
                if not isinstance(it, int) or it * GB + b >= 2:
                    pe.wait_ge(acc_done, FIRST + it * GB + b - 1)
                rows = slice(b * S, (b + 1) * S)
                for j in range(4):
                    w = bass.ds(quad_of(it) * 4 + j, 1)
                    ins = three_passes(nc, ps[:, 6 + b % 2, :], ol[:, par, j, rows], ot[:, par, j, rows],
                                       wol[:, w, :].rearrange("p a d -> p (a d)"),
                                       wot[:, w, :].rearrange("p a d -> p (a d)"), j == 0, j == 3)
                ins.then_inc(final, 1)

            def body(it, par, first, last):
                for j in range(4):
                    if j < 3:
                        score(it, j + 1)
                    elif not last:
                        score(it + 1, 0)
                    turn_prob(it, j)
                    if not first:
                        output(it - 1, 1 - par, j)
                    if j:
                        mix(it, j - 1)
                mix(it, 3)

            score(0, 0)
            blocks(pe, body)
            for b in range(GB):
                output(IT - 1, 1, b)


def ternary(nc, K, lead, trail, w_dram, b_dram, out):
    with Phase(nc, "ternary") as ph:
        sb, sem = ph.sb, ph.sem
        w = sb("w", [P, C, D])
        size = sb("size", [P, C, D])
        low = sb("low", [P, C, D])
        tern = sb("tern", [P, C, D])
        ternT = sb("ternT", [P, C, D], F32R)
        bias = sb("bias", [P, D])
        rows = sb("rows", [P, 1])
        scale = sb("scale", [P, 1])
        edge = sb("edge", [P, 2])
        loaded, abs_done, sums, own_dve, tern_done, turned, copied = (
            sem("loaded"), sem("abs_done"), sem("sums"), sem("own_dve"), sem("tern_done"), sem("turned"), sem("copied"))
        bias_done, product, y_done, stored = sem("bias_done"), sem("product"), sem("y_done"), sem("stored")
        block = ph.block()
        ps = K.ps

        @block.sync
        def _(sp):
            sp.dma_start(w[:], w_dram.rearrange("(c p) i -> p c i", p=P)).then_inc(loaded, 16)
            sp.dma_start(bias[:], b_dram.partition_broadcast(P)).then_inc(loaded, 16)
            with sp.Fori(0, G) as g:
                sp.wait_ge(y_done, (g + 1) * GB)
                at = bass.ds(g * GB, GB)
                sp.dma_start(out[at].rearrange("b s d -> s b d"), K.x[:, at, :]).then_inc(stored, 16)
            sp.wait_ge(stored, 16 * G)

        @block.gpsimd
        def _(pool):
            pool.wait_ge(loaded, 32)
            with pool.Fori(0, G) as g:
                xg = K.x[:, bass.ds(g * GB, GB), :]
                nc.gpsimd.tensor_tensor(xg, xg, bias[:].unsqueeze(1).broadcast_to([P, GB, D]), ALU.add
                                        ).then_inc(bias_done, 1)

        @block.scalar
        def _(act):
            act.wait_ge(loaded, 32)
            nc.scalar.activation(size[:], w[:], ACT.Abs, accum_out=rows[:]).then_inc(abs_done, 1)
            for c in range(C):
                act.wait_ge(turned, c + 1)
                nc.scalar.activation(ternT[:, c, :], ps[:, c, :], ACT.Copy).then_inc(copied, 1)

        @block.vector
        def _(dve):
            own = Own(dve, own_dve)
            dve.wait_ge(sums, 1)
            own(nc.vector.tensor_scalar(scale[:], ps[:, 4, 0:1], 1.0 / (D * D), None, ALU.mult))
            nc.vector.tensor_scalar(edge[:, 0:1], scale[:], 1e-10, 0.5, ALU.add, ALU.mult)
            own(nc.vector.tensor_scalar(edge[:, 1:2], scale[:], 1e-10, -0.5, ALU.add, ALU.mult))
            flat = lambda t: t[:].rearrange("p c d -> p (c d)")
            own(nc.vector.tensor_scalar(flat(low), flat(w), edge[:, 1:2], None, ALU.is_lt))
            nc.vector.scalar_tensor_tensor(flat(tern), flat(w), edge[:, 0:1], flat(low), ALU.is_gt, ALU.subtract
                                           ).then_inc(tern_done, 1)
            with dve.Fori(0, G) as g:
                dve.wait_ge(bias_done, g + 1)
                for b in range(GB):
                    dve.wait_ge(product, g * GB + b + 1)
                    xb = K.x[:, bass.ds(g * GB + b, 1), :].rearrange("p a d -> p (a d)")
                    nc.vector.scalar_tensor_tensor(xb, ps[:, b, :], scale[:, 0:1], xb, ALU.mult, ALU.add
                                                   ).then_inc(y_done, 1)

        @block.tensor
        def _(pe):
            pe.wait_ge(abs_done, 1)
            nc.tensor.matmul(ps[:, 4, 0:1], K.ones[:], rows[:], start=True, stop=True).then_inc(sums, 1)
            pe.wait_ge(tern_done, 1)
            for c in range(C):
                for o in range(C):
                    ins = nc.tensor.transpose(ps[:, c, o * P:(o + 1) * P], tern[:, o, c * P:(c + 1) * P], K.ident[:])
                ins.then_inc(turned, 1)
            pe.wait_ge(copied, C)
            for b in range(B):
                if b >= GB:
                    pe.wait_ge(y_done, b - GB + 1)
                r = slice(b * S, (b + 1) * S)
                for c in range(C):
                    nc.tensor.matmul(ps[:, b % GB, :], lead[:, c, r], ternT[:, c, :], start=(c == 0), stop=False)
                    ins = nc.tensor.matmul(ps[:, b % GB, :], trail[:, c, r], ternT[:, c, :], start=False,
                                           stop=(c == C - 1))
                ins.then_inc(product, 1)


class Kept:
    pass


def operands(ph):
    return ph.sb("lead", [P, C, T], F32R), ph.sb("trail", [P, C, T], F32R)


def two_layers(nc, a, out):
    q_dram = nc.dram_tensor("q_heads", [H1, P, T], F32).ap()
    k_dram = nc.dram_tensor("k_heads", [H1, P, T], F32).ap()
    v_dram = nc.dram_tensor("v_heads", [H1, S, B, DH1], F32).ap()
    with ExitStack() as stack:
        kept = lambda name, shape: stack.enter_context(nc.sbuf_tensor(name, shape, F32))
        K = Kept()
        K.x = kept("x_kept", [P, B, D])
        K.ident, K.ones = kept("ident", [P, P]), kept("ones", [P, P])
        K.eps5, K.eps6 = kept("eps5", [P, 1]), kept("eps6", [P, 1])
        K.scrap = kept("scrap", [P, 1])
        rq, rk = kept("rq", [P, B]), kept("rk", [P, B])
        K.ps = stack.enter_context(nc.psum_tensor("banks", [P, 8, 512], F32))
        setup(nc, K, a["x"])
        with Phase(nc, "of_ctx") as ph:
            lead, trail = operands(ph)
            turn(nc, K, "turn_ctx", lead, trail, ctx_dram=a["ctx_2048"])
            project(nc, K, "keys", lead, trail, a["L1_xattn_ki_w"], a["L1_xattn_ki_b"], k_dram, rk)
            values(nc, K, lead, trail, a["L1_xattn_vi_w"], v_dram)
        mlstm(nc, K, a["ctx_2048"], a["L0_xattn_Wi"], a["L0_xattn_bi"], a["L0_xattn_Wf"], a["L0_xattn_bf"],
              a["L0_xattn_ln_scale"])
        with Phase(nc, "of_x1") as ph:
            lead, trail = operands(ph)
            logits, wd = ph.sb("logits", [P, B, E]), ph.sb("wd", [P, E + 1, B])
            turn(nc, K, "turn_x1", lead, trail, rms=a["L0_ffn_rms_weight"], logits=logits,
                 router=a["L0_ffn_router_w"])
            choose(nc, K, logits, wd)
            experts(nc, K, lead, trail, wd, [a[f"L0_ffn_w_{n}"] for n in ("gate", "up", "down")],
                    [a[f"L0_ffn_sw_{n}"] for n in ("gate", "up", "down")])
        with Phase(nc, "of_x2") as ph:
            lead, trail = operands(ph)
            turn(nc, K, "turn_x2", lead, trail)
            project(nc, K, "queries", lead, trail, a["L1_xattn_q_w"], a["L1_xattn_q_b"], q_dram, rq)
        attend(nc, K, q_dram, k_dram, v_dram, a["L1_xattn_o_w"], a["L1_xattn_o_b"], a["L1_xattn_vi_b"],
               a["L1_xattn_nq_s"], a["L1_xattn_nki_s"], rq, rk)
        with Phase(nc, "of_x3") as ph:
            lead, trail = operands(ph)
            turn(nc, K, "turn_x3", lead, trail)
            ternary(nc, K, lead, trail, a["L1_ffn_weight"], a["L1_ffn_bias"], out)


_INS = ['x', 'ctx_2048', 'L0_xattn_Wi', 'L0_xattn_bi', 'L0_xattn_Wf', 'L0_xattn_bf', 'L0_xattn_ln_scale',
        'L0_ffn_rms_weight', 'L0_ffn_router_w', 'L0_ffn_w_gate', 'L0_ffn_w_up', 'L0_ffn_w_down',
        'L0_ffn_sw_gate', 'L0_ffn_sw_up', 'L0_ffn_sw_down', 'L1_xattn_q_w', 'L1_xattn_q_b',
        'L1_xattn_ki_w', 'L1_xattn_ki_b', 'L1_xattn_vi_w', 'L1_xattn_vi_b', 'L1_xattn_o_w', 'L1_xattn_o_b',
        'L1_xattn_nq_s', 'L1_xattn_nki_s', 'L1_ffn_weight', 'L1_ffn_bias']


def kernel(**inputs):
    import concourse.bacc as bacc
    from concourse.bass_utils import run_bass_kernel_spmd

    nc = bacc.Bacc("TRN2", target_bir_lowering=False, num_devices=1)
    arrays, args = {}, {}
    for name in _INS:
        v = np.ascontiguousarray(inputs[name])
        arrays[f"in_{name}"] = v
        args[name] = nc.dram_tensor(f"in_{name}", v.shape, mybir.dt.from_np(v.dtype), kind="ExternalInput").ap()
    out = nc.dram_tensor("out", (B, S, D), F32, kind="ExternalOutput").ap()
    two_layers(nc, args, out)
    return run_bass_kernel_spmd(nc, [arrays], core_ids=[0]).results[0]["out"]
```

```python
from contextlib import ExitStack

import numpy as np

import concourse.bass as bass
from concourse import mybir

F32 = mybir.dt.float32
F32R = mybir.dt.float32r
BF16 = mybir.dt.bfloat16
U32 = mybir.dt.uint32
ALU = mybir.AluOpType
ACT = mybir.ActivationFunctionType
AX = mybir.AxisListType.X

P = 128
B, S, D = 16, 128, 512
T = B * S
C = D // P
GB = 4
G = B // GB
N = GB * S
H0, DH0 = 16, 32
E, F = 8, 256
FC = F // P
TILES = 2 * T // P + E - 1
H1, DH1 = 16, 128
INNER = H1 * DH1
FAR = 1e30
FIRST = 1


class Own:

    def __init__(self, eng, sem):
        self.eng, self.sem, self.base, self.done, self.i, self.per = eng, sem, 0, 0, 0, 0

    def enter(self, i, per):
        self.base, self.done, self.i, self.per = self.base + self.done, 0, i, per

    def leave(self, trips):
        assert self.done == self.per, (self.done, self.per)
        self.base, self.done, self.i, self.per = self.base + trips * self.per, 0, 0, 0

    def __call__(self, ins):
        ins.then_inc(self.sem, 1)
        self.done += 1
        self.eng.wait_ge(self.sem, self.i * self.per + (self.base + self.done))


class Phase:

    def __init__(self, nc, name):
        self.nc, self.name, self.stack, self.sems = nc, name, ExitStack(), []

    def __enter__(self):
        self.stack.__enter__()
        return self

    def __exit__(self, *a):
        self.stack.__exit__(*a)
        if self.sems:
            self.nc.clear_and_free_semaphores(self.sems)
            self.nc.all_engine_barrier()

    def sb(self, name, shape, dt=F32):
        return self.stack.enter_context(self.nc.sbuf_tensor(f"{self.name}_{name}", shape, dt))

    def sem(self, name):
        self.sems.append(self.nc.alloc_semaphore(name=f"{self.name}_{name}"))
        return self.sems[-1]

    def hold(self, eng, sem):
        eng.sem_inc(sem, 1)

    def block(self):
        return self.stack.enter_context(self.nc.Block())


def within(nc, v, hi):
    return nc.s_assert_within(v, 0, hi, skip_runtime_bounds_check_because="the loop's count bounds it")


def three_passes(nc, out, lead_l, trail_l, lead_r, trail_r, first, last):
    nc.tensor.matmul(out, lead_l, lead_r, start=first, stop=False)
    nc.tensor.matmul(out, lead_l, trail_r, start=False, stop=False)
    return nc.tensor.matmul(out, trail_l, lead_r, start=False, stop=last)


class RowStats:

    def __init__(self, nc, K, ph):
        self.nc, self.K = nc, K
        self.summed, self.aggregated, self.rooted, self.inverted = (
            ph.sem("summed"), ph.sem("aggregated"), ph.sem("rooted"), ph.sem("inverted"))

    def batch(self, b):
        b = bass.ds(b, 1)
        self.nc.vector.bn_stats(self.K.stats[:, b, :].rearrange("p a d -> p (a d)"),
                                self.K.x[:, b, :].rearrange("p a d -> p (a d)")).then_inc(self.summed, 1)

    def deviations(self, dve):
        dve.wait_ge(self.summed, B)
        for b in range(B):
            ins = self.nc.vector.bn_aggr(self.K.mv[:, b, :], self.K.stats[:, b, :])
        ins.then_inc(self.aggregated, 1)
        dve.wait_ge(self.rooted, 1)
        self.nc.vector.reciprocal(self.K.rstd[:], self.K.rstd[:]).then_inc(self.inverted, 1)
        dve.wait_ge(self.inverted, 1)

    def root(self, act):
        act.wait_ge(self.aggregated, 1)
        self.nc.scalar.activation(self.K.rstd[:], self.K.mv[:, :, 1], ACT.Sqrt, bias=self.K.eps5[:, 0:1]
                                  ).then_inc(self.rooted, 1)


def setup(nc, K):
    with Phase(nc, "setup") as ph:
        blank, made = ph.sem("blank"), ph.sem("made")
        block = ph.block()

        @block.gpsimd
        def _(pool):
            nc.gpsimd.memset(K.ident[:], 0.0).then_inc(blank, 1)
            nc.gpsimd.memset(K.eps5[:], 1e-5)
            nc.gpsimd.memset(K.eps6[:], 1e-6)
            nc.gpsimd.memset(K.ones[:], 1.0).then_inc(blank, 1)
            pool.wait_ge(blank, 2)
            nc.gpsimd.affine_select(out=K.ident[:], in_=K.ident[:], compare_op=ALU.not_equal, fill=1.0,
                                    base=0, pattern=[[-1, P]], channel_multiplier=1).then_inc(made, 1)
            pool.wait_ge(made, 1)


class Gates:
    pass


def gates(nc, K, M, ctx_dram, Wi, bi, Wf, bf):
    with Phase(nc, "gates") as ph:
        sb, sem = ph.sb, ph.sem
        ctx = sb("ctx", [P, GB, D])
        xn = sb("xn", [P, GB, D])
        w_gate = sb("w_gate", [P, 3, C, 64])
        w_ctx = sb("w_ctx", [P, C, 64])
        bias = sb("bias", [64, 1])
        keep = sb("keep", [32, GB, S])
        pen = sb("pen", [32, GB, S])
        f_abs = sb("f_abs", [64, N])
        f_min = sb("f_min", [64, N])
        irow = sb("irow", [32, N])
        logf = sb("logf", [32, N])
        cumf = sb("cumf", [32, N])
        arow = sb("arow", [32, T])
        grow = sb("grow", [32, T])
        mrow = sb("mrow", [32, T])

        loaded_w, loaded_ctx = sem("loaded_w"), sem("loaded_ctx")
        masks, own_dve, own_act, own_pool = sem("masks"), sem("own_dve"), sem("own_act"), sem("own_pool")
        wsum, xn_done = sem("wsum"), sem("xn_done")
        turned, xT_done, cT_done = sem("turned"), sem("xT_done"), sem("cT_done")
        gates_done, sp_done, fmin_done = sem("gates_done"), sem("sp_done"), sem("fmin_done")
        m_done, em_done, nat_T, nat_done = sem("m_done"), sem("em_done"), sem("nat_T"), sem("nat_done")
        logf_done = sem("logf_done")
        g_lead, g_trail = sem("g_lead"), sem("g_trail")
        held_act = sem("held_act")
        block = ph.block()
        ps = K.ps

        @block.sync
        def _(sp):
            sp.dma_start(ctx[:], ctx_dram[0:GB].rearrange("b s d -> s b d")).then_inc(loaded_ctx, 16)
            sp.wait_ge(masks, 1)
            for w, at in ((Wi, 0), (Wf, 32)):
                for part in range(3):
                    sp.dma_start(w_gate[:, part, :, at:at + H0],
                                 w[part * D:(part + 1) * D, :].rearrange("(c p) h -> p c h", p=P)
                                 ).then_inc(loaded_w, 16)
            sp.dma_start(bias[0:H0, :], bi.rearrange("(h a) -> h a", a=1)).then_inc(loaded_w, 16)
            sp.dma_start(bias[32:32 + H0, :], bf.rearrange("(h a) -> h a", a=1)).then_inc(loaded_w, 16)
            with sp.Fori(1, G) as g:
                sp.wait_ge(turned, FIRST + (g - 1) * (2 * C) + C)
                sp.dma_start(ctx[:], ctx_dram[bass.ds(g * GB, GB)].rearrange("b s d -> s b d")
                             ).then_inc(loaded_ctx, 16)

        @block.gpsimd
        def _(pool):
            own = Own(pool, own_pool)
            nc.gpsimd.memset(w_gate[:], 0.0)
            nc.gpsimd.memset(bias[:], 0.0).then_inc(masks, 1)
            nc.gpsimd.memset(keep[:], 1.0)
            own(nc.gpsimd.memset(pen[:], 0.0))
            nc.gpsimd.memset(keep[:, :, 0:1], 0.0)
            nc.gpsimd.memset(pen[:, :, 0:1], -FAR).then_inc(masks, 1)
            pool.wait_ge(masks, 2)

        @block.scalar
        def _(act):
            own = Own(act, own_act)
            act.wait_ge(loaded_w, 8 * 16)

            def softplus():
                fa = f_abs[32:64, :]
                own(nc.scalar.activation(fa, fa, ACT.Exp, scale=-1.0))
                nc.scalar.activation(fa, fa, ACT.Ln, bias=1.0).then_inc(sp_done, 1)

            def body(g, first):
                for c in range(C):
                    act.wait_ge(turned, FIRST + g * (2 * C) + c + 1)
                    ph.hold(act, held_act)
                    nc.scalar.activation(M.ctxT[:, c, bass.ds(g * N, N)], ps[:, c, :], ACT.Copy).then_inc(cT_done, 1)
                if not first:
                    softplus()
                    act.wait_ge(logf_done, g)
                act.wait_ge(fmin_done, g + 1)
                own(nc.scalar.activation(f_abs[32:64, :], ps[32:64, 6, :], ACT.Abs, bias=bias[32:64, :]))

            body(0, True)
            with act.Fori(1, G) as g:
                own.enter(g - 1, 2)
                body(g, False)
            own.leave(G - 1)
            softplus()
            act.wait_ge(m_done, G)
            nc.scalar.activation(mrow[:], mrow[:], ACT.Exp, scale=-1.0).then_inc(em_done, 1)
            nc.scalar.activation(M.g[0:32, :], grow[:], ACT.Copy).then_inc(g_lead, 1)
            for kind in range(2):
                act.wait_ge(nat_T, kind + 1)
                nc.scalar.activation(M.nat[:, kind].rearrange("p g b h -> p (g b) h"),
                                     ps[:, kind, :].rearrange("p (n h) -> p n h", h=32)[:, :, 0:H0],
                                     ACT.Copy).then_inc(nat_done, 1)
            act.wait_ge(g_trail, 1)
            act.wait_ge(nat_done, 2)

        @block.vector
        def _(dve):
            own = Own(dve, own_dve)
            def normalise(g):
                for b in range(GB):
                    at = g * GB + b
                    ins = nc.vector.tensor_scalar(xn[:, b, :], K.x[:, bass.ds(at, 1), :].rearrange("p a d -> p (a d)"),
                                                  K.mv[:, bass.ds(at, 1), 0:1].rearrange("p a d -> p (a d)"),
                                                  K.rstd[:, bass.ds(at, 1)], ALU.subtract, ALU.mult)
                ins.then_inc(xn_done, 1)

            normalise(0)
            dve.wait_ge(loaded_w, 8 * 16)
            nc.vector.tensor_tensor(w_ctx[:], w_gate[:, 1], w_gate[:, 2], ALU.add).then_inc(wsum, 1)
            dve.wait_ge(masks, 2)

            def decays(g):
                cols = bass.ds(g * N, N)
                dve.wait_ge(sp_done, g + 1)
                nc.vector.tensor_tensor(logf[:], f_min[32:64, :], f_abs[32:64, :], ALU.subtract).then_inc(logf_done, 1)
                dve.wait_ge(logf_done, g + 1)
                own(nc.vector.tensor_tensor_scan(cumf[:], keep[:].rearrange("p b s -> p (b s)"), logf[:], 0.0,
                                                 ALU.mult, ALU.add))
                own(nc.vector.tensor_tensor(arow[:, cols], irow[:], cumf[:], ALU.subtract))
                own(nc.vector.tensor_tensor_scan(grow[:, cols], pen[:].rearrange("p b s -> p (b s)"), arow[:, cols], 0.0,
                                                 ALU.add, ALU.max))
                nc.vector.tensor_tensor(mrow[:, cols], cumf[:], grow[:, cols], ALU.add).then_inc(m_done, 1)

            def body(g, first):
                for c in range(C):
                    dve.wait_ge(turned, FIRST + g * (2 * C) + C + c + 1)
                    nc.vector.tensor_copy(M.xnT[:, c, bass.ds(g * N, N)], ps[:, 4 + c % 2, :]).then_inc(xT_done, 1)
                normalise(1 if first else within(nc, (g + 1) & (G - 1), G - 1))
                if not first:
                    decays(g - 1)
                dve.wait_ge(gates_done, g + 1)
                own(nc.vector.tensor_scalar(irow[:], ps[0:32, 6, :], bias[0:32, :], None, ALU.add))
                nc.vector.tensor_scalar(f_min[32:64, :], ps[32:64, 6, :], bias[32:64, :], 0.0, ALU.add, ALU.min
                                        ).then_inc(fmin_done, 1)

            body(0, True)
            with dve.Fori(1, G) as g:
                own.enter(g - 1, 4)
                dve.wait_ge(fmin_done, g)
                body(g, False)
            own.leave(G - 1)
            dve.wait_ge(fmin_done, G)
            decays(G - 1)
            dve.wait_ge(g_lead, 1)
            nc.vector.tensor_tensor(M.g[32:64, :], grow[:], M.g[0:32, :].bitcast(F32), ALU.subtract).then_inc(g_trail, 1)

        @block.tensor
        def _(pe):
            pe.sem_inc(turned, FIRST)
            pe.wait_ge(wsum, 1)
            with pe.Fori(0, G) as g:
                cols = bass.ds(g * N, N)
                pe.wait_ge(loaded_ctx, g * 16 + 16)
                for k in range(2 * C):
                    c, src = k % C, (ctx if k < C else xn)
                    if k == C:
                        pe.wait_ge(xn_done, g + 1)
                    if k >= C + 2:
                        pe.wait_ge(xT_done, g * C + c - 1)
                    for b in range(GB):
                        ins = nc.tensor.transpose(ps[:, k if k < C else C + c % 2, b * S:(b + 1) * S],
                                                  src[:, b, c * P:(c + 1) * P], K.ident[:])
                    ins.then_inc(turned, 1)
                pe.wait_ge(cT_done, g * C + C)
                for c in range(C):
                    nc.tensor.matmul(ps[0:64, 6, :], w_ctx[:, c, :], M.ctxT[:, c, cols], start=(c == 0), stop=False)
                pe.wait_ge(xT_done, g * C + C)
                for c in range(C):
                    ins = nc.tensor.matmul(ps[0:64, 6, :], w_gate[:, 0, c, :], M.xnT[:, c, cols], start=False,
                                           stop=(c == C - 1))
                ins.then_inc(gates_done, 1)
            pe.wait_ge(m_done, G)
            for kind, row in ((0, arow), (1, mrow)):
                if kind:
                    pe.wait_ge(em_done, 1)
                for b in range(B):
                    ins = nc.tensor.transpose(ps[:, kind, b * 32:(b + 1) * 32], row[:, b * S:(b + 1) * S],
                                              K.ident[0:32, 0:32])
                ins.then_inc(nat_T, 1)


def heads(nc, K, M, ctx_dram, ln_scale, blank_dram):
    PER = H0
    PAIRS = PER // 2
    RING = 4
    with Phase(nc, "heads") as ph:
        sb, sem = ph.sb, ph.sem
        ctx = sb("ctx", [P, GB, D])
        ctx1 = sb("ctx1", [P, 2, GB, H0, DH0 + 1])
        kT = sb("kT", [P, C, N])
        qz = sb("qz", [P, 2, 4, N])
        ident2 = sb("ident2", [64, H0])
        pick = sb("pick", [64, H0], F32R)
        far = sb("far", [P, GB, S], BF16)
        ident_b = sb("ident_b", [P, P], BF16)
        arg = sb("arg", [P, 2, GB, S])
        dec = sb("dec", [P, 2, GB, S])
        cmat = sb("cmat", [P, RING, GB, S])
        hraw = sb("hraw", [P, 2, GB, H0, DH0 + 1])
        sq = sb("sq", [P, GB * H0, DH0])
        small = sb("small", [P, 6, GB * H0])
        lnb = sb("lnb", [P, D])
        zeros = sb("zeros", [P, D])
        blanked, qz_blank = sem("blanked"), sem("qz_blank")

        loaded_w, loaded_ctx, masks, pick_done = sem("loaded_w"), sem("loaded_ctx"), sem("masks"), sem("pick_done")
        own_dve, own_pool, ctx1_done, kT_done, qz_done = sem("own_dve"), sem("own_pool"), sem("ctx1_done"), sem("kT_done"), sem("qz_done")
        qk, gb, arg_done, dec_done, c_done, pv, h_done = (
            sem("qk"), sem("gb"), sem("arg_done"), sem("dec_done"), sem("c_done"), sem("pv"), sem("h_done"))
        abs_done, mean_done, centred, sq_done, var_done, std_done, fac_done, norm_done, res_done = (
            sem("abs_done"), sem("mean_done"), sem("centred"), sem("sq_done"), sem("var_done"), sem("std_done"),
            sem("fac_done"), sem("norm_done"), sem("res_done"))
        held_act, held_pool, held_sp = sem("held_act"), sem("held_pool"), sem("held_sp")

        def after(g, n):
            if n < PER:
                return g, n
            return ((g + 1) % G if isinstance(g, int) else within(nc, (g + 1) & (G - 1), G - 1)), n - PER

        def half(g):
            return g % 2 if isinstance(g, int) else within(nc, g & 1, 1)

        def raw_heads(g):
            return hraw[:, bass.ds(half(g), 1)].rearrange("p a b h e -> p (a b h) e")

        row_stats = RowStats(nc, K, ph)
        block = ph.block()
        ps = K.ps

        @block.sync
        def _(sp):
            sp.dma_start(lnb[:], ln_scale.partition_broadcast(P)).then_inc(loaded_w, 16)

            def load(g):
                sp.dma_start(ctx[:], ctx_dram[bass.ds(g * GB, GB)].rearrange("b s d -> s b d")).then_inc(loaded_ctx, 16)

            load(0)
            sp.wait_ge(masks, 1)
            with sp.Fori(0, G) as g:
                sp.wait_ge(ctx1_done, g + 1)
                ph.hold(sp, held_sp)
                load(within(nc, (g + 1) & (G - 1), G - 1))
                quarter = (TILES + 1) // G * P
                sp.dma_start(blank_dram[bass.ds(g * quarter, quarter), :].rearrange("(n p) d -> p n d", p=P),
                             zeros[:].unsqueeze(1).broadcast_to([P, quarter // P, D])).then_inc(blanked, 16)
            sp.wait_ge(loaded_ctx, 16 * (G + 1))
            sp.wait_ge(loaded_w, 16)
            sp.wait_ge(blanked, 16 * G)

        def shift(eng, g):
            h = raw_heads(g)[:, :, 0:DH0]
            eng.tensor_tensor(h, h, small[:, 2].unsqueeze(2).broadcast_to([P, GB * H0, DH0]), ALU.subtract
                              ).then_inc(centred, 1)

        @block.gpsimd
        def _(pool):
            pool.sem_inc(norm_done, FIRST)
            pool.sem_inc(res_done, FIRST)
            own = Own(pool, own_pool)
            nc.gpsimd.memset(zeros[:], 0.0)
            nc.gpsimd.memset(ctx1[:, :, :, :, DH0:], 1.0)
            nc.gpsimd.memset(ident2[:], 0.0)
            nc.gpsimd.memset(far[:], 0.0)
            own(nc.gpsimd.memset(ident_b[:], 0.0))
            nc.gpsimd.affine_select(out=far[:], in_=far[:], compare_op=ALU.is_ge, fill=FAR, base=0,
                                    pattern=[[0, GB], [1, S]], channel_multiplier=-1)
            nc.gpsimd.affine_select(out=ident_b[:], in_=ident_b[:], compare_op=ALU.not_equal, fill=1.0,
                                    base=0, pattern=[[-1, P]], channel_multiplier=1)
            own(nc.gpsimd.affine_select(out=ident2[:], in_=ident2[:], compare_op=ALU.not_equal, fill=1.0,
                                        base=0, pattern=[[-1, H0]], channel_multiplier=1))
            nc.gpsimd.affine_select(out=ident2[:], in_=ident2[:], compare_op=ALU.not_equal, fill=1.0,
                                    base=-32, pattern=[[-1, H0]], channel_multiplier=1).then_inc(masks, 1)

            def values(g, count):
                pool.wait_ge(loaded_ctx, (count + 1) * 16)
                ph.hold(pool, held_pool)
                nc.gpsimd.tensor_copy(ctx1[:, bass.ds(half(g), 1), :, :, 0:DH0].rearrange("p a b h e -> p (a b h) e"),
                                      ctx[:].rearrange("p b (h e) -> p (b h) e", e=DH0)).then_inc(ctx1_done, 1)

            pool.wait_ge(loaded_w, 16)
            values(0, 0)
            values(1, 1)
            with pool.Fori(1, G) as g:
                own.enter(g - 1, 1)
                pool.wait_ge(mean_done, g)
                ph.hold(pool, held_pool)
                shift(nc.gpsimd, g - 1)
                pool.wait_ge(pv, g * PER)
                values(after(g, PER)[0], g + 1)
                pool.wait_ge(fac_done, g)
                ph.hold(pool, held_pool)
                nc.gpsimd.tensor_tensor(sq[:], raw_heads(g - 1)[:, :, 0:DH0],
                                        small[:, 5].unsqueeze(2).broadcast_to([P, GB * H0, DH0]),
                                        ALU.mult).then_inc(norm_done, 1)
                pool.wait_ge(norm_done, FIRST + g)
                ph.hold(pool, held_pool)
                out = sq[:].rearrange("p (b h) e -> p b (h e)", b=GB)
                own(nc.gpsimd.tensor_tensor(out, out, lnb[:].unsqueeze(1).broadcast_to([P, GB, D]), ALU.mult))
                xg = K.x[:, bass.ds((g - 1) * GB, GB), :]
                nc.gpsimd.tensor_tensor(xg, xg, out, ALU.add).then_inc(res_done, 1)
            own.leave(G - 1)

        @block.scalar
        def _(act):
            act.wait_ge(masks, 1)
            act.wait_ge(qz_blank, 1)
            nc.scalar.activation(pick[:], ident2[:], ACT.Copy).then_inc(pick_done, 1)

            def keys(g, c):
                nc.scalar.activation(kT[:, c, :], M.ctxT[:, c, bass.ds(g * N, N)], ACT.Copy).then_inc(kT_done, 1)

            def query(g, h):
                c, j = divmod(h, 4)
                r = slice(32 * j, 32 * j + 32)
                nc.scalar.activation(qz[r, c % 2, j, :], M.xnT[r, c, bass.ds(g * N, N)], ACT.Copy).then_inc(qz_done, 1)

            keys(0, 0)
            for h in range(4):
                query(0, h)
            nc.scalar.activation(K.scrap[:], K.ones[:, 0:1], ACT.Exp)

            def exp(g, n, first):
                act.wait_ge(arg_done, g * PER + n + 1)
                if not (first and n < 2):
                    act.wait_ge(c_done, g * PER + n - 1)
                nc.scalar.activation(dec[:, n % 2], arg[:, n % 2], ACT.Exp).then_inc(dec_done, 1)

            def pair(g, k):
                act.wait_ge(pv, g * PER + 2 * k + 2)
                if k == 0 and not (isinstance(g, int) and g == 0):
                    act.wait_ge(norm_done, FIRST + g - 1)
                ph.hold(act, held_act)
                nc.scalar.activation(hraw[:, bass.ds(half(g), 1), :, 2 * k:2 * k + 2, :].rearrange("p a b j e -> p (a b) j e"),
                                     ps[:, 2 + k % 2, 0:GB * 2 * (DH0 + 1)].rearrange("p (b j e) -> p b j e", b=GB, j=2),
                                     ACT.Copy).then_inc(h_done, 1)

            def row_sums(g):
                act.wait_ge(h_done, (g + 1) * PAIRS)
                ph.hold(act, held_act)
                nc.scalar.activation(small[:, 0], raw_heads(g)[:, :, DH0], ACT.Abs).then_inc(abs_done, 1)

            def square(g):
                act.wait_ge(centred, g + 1)
                act.wait_ge(res_done, FIRST + g)
                ph.hold(act, held_act)
                nc.scalar.activation(sq[:], raw_heads(g)[:, :, 0:DH0], ACT.Square).then_inc(sq_done, 1)

            def deviation(g):
                act.wait_ge(var_done, g + 1)
                nc.scalar.activation(small[:, 4], small[:, 3], ACT.Sqrt, bias=K.eps6[:, 0:1]).then_inc(std_done, 1)

            def body(g, first):
                for n in range(PER):
                    exp(g, n + 2, first)
                    if n % 2 == 0:
                        if n:
                            pair(g, n // 2 - 1)
                        elif not first:
                            pair(g - 1, PAIRS - 1)
                    if n % 4 == 2:
                        act.wait_ge(qk, g * PAIRS + (n // 4) * 2 + 2)
                        ph.hold(act, held_act)
                        keys(after(g, PER)[0], n // 4)
                    if n or not first:
                        act.wait_ge(qk, g * PAIRS + (n - 1) // 4 * 2 + 2)
                        ph.hold(act, held_act)
                        query(*after(g, n + 7))
                    if not first:
                        if n == 1:
                            row_sums(g - 1)
                        if n == 9:
                            square(g - 1)
                        if n == 12:
                            deviation(g - 1)

            exp(0, 0, True)
            exp(0, 1, True)
            for c in range(1, C):
                keys(0, c)
            for h in range(4, 8):
                query(0, h)
            body(0, True)
            with act.Fori(1, G) as g:
                body(g, False)
            pair(G - 1, PAIRS - 1)
            row_sums(G - 1)
            square(G - 1)
            deviation(G - 1)
            row_stats.root(act)

        @block.vector
        def _(dve):
            own = Own(dve, own_dve)

            def argument(g, n):
                g1, h = after(g, n)
                dve.wait_ge(gb, g * PER + n + 1)
                nc.vector.tensor_tensor(arg[:, n % 2], M.nat[:, 0, bass.ds(g1, 1), :, h:h + 1].rearrange("p a b h -> p (a b) h")
                                        .broadcast_to([P, GB, S]),
                                        ps[:, n % 2, :].rearrange("p (b s) -> p b s", b=GB),
                                        ALU.subtract).then_inc(arg_done, 1)

            def decayed(g, n, first):
                if n % 2 == 0:
                    dve.wait_ge(qk, g * PAIRS + n // 2 + 1)
                dve.wait_ge(dec_done, g * PER + n + 1)
                if not (first and n < RING):
                    dve.wait_ge(pv, g * PER + n - RING + 1)
                nc.vector.scalar_tensor_tensor(cmat[:, n % RING].rearrange("p b s -> p (b s)"), ps[:, 4 + n % 4, :],
                                               DH0 ** -0.5, dec[:, n % 2].rearrange("p b s -> p (b s)"),
                                               ALU.mult, ALU.mult).then_inc(c_done, 1)

            def divisor(g):
                dve.wait_ge(abs_done, g + 1)
                own(nc.vector.tensor_tensor(small[:, 1], small[:, 0],
                                            M.nat[:, 1, bass.ds(g, 1)].rearrange("p a b h -> p (a b h)"), ALU.max))
                own(nc.vector.tensor_scalar(small[:, 1], small[:, 1], 1e-6, None, ALU.add))
                own(nc.vector.reciprocal(small[:, 1], small[:, 1]))

            def mean(g):
                own(nc.vector.tensor_reduce(small[:, 2], raw_heads(g)[:, :, 0:DH0], AX, ALU.add))
                nc.vector.tensor_scalar(small[:, 2], small[:, 2], 1.0 / DH0, None, ALU.mult).then_inc(mean_done, 1)

            def variance(g):
                dve.wait_ge(sq_done, g + 1)
                own(nc.vector.tensor_reduce(small[:, 3], sq[:], AX, ALU.add))
                own(nc.vector.scalar_tensor_tensor(small[:, 3], small[:, 3], 1.0 / DH0, small[:, 1], ALU.mult, ALU.mult))
                nc.vector.tensor_tensor(small[:, 3], small[:, 3], small[:, 1], ALU.mult).then_inc(var_done, 1)

            def factor(g):
                dve.wait_ge(std_done, g + 1)
                own(nc.vector.reciprocal(small[:, 4], small[:, 4]))
                nc.vector.tensor_tensor(small[:, 5], small[:, 4], small[:, 1], ALU.mult).then_inc(fac_done, 1)

            def body(g, first):
                for n in range(PER):
                    argument(g, n + 2)
                    decayed(g, n + 1, first)
                    if not first:
                        for at, step in ((2, divisor), (3, mean), (10, variance), (13, factor)):
                            if n == at:
                                step(g - 1)

            nc.vector.memset(qz[:], 0.0).then_inc(qz_blank, 1)
            argument(0, 0)
            argument(0, 1)
            decayed(0, 0, True)
            body(0, True)
            with dve.Fori(1, G) as g:
                own.enter(g - 1, 7)
                body(g, False)
            own.leave(G - 1)
            last = G - 1
            dve.wait_ge(res_done, FIRST + 2)
            for b in range(4):
                row_stats.batch(b)
            divisor(last)
            mean(last)
            dve.wait_ge(mean_done, G)
            shift(nc.vector, last)
            for b in range(4, 6):
                row_stats.batch(b)
            variance(last)
            for b in range(6, 8):
                row_stats.batch(b)
            factor(last)
            dve.wait_ge(fac_done, G)
            for b in range(GB):
                r = slice(b * H0, (b + 1) * H0)
                ins = nc.vector.tensor_tensor(sq[:, r, :], raw_heads(last)[:, r, 0:DH0],
                                              small[:, 5, r].unsqueeze(2).broadcast_to([P, H0, DH0]), ALU.mult)
            own(ins)
            out = sq[:].rearrange("p (b h) e -> p b (h e)", b=GB)
            own(nc.vector.tensor_tensor(out, out, lnb[:].unsqueeze(1).broadcast_to([P, GB, D]), ALU.mult))
            xg = K.x[:, last * GB:, :]
            own(nc.vector.tensor_tensor(xg, xg, out, ALU.add))
            dve.wait_ge(res_done, FIRST + last)
            for b in range(8, B):
                row_stats.batch(b)
            row_stats.deviations(dve)

        @block.tensor
        def _(pe):
            pe.wait_ge(masks, 1)
            pe.wait_ge(pick_done, 1)

            def maxima(g, n, first):
                g1, h = after(g, n)
                if not (first and n < 2):
                    pe.wait_ge(arg_done, g * PER + n - 1)
                nc.tensor.matmul(ps[:, n % 2, :], ident_b[:], far[:].rearrange("p b s -> p (b s)"),
                                 start=True, stop=False)
                nc.tensor.matmul(ps[:, n % 2, :], pick[:, h:h + 1].broadcast_to([64, P]), M.g[:, bass.ds(g1 * N, N)],
                                 start=False, stop=True).then_inc(gb, 1)

            def scores(g, n, first):
                g1, h = after(g, n)
                c = h // 4
                if h % 4 == 0:
                    pe.wait_ge(kT_done, (g * C + c + 1) if n < PER else (g * C + C + 1))
                    pe.wait_ge(qz_done, g * PER + n + 4)
                if not (first and n < 4):
                    pe.wait_ge(c_done, g * PER + n - 2)
                for b in range(GB):
                    for j in (h % 4, h % 4 + 1):
                        ins = nc.tensor.matmul(ps[:, 4 + j, b * S:(b + 1) * S], kT[:, c, b * S:(b + 1) * S],
                                               qz[:, c % 2, j, b * S:(b + 1) * S], start=True, stop=True)
                ins.then_inc(qk, 1)

            def outputs(g, n, first):
                if n == 0:
                    pe.wait_ge(ctx1_done, g + 1)
                if n % 2 == 0 and not (first and n < 4):
                    pe.wait_ge(h_done, g * PAIRS + n // 2 - 1)
                pe.wait_ge(c_done, g * PER + n + 1)
                for b in range(GB):
                    at = (b * 2 + n % 2) * (DH0 + 1)
                    ins = nc.tensor.matmul(ps[:, 2 + n // 2 % 2, at:at + DH0 + 1], cmat[:, n % RING, b, :],
                                           ctx1[:, bass.ds(half(g), 1), b, n, :].rearrange("p a e -> p (a e)"),
                                           start=True, stop=True)
                ins.then_inc(pv, 1)

            def body(g, first):
                for n in range(PER):
                    maxima(g, n + 2, first)
                    if n % 2 == 0:
                        scores(g, n + 2, first)
                    outputs(g, n, first)

            maxima(0, 0, True)
            scores(0, 0, True)
            maxima(0, 1, True)
            body(0, True)
            with pe.Fori(1, G) as g:
                body(g, False)


def mlstm(nc, K, ctx_dram, Wi, bi, Wf, bf, ln_scale, blank_dram):
    with Phase(nc, "mlstm") as ph:
        M = Gates()
        M.xcT = ph.sb("xcT", [P, 2, C, T])
        M.xnT, M.ctxT = M.xcT[:, 0], M.xcT[:, 1]
        M.nat = ph.sb("nat", [P, 2, G, GB, H0])
        M.g = ph.sb("g", [64, T], F32R)
        gates(nc, K, M, ctx_dram, Wi, bi, Wf, bf)
        heads(nc, K, M, ctx_dram, ln_scale, blank_dram)


def turn(nc, K, ph, block, stage, lead, trail, ctx_dram=None, rms=None, logits=None, router=None, normal=None):
    sb, sem = ph.sb, ph.sem
    norm = ctx_dram is None
    mv, scale = K.mv, (K.rstd if rms is None else sb("scale", [P, B]))
    square = sb("square", [P, B])
    loaded = [sem("turn_loaded0"), sem("turn_loaded1")]
    staged, turned, lead_done, trail_done = sem("turn_staged"), sem("turn_turned"), sem("turn_lead_done"), sem("turn_trail_done")
    ms_done, rms_done = sem("turn_ms_done"), sem("turn_rms_done")
    plain_done, logit_mm, logit_done = sem("turn_plain_done"), sem("turn_logit_mm"), sem("turn_logit_done")
    loaded_w, own_dve, held_act = sem("turn_loaded_w"), sem("turn_own_dve"), sem("turn_held_act")
    if rms is not None:
        copied = [sem("turn_copied0"), sem("turn_copied1")]
        wcol = sb("wcol", [P, C])
        rw = sb("rw", [P, C, E])
        plain = sb("plain", [P, 2, C, N])
    BANKS = 2 * C
    ps = K.ps

    @block.sync
    def _(sp):
        if rms is not None:
            sp.dma_start(wcol[:], rms.rearrange("(c p) -> p c", p=P), allow_slow_non_contiguous=True).then_inc(loaded_w, 16)
            sp.dma_start(rw[:], router.rearrange("(c p) e -> p c e", p=P)).then_inc(loaded_w, 16)
            with sp.Fori(0, G // 2) as i:
                for q in range(2):
                    sp.wait_ge(staged, i * 2 + q + 1)
                    sp.dma_start(normal[:, bass.ds((i * 2 + q) * GB, GB), :], stage[:, q]).then_inc(copied[q], 16)
            for q in range(2):
                sp.wait_ge(copied[q], FIRST + G // 2 * 16)
        if not norm:
            for q in range(2):
                sp.dma_start(stage[:, q], ctx_dram[q * GB:(q + 1) * GB].rearrange("b s d -> s b d")
                             ).then_inc(loaded[q], 16)
            for q in range(2):
                sp.wait_ge(turned, (q + 1) * C)
                sp.dma_start(stage[:, q], ctx_dram[(2 + q) * GB:(3 + q) * GB].rearrange("b s d -> s b d")
                             ).then_inc(loaded[q], 16)

    @block.vector
    def _(dve):
        dve.sem_inc(trail_done, BANKS)
        for first in () if rms is None else copied:
            dve.sem_inc(first, FIRST)
        own = Own(dve, own_dve)
        if rms is not None:
            own(nc.vector.tensor_tensor(square[:], mv[:, :, 1], K.rstd[:], ALU.mult))
            nc.vector.tensor_tensor(square[:], square[:], K.rstd[:], ALU.mult).then_inc(ms_done, 1)
            dve.wait_ge(rms_done, 1)
            own(nc.vector.reciprocal(square[:], square[:]))
            own(nc.vector.tensor_tensor(scale[:], K.rstd[:], square[:], ALU.mult))
            dve.wait_ge(loaded_w, 32)

        def stage_rows(i, q):
            if rms is not None:
                dve.wait_ge(copied[q], FIRST + i * 16)
            if not (isinstance(i, int) and i == 0):
                dve.wait_ge(turned, (i - 1) * (2 * C) + (q + 1) * C)
            for b in range(GB):
                g4 = (i * 2 + q) * GB + b
                ins = nc.vector.tensor_scalar(
                    stage[:, q, b, :], K.x[:, bass.ds(g4, 1), :].rearrange("p a d -> p (a d)"),
                    mv[:, bass.ds(g4, 1), 0:1].rearrange("p a d -> p (a d)"), scale[:, bass.ds(g4, 1)],
                    ALU.subtract, ALU.mult)
            ins.then_inc(staged, 1)

        def body(i, more):
            for q in range(2):
                cols = bass.ds((i * 2 + q) * N, N)
                for c in range(C):
                    dve.wait_ge(lead_done, i * (2 * C) + q * C + c + 1)
                    src = ps[:, c + 4 * q, :] if rms is None else plain[:, q, c, :]
                    nc.vector.tensor_tensor(trail[:, c, cols], src, lead[:, c, cols].bitcast(F32),
                                            ALU.subtract).then_inc(trail_done, 1)
                if norm and more:
                    stage_rows(i + 1, q)

        if norm:
            stage_rows(0, 0)
            stage_rows(0, 1)
        with dve.Fori(0, G // 2 - 1) as i:
            body(i, True)
        body(G // 2 - 1, False)

    @block.scalar
    def _(act):
        act.sem_inc(logit_done, 2)
        if rms is not None:
            act.wait_ge(ms_done, 1)
            nc.scalar.activation(square[:], square[:], ACT.Sqrt, bias=K.eps6[:, 0:1]).then_inc(rms_done, 1)
            act.wait_ge(loaded_w, 32)
        with act.Fori(0, G // 2) as i:
            for q in range(2):
                cols = bass.ds((i * 2 + q) * N, N)
                for c in range(C):
                    act.wait_ge(turned, i * (2 * C) + q * C + c + 1)
                    if rms is None:
                        ph.hold(act, held_act)
                        nc.scalar.activation(lead[:, c, cols], ps[:, c + 4 * q, :], ACT.Copy).then_inc(lead_done, 1)
                    else:
                        act.wait_ge(logit_mm, i * 2 + q + 1)
                        act.wait_ge(trail_done, i * BANKS + q * C + c + 1)
                        nc.scalar.activation(plain[:, q, c, :], ps[:, c + 4 * q, :], ACT.Identity,
                                             scale=wcol[:, c:c + 1]).then_inc(plain_done, 1)
                        act.wait_ge(plain_done, i * (2 * C) + q * C + c + 1)
                        ph.hold(act, held_act)
                        nc.scalar.activation(lead[:, c, cols], plain[:, q, c, :], ACT.Copy).then_inc(lead_done, 1)
            if rms is not None:
                for q in range(2):
                    act.wait_ge(logit_mm, 2 + i * 2 + q + 1)
                    ph.hold(act, held_act)
                    nc.scalar.activation(logits[:, bass.ds((i * 2 + q) * GB, GB), :],
                                         ps[:, 4 * q, 0:GB * E].rearrange("p (b e) -> p b e", b=GB),
                                         ACT.Identity).then_inc(logit_done, 1)

    @block.tensor
    def _(pe):
        pe.sem_inc(logit_mm, 2)
        with pe.Fori(0, G // 2) as i:
            for q in range(2):
                if norm:
                    pe.wait_ge(staged, i * 2 + q + 1)
                else:
                    pe.wait_ge(loaded[q], i * 16 + 16)
                if rms is not None:
                    pe.wait_ge(logit_done, i * 2 + q + 1)
                for c in range(C):
                    pe.wait_ge(trail_done, i * BANKS + q * C + c + 1)
                    for b in range(GB):
                        ins = nc.tensor.transpose(ps[:, c + 4 * q, b * S:(b + 1) * S],
                                                  stage[:, q, b, c * P:(c + 1) * P], K.ident[:])
                    ins.then_inc(turned, 1)
            if rms is not None:
                for q in range(2):
                    pe.wait_ge(plain_done, i * (2 * C) + (q + 1) * C)
                    pe.wait_ge(loaded_w, 32)
                    for b in range(GB):
                        for c in range(C):
                            ins = nc.tensor.matmul(ps[:, 4 * q, b * E:(b + 1) * E], plain[:, q, c, b * S:(b + 1) * S],
                                                   rw[:, c, :], start=(c == 0), stop=(c == C - 1))
                    ins.then_inc(logit_mm, 1)

    def all_turned(eng):
        eng.wait_ge(trail_done, BANKS + G * C)
        if rms is not None:
            eng.wait_ge(logit_done, 2 + G)

    return all_turned


def choose(nc, K, R, ph, block, bank, logits):
    sb, sem = ph.sb, ph.sem
    top = sb("top", [P, B, 8])
    idx = sb("idx", [P, B, 8], U32)
    pos = sb("pos", [P, B, 2])
    row = sb("row", [P, B])
    chosen = sb("chosen", [P, 2, B, E])
    both = sb("both", [P, B, E])
    number = sb("number", [P, B, E])
    tile_number = sb("tile_number", [P, TILES + 1, E])
    tile_size = sb("tile_size", [P, E, B])
    before = sb("before", [P, P])
    keep = sb("keep", [P, E, B])
    count = sb("count", [P, E, B])
    incl = sb("incl", [P, E, B])
    excl = sb("excl", [P, E, B])
    full = sb("full", [P, E, B])
    tiles = sb("tiles", [P, E])
    tiles_incl = sb("tiles_incl", [P, E])
    base = sb("base", [P, E])
    place = sb("place", [P, B, E])
    at = sb("at", [P, 2, B])
    passed = sb("passed", [P, TILES + 1, E])
    whose = sb("whose", [P, TILES + 1])
    own_dve, shifted, exped, numbered, blank = sem("choose_own"), sem("shifted"), sem("exped"), sem("numbered"), sem("blank")
    both_done, counted = sem("both_done"), sem("counted")
    placed, slots_done = sem("placed"), sem("slots_done")
    counts_of = K.ps[:, bank, 0:2 * B * E].rearrange("p (k n) -> p k n", k=2)

    @block.gpsimd
    def _(pool):
        iota = lambda t, pattern: nc.gpsimd.iota(t[:], pattern=pattern, base=0, channel_multiplier=0,
                                                 allow_small_or_imprecise_dtypes=True)
        iota(number, [[0, B], [1, E]])
        iota(tile_number, [[1, TILES + 1], [0, E]])
        iota(tile_size, [[0, E], [P, B]])
        nc.gpsimd.memset(keep[:], 1.0).then_inc(blank, 1)
        nc.gpsimd.affine_select(out=before[:], in_=K.ones[:], compare_op=ALU.is_ge, fill=0.0, base=-1,
                                pattern=[[1, P]], channel_multiplier=-1)
        pool.wait_ge(blank, 1)
        nc.gpsimd.memset(keep[:, :, 0:1], 0.0).then_inc(numbered, 1)

    @block.scalar
    def _(act):
        act.wait_ge(shifted, 1)
        nc.scalar.activation(logits[:], logits[:], ACT.Exp).then_inc(exped, 1)

    @block.vector
    def _(dve):
        own = Own(dve, own_dve)
        wide = lambda v: v.unsqueeze(2).broadcast_to([P, B, E])
        own(nc.vector.tensor_reduce(row[:], logits[:], AX, ALU.max))
        nc.vector.tensor_tensor(logits[:], logits[:], wide(row[:]), ALU.subtract).then_inc(shifted, 1)
        dve.wait_ge(exped, 1)
        own(nc.vector.tensor_reduce(row[:], logits[:], AX, ALU.add))
        own(nc.vector.reciprocal(row[:], row[:]))
        own(nc.vector.tensor_tensor(logits[:], logits[:], wide(row[:]), ALU.mult))
        for b in range(B):
            ins = nc.vector.max(top[:, b, :], logits[:, b, :])
        own(ins)
        for b in range(B):
            ins = nc.vector.max_index(idx[:, b, :], top[:, b, :], logits[:, b, :])
        own(ins)
        own(nc.vector.tensor_copy(pos[:], idx[:, :, 0:2]))
        dve.wait_ge(numbered, 1)
        for j in range(2):
            ins = nc.vector.tensor_tensor(chosen[:, j], number[:], wide(pos[:, :, j]), ALU.is_equal)
        own(ins)
        nc.vector.tensor_tensor(both[:], chosen[:, 0], chosen[:, 1], ALU.add).then_inc(both_done, 1)
        own(nc.vector.tensor_tensor(row[:], top[:, :, 0], top[:, :, 1], ALU.add))
        own(nc.vector.reciprocal(row[:], row[:]))
        for j in range(2):
            nc.vector.tensor_tensor(R.weight[:, j, :], top[:, :, j], row[:], ALU.mult)
        dve.wait_ge(counted, 1)
        own(nc.vector.tensor_copy(count[:], counts_of[:, 1].rearrange("p (b e) -> p e b", e=E)))
        flat = lambda t: t[:].rearrange("p e b -> p (e b)")
        own(nc.vector.tensor_tensor_scan(flat(incl), flat(keep), flat(count), 0.0, ALU.mult, ALU.add))
        nc.vector.tensor_tensor(excl[:], incl[:], count[:], ALU.subtract)
        own(nc.vector.tensor_tensor(full[:], incl[:, :, B - 1:B].broadcast_to([P, E, B]), tile_size[:], ALU.is_gt))
        own(nc.vector.tensor_reduce(tiles[:], full[:], AX, ALU.add))
        own(nc.vector.tensor_tensor_scan(tiles_incl[:], K.ones[:, 0:E], tiles[:], 0.0, ALU.mult, ALU.add))
        own(nc.vector.tensor_tensor(base[:], tiles_incl[:], tiles[:], ALU.subtract))
        own(nc.vector.scalar_tensor_tensor(place[:], base[:].unsqueeze(1).broadcast_to([P, B, E]), float(P),
                                           excl[:].rearrange("p e b -> p b e"), ALU.mult, ALU.add))
        nc.vector.tensor_tensor(place[:], place[:], counts_of[:, 0].rearrange("p (b e) -> p b e", e=E), ALU.add
                                ).then_inc(placed, 1)
        dve.wait_ge(placed, 1)
        for j in range(2):
            ins = nc.vector.tensor_tensor(chosen[:, j], chosen[:, j], place[:], ALU.mult)
        own(ins)
        for j in range(2):
            ins = nc.vector.tensor_reduce(at[:, j], chosen[:, j], AX, ALU.add)
        own(ins)
        nc.vector.tensor_copy(R.slot[:], at[:]).then_inc(slots_done, 1)
        own(nc.vector.tensor_tensor(passed[:], tiles_incl[:].unsqueeze(1).broadcast_to([P, TILES + 1, E]),
                                    tile_number[:], ALU.is_le))
        own(nc.vector.tensor_reduce(whose[:], passed[:], AX, ALU.add))
        own(nc.vector.tensor_scalar(whose[:], whose[:], float(E - 1), None, ALU.min))
        own(nc.vector.tensor_copy(R.expert[:], whose[:]))

    def counts(pe):
        pe.wait_ge(both_done, 1)
        pe.wait_ge(numbered, 1)
        flat = both[:].rearrange("p b e -> p (b e)")
        nc.tensor.matmul(counts_of[:, 0], before[:], flat, start=True, stop=True)
        nc.tensor.matmul(counts_of[:, 1], K.ones[:], flat, start=True, stop=True).then_inc(counted, 1)

    return counts, placed, slots_done


SHARED = 2 * C * F + FC * D


def shared_weights(nc, ph, block, raw, weights):
    loaded = ph.sem("shared_loaded")

    @block.gpsimd
    def _(pool):
        for w, at, n in zip(weights, (0, C * F, 2 * C * F), (C * F, C * F, FC * D)):
            pool.dma_start(raw[:, at:at + n].rearrange("p (c f) -> p c f", f=w.shape[-1]),
                         w.rearrange("(c p) f -> p c f", p=P)).then_inc(loaded, 16)
        pool.wait_ge(loaded, 48)


def shared_expert(nc, K, R, lead, trail, normal, logits, rows_dram, raw):
    CH = SHARED // 512
    UP, DOWN = C * F, 2 * C * F
    with Phase(nc, "shared") as ph:
        sb, sem = ph.sb, ph.sem
        wl = sb("wl", [P, CH * 512], F32R)
        wt = sb("wt", [P, CH * 512], F32R)
        gated = sb("gated", [P, FC, N])
        hid = sb("hid", [P, FC, N])
        hl = sb("hl", [P, 2, FC, N], F32R)
        ht = sb("ht", [P, 2, FC, N], F32R)
        wl_done, wt_done, sorted_rows = sem("wl_done"), sem("wt_done"), sem("sorted_rows")
        gu, silu_done, hid_done, hl_done, ht_done = sem("gu"), sem("silu_done"), sem("hid_done"), sem("hl_done"), sem("ht_done")
        down, acc_done = sem("down"), sem("acc_done")
        block = ph.block()
        ps = K.ps

        @block.scalar
        def _(act):
            for k in range(CH):
                cols = slice(k * 512, (k + 1) * 512)
                nc.scalar.activation(wl[:, cols], raw[:, cols], ACT.Copy).then_inc(wl_done, 1)

        @block.vector
        def _(dve):
            for k in range(CH):
                dve.wait_ge(wl_done, k + 1)
                cols = slice(k * 512, (k + 1) * 512)
                nc.vector.tensor_tensor(wt[:, cols], raw[:, cols], wl[:, cols].bitcast(F32), ALU.subtract
                                        ).then_inc(wt_done, 1)

        counts, placed, slots_done = choose(nc, K, R, ph, block, 7, logits)

        @block.gpsimd
        def _(pool):
            def scatter(b):
                for j in range(2):
                    nc.gpsimd.indirect_dma_start(
                        out=rows_dram, out_offset=bass.IndirectOffsetOnAxis(ap=R.slot[:, j, b:b + 1], axis=0),
                        in_=normal[:, b, :], in_offset=None).then_inc(sorted_rows, 16)

            pool.wait_ge(slots_done, 1)
            for b in range(B):
                scatter(b)
            pool.wait_ge(sorted_rows, 16 * 2 * B)

        @block.scalar
        def _(act):
            for u in range(G):
                for f in range(FC):
                    act.wait_ge(gu, 2 * u + f + 1)
                    if u:
                        act.wait_ge(hid_done, 2 * u + f - 1)
                    nc.scalar.activation(gated[:, f, :], ps[:, 2 * f, :], ACT.Silu).then_inc(silu_done, 1)
                for f in range(FC):
                    act.wait_ge(hid_done, 2 * u + f + 1)
                    if u >= 2:
                        act.wait_ge(down, 4 * (u - 1))
                    nc.scalar.activation(hl[:, u % 2, f, :], hid[:, f, :], ACT.Copy).then_inc(hl_done, 1)

        @block.vector
        def _(dve):
            def add(u):
                for b in range(GB):
                    dve.wait_ge(down, 4 * u + b + 1)
                    xb = K.x[:, u * GB + b, :]
                    nc.vector.tensor_tensor(xb, xb, ps[:, 4 + b, :], ALU.add).then_inc(acc_done, 1)

            for u in range(G):
                for f in range(FC):
                    dve.wait_ge(silu_done, 2 * u + f + 1)
                    if u:
                        dve.wait_ge(ht_done, 2 * u)
                    nc.vector.tensor_tensor(hid[:, f, :], gated[:, f, :], ps[:, 2 * f + 1, :],
                                            ALU.mult).then_inc(hid_done, 1)
                for f in range(FC):
                    dve.wait_ge(hl_done, 2 * u + f + 1)
                    dve.wait_ge(hid_done, 2 * u + f + 1)
                    nc.vector.tensor_tensor(ht[:, u % 2, f, :], hid[:, f, :], hl[:, u % 2, f, :].bitcast(F32),
                                            ALU.subtract).then_inc(ht_done, 1)
                if u:
                    add(u - 1)
            add(G - 1)

        @block.tensor
        def _(pe):
            def up(u):
                cols = slice(u * N, (u + 1) * N)
                for f in range(FC):
                    if u:
                        pe.wait_ge(hid_done, 2 * u + f - 1)
                    for bank, at in ((2 * f, 0), (2 * f + 1, UP)):
                        if u == 0:
                            pe.wait_ge(wt_done, 4 if at else 2)
                        for c in range(C):
                            w = slice(at + c * F + f * P, at + c * F + (f + 1) * P)
                            ins = three_passes(nc, ps[:, bank, :], wl[:, w], wt[:, w], lead[:, c, cols],
                                               trail[:, c, cols], c == 0, c == C - 1)
                    ins.then_inc(gu, 1)
                    if u == 0 and f == 0:
                        counts(pe)

            def down_product(u):
                pe.wait_ge(ht_done, 2 * u + 2)
                for b in range(GB):
                    if u:
                        pe.wait_ge(acc_done, 4 * u - 3 + b)
                    else:
                        pe.wait_ge(wt_done, CH)
                        if b == GB - 1:
                            pe.wait_ge(placed, 1)
                    rows = slice(b * S, (b + 1) * S)
                    for f in range(FC):
                        w = slice(DOWN + f * D, DOWN + (f + 1) * D)
                        ins = three_passes(nc, ps[:, 4 + b, :], hl[:, u % 2, f, rows], ht[:, u % 2, f, rows],
                                           wl[:, w], wt[:, w], f == 0, f == FC - 1)
                    ins.then_inc(down, 1)

            for u in range(G):
                up(u)
                if u:
                    down_product(u - 1)
            down_product(G - 1)


def routed_experts(nc, K, R, rows_dram, y_dram, rms, weights):
    GU, DN = C * 2 * F, FC * D
    ACT_CUTS, DVE_CUTS, POOL_CUTS = 3, 3, 2
    with Phase(nc, "routed") as ph:
        sb, sem = ph.sb, ph.sem
        raw = sb("raw", [P, 4, GU + DN])
        wl = sb("wl", [P, 2, GU + DN], F32R)
        wt = sb("wt", [P, 2, GU + DN], F32R)
        h = sb("h", [P, 2, D])
        wcol = sb("wcol", [P, C])
        lead = sb("lead", [P, 2, C, P], F32R)
        trail = sb("trail", [P, 2, C, P], F32R)
        gated = sb("gated", [P, 2, F])
        hid = sb("hid", [P, 2, F])
        hl = sb("hl", [P, 2, FC, P], F32R)
        ht = sb("ht", [P, 2, FC, P], F32R)
        y = sb("y", [P, 2, D])
        raw_loaded = [sem(f"raw_loaded{k}") for k in range(4)]
        h_loaded = [sem("h_loaded0"), sem("h_loaded1")]
        stored = [sem("stored0"), sem("stored1")]
        wp_done = sem("wp_done")
        col_loaded, wl_done, wt_done, turned, lead_done, trail_done = (
            sem("col_loaded"), sem("wl_done"), sem("wt_done"), sem("turned"), sem("lead_done"), sem("trail_done"))
        gu, silu_done, hid_done, hid_turned, hl_done, ht_done, down, y_done = (
            sem("gu"), sem("silu_done"), sem("hid_done"), sem("hid_turned"), sem("hl_done"), sem("ht_done"),
            sem("down"), sem("y_done"))
        own_lead, held_pool, held_act, held_sp = sem("own_lead"), sem("held_pool"), sem("held_act"), sem("held_sp")
        block = ph.block()
        ps = K.ps

        def number(t):
            return t[0] * 4 + t[1]

        def move(t, d):
            m = t[1] + d
            return t[0] + m // 4, m % 4

        def pair(t):
            return t[0] * 2 + t[1] // 2

        def counts(t, least):
            return not isinstance(t[0], int) or number(t) >= least

        def slots(eng, slot):
            for m in range(3):
                slot((0, m))
            with eng.Fori(0, (TILES - 3) // 4) as k:
                for m in range(3, 7):
                    slot((k + m // 4, m % 4))

        LAST = (TILES // 4, TILES % 4)

        @block.sync
        def _(sp):
            def load_rows(t):
                n = number(t)
                if counts(t, 2):
                    sp.wait_ge(turned, n - 1)
                    ph.hold(sp, held_sp)
                sp.dma_start(h[:, t[1] % 2, :], rows_dram[bass.ds(n * P, P), :]).then_inc(h_loaded[t[1] % 2], 16)

            def load_weights(t):
                n = number(t)
                if counts(t, 4):
                    sp.wait_ge(wt_done, (n - 3) * DVE_CUTS)
                    ph.hold(sp, held_sp)
                    sp.wait_ge(wp_done, (n - 3) * POOL_CUTS)
                    ph.hold(sp, held_sp)
                e = sp.value_load(R.expert[0:1, bass.ds(n, 1)], min_val=0, max_val=E - 1)
                for w, at, size, where in ((weights[0], 0, 2 * F, 0), (weights[1], 0, 2 * F, F), (weights[2], GU, D, 0)):
                    wide = w.shape[-1]
                    part = raw[:, t[1], 0:GU] if at == 0 else raw[:, t[1], GU:]
                    sp.dma_start(part.rearrange("p (c f) -> p c f", f=size)[:, :, where:where + wide],
                                 w[bass.ds(e, 1)].rearrange("e (c p) f -> p (e c) f", p=P)).then_inc(raw_loaded[t[1]], 16)

            load_rows((0, 0))
            load_weights((0, 0))
            load_rows((0, 1))
            load_weights((0, 1))
            for m in range(2, 4):
                load_weights((0, m))
                load_rows((0, m))
            with sp.Fori(1, (TILES + 1) // 4) as k:
                for m in range(4):
                    load_weights((k, m))
                    load_rows((k, m))
            for s in h_loaded:
                sp.wait_ge(s, (TILES + 1) // 2 * 16)
            for s in raw_loaded:
                sp.wait_ge(s, (TILES + 1) // 4 * 48)

        @block.gpsimd
        def _(pool):
            def trailing(t, k):
                par, cols = t[1] % 2, slice(k * 512, (k + 1) * 512)
                nc.gpsimd.tensor_tensor(wt[:, par, cols], raw[:, t[1], cols], wl[:, par, cols].bitcast(F32),
                                        ALU.subtract).then_inc(wp_done, 1)

            def cut_gate_up(t):
                pool.wait_ge(wl_done, number(t) * ACT_CUTS + 2)
                pool.sem_inc(held_pool, 1)
                trailing(t, 3)

            def cut_down(t):
                n, par = number(t), t[1] % 2
                pool.wait_ge(raw_loaded[t[1]], t[0] * 48 + 48)
                if counts(t, 2):
                    pool.wait_ge(down, n - 1)
                pool.sem_inc(held_pool, 1)
                nc.gpsimd.tensor_scalar(wl[:, par, 5 * 512:], raw[:, t[1], 5 * 512:], 1.0, None, ALU.mult
                                        ).then_inc(own_lead, 1)
                pool.wait_ge(own_lead, n + 1)
                pool.sem_inc(held_pool, 1)
                trailing(t, 5)

            def slot(t):
                cut_down(t)
                cut_gate_up(move(t, 1))

            cut_gate_up((0, 0))
            slots(pool, slot)

        @block.scalar
        def _(act):
            act.dma_start(wcol[:], rms.rearrange("(c p) -> p c", p=P), allow_slow_non_contiguous=True).then_inc(col_loaded, 16)
            nc.scalar.activation(K.scrap[:], K.ones[:, 0:1], ACT.Silu)
            act.wait_ge(col_loaded, 16)

            def lead_of(t):
                n, par = number(t), t[1] % 2
                act.wait_ge(turned, n + 1)
                if counts(t, 2):
                    act.wait_ge(gu, n - 1)
                ph.hold(act, held_act)
                for c in range(C):
                    ins = nc.scalar.activation(lead[:, par, c, :], ps[:, par, c * P:(c + 1) * P], ACT.Copy,
                                               scale=wcol[:, c:c + 1])
                ins.then_inc(lead_done, 1)

            def silu(t):
                n, par = number(t), t[1] % 2
                act.wait_ge(gu, n + 1)
                if counts(t, 2):
                    act.wait_ge(hid_done, n - 1)
                ph.hold(act, held_act)
                nc.scalar.activation(gated[:, par, :], ps[:, 2 + par, 0:F], ACT.Silu).then_inc(silu_done, 1)

            def hidden_lead(t):
                n, par = number(t), t[1] % 2
                act.wait_ge(hid_turned, n + 1)
                if counts(t, 2):
                    act.wait_ge(down, n - 1)
                ph.hold(act, held_act)
                nc.scalar.activation(hl[:, par], ps[:, 4 + par, 0:F].rearrange("p (f s) -> p f s", f=FC),
                                     ACT.Copy).then_inc(hl_done, 1)

            def keep(t):
                n, par = number(t), t[1] % 2
                act.wait_ge(down, n + 1)
                if counts(t, 2):
                    act.wait_ge(stored[par], pair(t) * 16)
                ph.hold(act, held_act)
                nc.scalar.activation(y[:, par, :], ps[:, 6 + par, :], ACT.Copy).then_inc(y_done, 1)
                act.wait_ge(y_done, n + 1)
                act.dma_start(y_dram[bass.ds(n * P, P), :], y[:, par, :]).then_inc(stored[par], 16)

            def cut(t, first, last):
                n, par = number(t), t[1] % 2
                act.wait_ge(raw_loaded[t[1]], t[0] * 48 + 48)
                if counts(t, 2):
                    act.wait_ge(down if first == 4 else gu, n - 1)
                ph.hold(act, held_act)
                cols = slice(first * 512, (last + 1) * 512)
                nc.scalar.activation(wl[:, par, cols], raw[:, t[1], cols], ACT.Copy).then_inc(wl_done, 1)

            def slot(t):
                lead_of(move(t, 1))
                if counts(t, 1):
                    hidden_lead(move(t, -1))
                cut(t, 4, 4)
                cut(move(t, 1), 0, 1)
                silu(t)
                cut(move(t, 1), 2, 3)
                if counts(t, 1):
                    keep(move(t, -1))

            lead_of((0, 0))
            cut((0, 0), 0, 1)
            cut((0, 0), 2, 3)
            slots(act, slot)
            hidden_lead(move(LAST, -1))
            keep(move(LAST, -1))
            act.wait_ge(stored[0], (TILES + 1) // 2 * 16)
            act.wait_ge(stored[1], TILES // 2 * 16)

        @block.vector
        def _(dve):
            def cut(t, index, first, last):
                par, cols = t[1] % 2, slice(first * 512, (last + 1) * 512)
                dve.wait_ge(wl_done, number(t) * ACT_CUTS + index + 1)
                nc.vector.tensor_tensor(wt[:, par, cols], raw[:, t[1], cols], wl[:, par, cols].bitcast(F32),
                                        ALU.subtract).then_inc(wt_done, 1)

            def trail_of(t):
                n, par = number(t), t[1] % 2
                dve.wait_ge(lead_done, n + 1)
                for c in range(C):
                    ins = nc.vector.scalar_tensor_tensor(trail[:, par, c, :], ps[:, par, c * P:(c + 1) * P], wcol[:, c:c + 1],
                                                         lead[:, par, c, :].bitcast(F32), ALU.mult, ALU.subtract)
                ins.then_inc(trail_done, 1)

            def hidden(t):
                n, par = number(t), t[1] % 2
                dve.wait_ge(silu_done, n + 1)
                if counts(t, 2):
                    dve.wait_ge(hid_turned, n - 1)
                nc.vector.tensor_tensor(hid[:, par, :], gated[:, par, :], ps[:, 2 + par, F:2 * F], ALU.mult
                                        ).then_inc(hid_done, 1)

            def hidden_trail(t):
                n, par = number(t), t[1] % 2
                dve.wait_ge(hl_done, n + 1)
                nc.vector.tensor_tensor(ht[:, par], ps[:, 4 + par, 0:F].rearrange("p (f s) -> p f s", f=FC),
                                        hl[:, par].bitcast(F32), ALU.subtract).then_inc(ht_done, 1)

            def slot(t):
                trail_of(move(t, 1))
                if counts(t, 1):
                    hidden_trail(move(t, -1))
                cut(t, 2, 4, 4)
                cut(move(t, 1), 0, 0, 1)
                hidden(t)
                cut(move(t, 1), 1, 2, 2)

            dve.wait_ge(col_loaded, 16)
            trail_of((0, 0))
            cut((0, 0), 0, 0, 1)
            cut((0, 0), 1, 2, 2)
            slots(dve, slot)
            hidden_trail(move(LAST, -1))

        @block.tensor
        def _(pe):
            def turn_rows(t):
                n, par = number(t), t[1] % 2
                pe.wait_ge(h_loaded[par], pair(t) * 16 + 16)
                if counts(t, 2):
                    pe.wait_ge(trail_done, n - 1)
                for c in range(C):
                    ins = nc.tensor.transpose(ps[:, par, c * P:(c + 1) * P], h[:, par, c * P:(c + 1) * P], K.ident[:])
                ins.then_inc(turned, 1)

            def gate_up(t):
                n, par = number(t), t[1] % 2
                pe.wait_ge(trail_done, n + 1)
                pe.wait_ge(wt_done, n * DVE_CUTS + 2)
                pe.wait_ge(wp_done, n * POOL_CUTS + 1)
                if counts(t, 2):
                    pe.wait_ge(hid_done, n - 1)
                for c in range(C):
                    w = slice(c * 2 * F, (c + 1) * 2 * F)
                    ins = three_passes(nc, ps[:, 2 + par, :], lead[:, par, c, :], trail[:, par, c, :], wl[:, par, w],
                                       wt[:, par, w], c == 0, c == C - 1)
                ins.then_inc(gu, 1)

            def turn_hidden(t):
                n, par = number(t), t[1] % 2
                pe.wait_ge(hid_done, n + 1)
                if counts(t, 2):
                    pe.wait_ge(ht_done, n - 1)
                for f in range(FC):
                    ins = nc.tensor.transpose(ps[:, 4 + par, f * P:(f + 1) * P], hid[:, par, f * P:(f + 1) * P], K.ident[:])
                ins.then_inc(hid_turned, 1)

            def down_product(t):
                n, par = number(t), t[1] % 2
                pe.wait_ge(ht_done, n + 1)
                pe.wait_ge(wt_done, n * DVE_CUTS + 3)
                pe.wait_ge(wp_done, n * POOL_CUTS + 2)
                if counts(t, 2):
                    pe.wait_ge(y_done, n - 1)
                for f in range(FC):
                    w = slice(GU + f * D, GU + (f + 1) * D)
                    ins = three_passes(nc, ps[:, 6 + par, :], hl[:, par, f, :], ht[:, par, f, :], wl[:, par, w],
                                       wt[:, par, w], f == 0, f == FC - 1)
                ins.then_inc(down, 1)

            def slot(t):
                turn_rows(move(t, 1))
                if counts(t, 1):
                    turn_hidden(move(t, -1))
                gate_up(t)
                if counts(t, 1):
                    down_product(move(t, -1))

            turn_rows((0, 0))
            slots(pe, slot)
            turn_hidden(move(LAST, -1))
            down_product(move(LAST, -1))


def combine(nc, K, R, y_dram, L, w_dram):
    RING = 4
    with Phase(nc, "combine") as ph:
        y = ph.sb("y", [P, RING, 2, D])
        fetched = [ph.sem(f"fetched{k}") for k in range(RING)]
        first_done, acc_done = ph.sem("first_done"), ph.sem("acc_done")
        w, size, low, tern = (ph.sb(n, [P, C, D]) for n in ("w", "size", "low", "tern"))
        rows, edge = ph.sb("rows", [P, 1]), ph.sb("edge", [P, 2])
        loaded, abs_done, sums, own_dve, tern_done, turned, copied = (
            ph.sem(n) for n in ("loaded", "abs_done", "sums", "own_dve", "tern_done", "turned", "copied"))
        row_stats = RowStats(nc, K, ph)
        block = ph.block()
        ps = K.ps

        @block.sync
        def _(sp):
            sp.dma_start(w[:], w_dram.rearrange("(c p) i -> p c i", p=P)).then_inc(loaded, 16)

        @block.tensor
        def _(pe):
            pe.wait_ge(abs_done, 1)
            nc.tensor.matmul(ps[:, 4, 0:1], K.ones[:], rows[:], start=True, stop=True).then_inc(sums, 1)
            pe.wait_ge(tern_done, 1)
            for c in range(C):
                for o in range(C):
                    ins = nc.tensor.transpose(ps[:, c, o * P:(o + 1) * P], tern[:, o, c * P:(c + 1) * P], K.ident[:])
                ins.then_inc(turned, 1)

        @block.scalar
        def _(act):
            act.wait_ge(loaded, 16)
            nc.scalar.activation(size[:], w[:], ACT.Abs, accum_out=rows[:]).then_inc(abs_done, 1)
            for c in range(C):
                act.wait_ge(turned, c + 1)
                nc.scalar.activation(L.ternT[:, c, :], ps[:, c, :], ACT.Copy).then_inc(copied, 1)
            row_stats.root(act)
            act.wait_ge(copied, C)

        @block.gpsimd
        def _(pool):
            for b in range(B):
                if b >= RING:
                    pool.wait_ge(acc_done, b - RING + 1)
                for j in range(2):
                    nc.gpsimd.indirect_dma_start(
                        out=y[:, b % RING, j, :], out_offset=None, in_=y_dram,
                        in_offset=bass.IndirectOffsetOnAxis(ap=R.slot[:, j, b:b + 1], axis=0)
                    ).then_inc(fetched[b % RING], 16)

        @block.vector
        def _(dve):
            own = Own(dve, own_dve)
            flat = lambda t: t[:].rearrange("p c d -> p (c d)")

            def edges():
                dve.wait_ge(sums, 1)
                own(nc.vector.tensor_scalar(L.scale[:], ps[:, 4, 0:1], 1.0 / (D * D), None, ALU.mult))
                nc.vector.tensor_scalar(edge[:, 0:1], L.scale[:], 1e-10, 0.5, ALU.add, ALU.mult)
                own(nc.vector.tensor_scalar(edge[:, 1:2], L.scale[:], 1e-10, -0.5, ALU.add, ALU.mult))
                own(nc.vector.tensor_scalar(flat(low), flat(w), edge[:, 1:2], None, ALU.is_lt))

            def threes():
                nc.vector.scalar_tensor_tensor(flat(tern), flat(w), edge[:, 0:1], flat(low), ALU.is_gt, ALU.subtract
                                               ).then_inc(tern_done, 1)

            for b in range(B):
                for at, step in ((5, edges), (8, threes)):
                    if b == at:
                        step()
                dve.wait_ge(fetched[b % RING], 32 * (b // RING + 1))
                xb = K.x[:, b, :]
                nc.vector.scalar_tensor_tensor(xb, y[:, b % RING, 0, :], R.weight[:, 0, b:b + 1], xb, ALU.mult, ALU.add
                                               ).then_inc(first_done, 1)
                dve.wait_ge(first_done, b + 1)
                if b:
                    dve.wait_ge(acc_done, b)
                nc.vector.scalar_tensor_tensor(xb, y[:, b % RING, 1, :], R.weight[:, 1, b:b + 1], xb, ALU.mult, ALU.add
                                               ).then_inc(acc_done, 1)
                if b:
                    row_stats.batch(b - 1)
            dve.wait_ge(acc_done, B)
            row_stats.batch(B - 1)
            row_stats.deviations(dve)


def project(nc, K, name, lead, trail, ctx_dram, w_dram, b_dram, out_dram, rstd, ahead=()):
    W2 = 2 * P
    with Phase(nc, name) as ph:
        sb, sem = ph.sb, ph.sem
        raw = sb("raw", [P, C, W2])
        wl = sb("wl", [P, 2, C, W2], F32R)
        wt = sb("wt", [P, 2, C, W2], F32R)
        bias = sb("bias", [P, H1])
        head = sb("head", [P, 2, T])
        sq = sb("sq", [P, 2, N])
        total = sb("total", [P, T])
        raw_loaded, bias_loaded, wl_done, wt_done = sem("raw_loaded"), sem("bias_loaded"), sem("wl_done"), sem("wt_done")
        product, head_done, sq_done, acc_done, held = sem("product"), sem("head_done"), sem("sq_done"), sem("acc_done"), sem("held")
        stored = [sem("stored0"), sem("stored1")]
        sums, std_done, own_dve, blank = sem("sums"), sem("std_done"), sem("own_dve"), sem("blank")
        held_act, held_sp, ahead_loaded = sem("held_act"), sem("held_sp"), sem("ahead_loaded")
        block = ph.block()
        ps = K.ps
        all_turned = turn(nc, K, ph, block, head[:].rearrange("p q (b d) -> p q b d", b=GB), lead, trail, ctx_dram)
        UN = 4 * G

        @block.sync
        def _(sp):
            def load(pair):
                sp.dma_start(raw[:], w_dram[:, bass.ds(pair * W2, W2)].rearrange("(c p) n -> p c n", p=P)
                             ).then_inc(raw_loaded, 16)

            load(0)
            sp.dma_start(bias[:], b_dram.rearrange("(h p) -> p h", p=P), allow_slow_non_contiguous=True).then_inc(bias_loaded, 16)
            for tile, rows, by_element in ahead:
                sp.dma_start(tile, rows, allow_slow_non_contiguous=by_element).then_inc(ahead_loaded, 16)
            with sp.Fori(0, H1 // 4) as i:
                for p in range(2):
                    sp.wait_ge(wt_done, (i * 2 + p + 1) * 2)
                    ph.hold(sp, held_sp)
                    load(within(nc, (i * 2 + p + 1) & (H1 // 2 - 1), H1 // 2 - 1))
            sp.wait_ge(raw_loaded, 16 * (H1 // 2 + 1))
            if ahead:
                sp.wait_ge(ahead_loaded, 16 * len(ahead))

        def halves(p):
            return (lambda w: w[:, 2 * p:2 * p + 2, :])

        @block.gpsimd
        def _(pool):
            def cut(pair, p):
                pool.wait_ge(raw_loaded, (pair + 1) * 16)
                pool.sem_inc(held, 1)
                for k in range(2):
                    nc.gpsimd.tensor_scalar(halves(k)(wl[:, p]), halves(k)(raw[:]), 1.0, None, ALU.mult
                                            ).then_inc(wl_done, 1)

            nc.gpsimd.memset(total[:], 0.0).then_inc(blank, 1)
            with pool.Fori(0, H1 // 4) as i:
                for p in range(2):
                    pool.wait_ge(product, FIRST + i * UN + 8 * p)
                    cut(i * 2 + p + 1, 1 - p)

        @block.scalar
        def _(act):
            act.sem_inc(sq_done, FIRST)
            act.sem_inc(stored[0], FIRST)
            act.sem_inc(stored[1], FIRST)
            act.wait_ge(raw_loaded, 16)
            for k in range(2):
                nc.scalar.activation(halves(k)(wl[:, 0]), halves(k)(raw[:]), ACT.Copy).then_inc(wl_done, 1)
            act.wait_ge(bias_loaded, 16)
            with act.Fori(0, H1 // 4) as i:
                for n in range(UN):
                    hh, g = divmod(n, G)
                    b = bias[:, bass.ds(i * 4 + hh, 1)]
                    if g == 0:
                        act.wait_ge(stored[hh % 2], FIRST + (i * 2 + hh // 2) * 16)
                    act.wait_ge(product, FIRST + i * UN + n + 1)
                    ph.hold(act, held_act)
                    nc.scalar.activation(head[:, hh % 2, g * N:(g + 1) * N], ps[:, n % 8, :], ACT.Identity,
                                         bias=b).then_inc(head_done, 1)
                    act.wait_ge(acc_done, FIRST + i * UN + max(n - 1, 0))
                    ph.hold(act, held_act)
                    nc.scalar.activation(sq[:, n % 2, :], ps[:, n % 8, :], ACT.Square, bias=b).then_inc(sq_done, 1)
                    if g == G - 1:
                        act.wait_ge(head_done, i * UN + n + 1)
                        act.dma_start(out_dram[bass.ds(i * 4 + hh, 1)].rearrange("h p t -> (h p) t"),
                                      head[:, hh % 2, :]).then_inc(stored[hh % 2], 16)
            act.wait_ge(sums, 1)
            nc.scalar.activation(rstd[:], ps[:, 0, 0:B], ACT.Sqrt, scale=1.0 / INNER, bias=K.eps6[:, 0:1]
                                 ).then_inc(std_done, 1)
            for k in range(2):
                act.wait_ge(stored[k], FIRST + 16 * (H1 // 2))

        @block.vector
        def _(dve):
            dve.sem_inc(acc_done, FIRST)
            def cut(pair, p):
                for k in range(2):
                    dve.wait_ge(wl_done, pair * 2 + k + 1)
                    nc.vector.tensor_tensor(halves(k)(wt[:, p]), halves(k)(raw[:]), halves(k)(wl[:, p]).bitcast(F32),
                                            ALU.subtract).then_inc(wt_done, 1)

            cut(0, 0)
            dve.wait_ge(blank, 1)
            with dve.Fori(0, H1 // 4) as i:
                for n in range(UN):
                    g = n % G
                    dve.wait_ge(sq_done, FIRST + i * UN + n + 1)
                    dve.wait_ge(acc_done, FIRST + i * UN + max(n - 3, 0))
                    t = total[:, g * N:(g + 1) * N]
                    nc.vector.tensor_tensor(t, t, sq[:, n % 2, :], ALU.add).then_inc(acc_done, 1)
                    if n % 8 == 1:
                        p = n // 8
                        dve.wait_ge(product, FIRST + i * UN + 8 * p)
                        cut(i * 2 + p + 1, 1 - p)
            dve.wait_ge(std_done, 1)
            Own(dve, own_dve)(nc.vector.reciprocal(rstd[:], rstd[:]))

        @block.tensor
        def _(pe):
            pe.sem_inc(product, FIRST)
            all_turned(pe)
            with pe.Fori(0, H1 // 4) as i:
                for n in range(UN):
                    hh, g = divmod(n, G)
                    p = hh // 2
                    if n % 8 == 0:
                        pe.wait_ge(wt_done, (i * 2 + p + 1) * 2)
                    pe.wait_ge(sq_done, FIRST + i * UN + max(n - 7, 0))
                    w = slice((hh % 2) * P, (hh % 2 + 1) * P)
                    cols = slice(g * N, (g + 1) * N)
                    for c in range(C):
                        ins = three_passes(nc, ps[:, n % 8, :], wl[:, p, c, w], wt[:, p, c, w], lead[:, c, cols],
                                           trail[:, c, cols], c == 0, c == C - 1)
                    ins.then_inc(product, 1)
            pe.wait_ge(acc_done, FIRST + H1 * G)
            for b in range(B):
                ins = nc.tensor.matmul(ps[:, 0, b:b + 1], total[:, b * S:(b + 1) * S], K.ones[:, 0:1],
                                       start=True, stop=True)
            ins.then_inc(sums, 1)


def values(nc, K, lead, trail, w_dram, v_dram):
    with Phase(nc, "values") as ph:
        sb, sem = ph.sb, ph.sem
        raw = sb("raw", [P, C, N])
        wl = sb("wl", [P, 2, C, N], F32R)
        wt = sb("wt", [P, 2, C, N], F32R)
        out = sb("out", [P, 2, 4, GB, DH1])
        raw_loaded, wl_done, wt_done, held = sem("raw_loaded"), sem("wl_done"), sem("wt_done"), sem("held")
        product, even_done, odd_done = sem("product"), sem("even_done"), sem("odd_done")
        first_loaded = [sem(f"first_loaded{c}") for c in range(C)]
        stored, held_sp = [sem("stored0"), sem("stored1")], sem("held_sp")
        row_stats = RowStats(nc, K, ph)
        block = ph.block()
        ps = K.ps
        QUADS = H1 // 4

        @block.sync
        def _(sp):
            sp.sem_inc(stored[0], FIRST)
            sp.sem_inc(stored[1], FIRST)
            def load(quad):
                sp.dma_start(raw[:], w_dram[:, bass.ds(quad * N, N)].rearrange("(c p) n -> p c n", p=P)
                             ).then_inc(raw_loaded, 16)

            for c in range(C):
                sp.dma_start(raw[:, c, :], w_dram[c * P:(c + 1) * P, 0:N]).then_inc(first_loaded[c], 16)
            with sp.Fori(0, QUADS // 2) as i:
                for p in range(2):
                    sp.wait_ge(wt_done, (i * 2 + p + 1) * C)
                    ph.hold(sp, held_sp)
                    load(within(nc, (i * 2 + p + 1) & (QUADS - 1), QUADS - 1))
                    for k in range(G):
                        done = (i * 2 + p) * (B // 2) + (k + 1) * 2
                        sp.wait_ge(even_done, FIRST + done)
                        sp.wait_ge(odd_done, FIRST + done)
                        sp.dma_start(v_dram[bass.ds((i * 2 + p) * 4, 4), :, k * GB:(k + 1) * GB, :]
                                     .rearrange("h l b e -> l h (b e)"),
                                     out[:, k % 2].rearrange("p h b e -> p h (b e)")).then_inc(stored[k % 2], 16)
            for k in range(2):
                sp.wait_ge(stored[k], FIRST + 16 * 2 * QUADS)
            sp.wait_ge(raw_loaded, 16 * QUADS)

        @block.gpsimd
        def _(pool):
            def cut(quad, p):
                pool.wait_ge(raw_loaded, quad * 16)
                pool.sem_inc(held, 1)
                for c in range(C):
                    nc.gpsimd.tensor_scalar(wl[:, p, c, :], raw[:, c, :], 1.0, None, ALU.mult).then_inc(wl_done, 1)

            with pool.Fori(0, QUADS // 2) as i:
                for p in range(2):
                    pool.wait_ge(product, FIRST + i * 2 * B + B * p)
                    cut(i * 2 + p + 1, 1 - p)

        def slot(b):
            return (lambda out: out[:, (b // GB) % 2, :, b % GB, :])

        @block.scalar
        def _(act):
            act.sem_inc(even_done, FIRST)
            for c in range(C):
                act.wait_ge(first_loaded[c], 16)
                nc.scalar.activation(wl[:, 0, c, :], raw[:, c, :], ACT.Copy).then_inc(wl_done, 1)
            with act.Fori(0, QUADS // 2) as i:
                for n in range(2 * B):
                    p, b = divmod(n, B)
                    if b % 2 == 0:
                        if b % GB == 0:
                            act.wait_ge(stored[(b // GB) % 2], FIRST + ((i * 2 + p) * 2 + b // (2 * GB)) * 16)
                        act.wait_ge(product, FIRST + i * 2 * B + n + 1)
                        nc.scalar.activation(slot(b)(out), ps[:, n % 8, :].rearrange("p (h e) -> p h e", h=4),
                                             ACT.Copy).then_inc(even_done, 1)
            row_stats.root(act)

        @block.vector
        def _(dve):
            dve.sem_inc(odd_done, FIRST)
            def cut(quad, p, c):
                dve.wait_ge(wl_done, quad * C + c + 1)
                nc.vector.tensor_tensor(wt[:, p, c, :], raw[:, c, :], wl[:, p, c, :].bitcast(F32),
                                        ALU.subtract).then_inc(wt_done, 1)

            for c in range(C):
                cut(0, 0, c)
            with dve.Fori(0, QUADS // 2) as i:
                for n in range(2 * B):
                    p, b = divmod(n, B)
                    if b % 2 == 1:
                        if b % GB == 1:
                            dve.wait_ge(stored[(b // GB) % 2], FIRST + ((i * 2 + p) * 2 + b // (2 * GB)) * 16)
                        dve.wait_ge(product, FIRST + i * 2 * B + n + 1)
                        nc.vector.tensor_copy(slot(b)(out), ps[:, n % 8, :].rearrange("p (h e) -> p h e", h=4)
                                              ).then_inc(odd_done, 1)
                        if b % 4 == 3:
                            row_stats.batch(i * (B // 2) + (p * 4 + b // 4))
                        if b in (3, 5, 7, 9):
                            cut(i * 2 + p + 1, 1 - p, (b - 3) // 2)
            row_stats.deviations(dve)

        @block.tensor
        def _(pe):
            pe.sem_inc(product, FIRST)
            with pe.Fori(0, QUADS // 2) as i:
                for n in range(2 * B):
                    p, b = divmod(n, B)
                    if b == 0:
                        pe.wait_ge(wt_done, (i * 2 + p + 1) * C)
                    pe.wait_ge(odd_done if b % 2 else even_done, FIRST + i * B + max((n - 8) // 2 + 1, 0))
                    rows = slice(b * S, (b + 1) * S)
                    for c in range(C):
                        ins = three_passes(nc, ps[:, n % 8, :], lead[:, c, rows], trail[:, c, rows], wl[:, p, c, :],
                                           wt[:, p, c, :], c == 0, c == C - 1)
                    ins.then_inc(product, 1)


class Weights:
    pass


def attend_weights(ph, o_w, o_b, v_b, nq, nk):
    A = Weights()
    A.raw = ph.sb("raw", [P, H1, D])
    A.kcol, A.qcol, A.vbias = (ph.sb(n, [P, H1]) for n in ("kcol", "qcol", "vbias"))
    A.obias = ph.sb("obias", [P, D])
    A.loads = [(A.raw[:], o_w.rearrange("(h p) d -> p h d", p=P), False),
               (A.obias[:], o_b.partition_broadcast(P), False)]
    A.loads += [(t[:], d.rearrange("(h p) -> p h", p=P), True) for t, d in ((A.kcol, nk), (A.qcol, nq), (A.vbias, v_b))]
    return A


def attend(nc, K, A, q_dram, k_dram, v_dram, rq, rk):
    QUADS = H1 // 4
    IT = G * QUADS
    with Phase(nc, "attend") as ph:
        sb, sem = ph.sb, ph.sem
        wol = sb("wol", [P, H1, D], F32R)
        wot = sb("wot", [P, H1, D], F32R)
        q, k = A.raw[:, 0:4], A.raw[:, 4:8]
        v = A.raw[:, 8:12].rearrange("p j (b e) -> p j b e", b=GB)
        kn = A.raw[:, 12:14]
        prob = A.raw[:, 14:16].rearrange("p j (b s) -> p j b s", b=GB)
        kcol, qcol, vbias, obias = A.kcol, A.qcol, A.vbias, A.obias
        rkb = sb("rkb", [P, T])
        probT = sb("probT", [P, 2, N])
        ol = sb("ol", [P, 2, 4, N], F32R)
        ot = sb("ot", [P, 2, 4, N], F32R)
        row = sb("row", [P, 2, 4, GB])
        qk_ring = [sem(f"qk_ring{j}") for j in range(4)]
        v_ring = [sem(f"v_ring{j}") for j in range(4)]
        wol_done, wot_done = sem("wol_done"), sem("wot_done")
        bias_done, spread, rkb_done = sem("bias_done"), sem("spread"), sem("rkb_done")
        kn_done, scores, max_done, exp_done, sum_done, prob_done = (
            sem("kn_done"), sem("scores"), sem("max_done"), sem("exp_done"), sem("sum_done"), sem("prob_done"))
        prob_T, probT_done, mixed, ol_done, ot_done, final, acc_done = (
            sem("prob_T"), sem("probT_done"), sem("mixed"), sem("ol_done"), sem("ot_done"), sem("final"), sem("acc_done"))
        own_dve, row_done, held_sp, held_act = sem("own_dve"), sem("row_done"), sem("held_sp"), sem("held_act")

        def group(it):
            return it >> 2 if isinstance(it, int) else within(nc, it >> 2, G - 1)

        def quad_of(it):
            return it & 3 if isinstance(it, int) else within(nc, it & 3, QUADS - 1)

        def blocks(eng, body):
            body(0, 0, True, False)
            body(1, 1, False, False)
            with eng.Fori(1, IT // 2 - 1) as i:
                body(i * 2, 0, False, False)
                body(i * 2 + 1, 1, False, False)
            body(IT - 2, 0, False, False)
            body(IT - 1, 1, False, True)

        row_stats = RowStats(nc, K, ph)
        block = ph.block()
        ps = K.ps

        @block.sync
        def _(sp):
            def load_qk(it, j):
                g, h = group(it), quad_of(it) * 4 + j
                cols = bass.ds(g * N, N)
                sp.dma_start(q[:, j, :], q_dram[bass.ds(h, 1), :, cols].rearrange("h p t -> (h p) t")).then_inc(qk_ring[j], 16)
                sp.dma_start(k[:, j, :], k_dram[bass.ds(h, 1), :, cols].rearrange("h p t -> (h p) t")).then_inc(qk_ring[j], 16)

            def load_v(it, j):
                g, h = group(it), quad_of(it) * 4 + j
                sp.dma_start(v[:, j].rearrange("p b e -> p (b e)"),
                             v_dram[bass.ds(h, 1), :, bass.ds(g * GB, GB), :].rearrange("h l b e -> (h l) (b e)")
                             ).then_inc(v_ring[j], 16)

            sp.wait_ge(wot_done, 2)
            for j in range(4):
                load_qk(0, j)
            sp.wait_ge(wot_done, 3)
            for j in range(4):
                load_v(0, j)
            with sp.Fori(1, IT) as it:
                for what, j in (("qk", 0), ("qk", 1), ("qk", 2), ("v", 0), ("qk", 3), ("v", 1), ("v", 2), ("v", 3)):
                    if what == "qk":
                        sp.wait_ge(scores, (it - 1) * 4 + j + 1)
                        ph.hold(sp, held_sp)
                        load_qk(it, j)
                    else:
                        sp.wait_ge(mixed, (it - 1) * 4 + j + 1)
                        ph.hold(sp, held_sp)
                        load_v(it, j)

        @block.gpsimd
        def _(pool):
            with pool.Fori(0, G) as g:
                xg = K.x[:, bass.ds(g * GB, GB), :]
                nc.gpsimd.tensor_tensor(xg, xg, obias[:].unsqueeze(1).broadcast_to([P, GB, D]), ALU.add
                                        ).then_inc(bias_done, 1)

        @block.scalar
        def _(act):
            act.sem_inc(exp_done, FIRST)
            act.sem_inc(probT_done, FIRST)
            for i in range(QUADS):
                at = slice(i * 4, i * 4 + 4)
                nc.scalar.activation(wol[:, at, :], A.raw[:, at, :], ACT.Copy).then_inc(wol_done, 1)
            for g in range(G):
                act.wait_ge(spread, g + 1)
                nc.scalar.activation(rkb[:, g * N:(g + 1) * N], ps[:, g, :], ACT.Copy).then_inc(rkb_done, 1)
            nc.scalar.activation(K.scrap[:], K.ones[:, 0:1], ACT.Exp)

            def softmax(it, j):
                n, g = it * 4 + j, group(it)
                act.wait_ge(max_done, n + 1)
                ph.hold(act, held_act)
                for b in range(GB):
                    ins = nc.scalar.activation(prob[:, j % 2, b, :], ps[:, j % 2, b * S:(b + 1) * S], ACT.Exp,
                                               bias=row[:, j % 2, 1, b:b + 1], scale=rq[:, bass.ds(g * GB + b, 1)],
                                               accum_out=row[:, j % 2, 2, b:b + 1])
                ins.then_inc(exp_done, 1)

            def turned(it, j):
                act.wait_ge(prob_T, it * 4 + j + 1)
                nc.scalar.activation(probT[:, j % 2, :], ps[:, 2 + j % 2, :], ACT.Copy).then_inc(probT_done, 1)

            def head(it, par, j):
                act.wait_ge(mixed, it * 4 + j + 1)
                ph.hold(act, held_act)
                nc.scalar.activation(ol[:, par, j, :], ps[:, 4 + j % 2, :], ACT.Identity,
                                     bias=vbias[:, bass.ds(quad_of(it) * 4 + j, 1)]).then_inc(ol_done, 1)

            def body(it, par, first, last):
                for j in range(4):
                    if j == 0 and not first:
                        head(it - 1, 1 - par, 2)
                        head(it - 1, 1 - par, 3)
                    if j >= 2:
                        head(it, par, j - 2)
                    if j < 3:
                        softmax(it, j + 1)
                    elif not last:
                        softmax(it + 1, 0)
                    turned(it, j)

            softmax(0, 0)
            blocks(act, body)
            head(IT - 1, 1, 2)
            head(IT - 1, 1, 3)
            row_stats.root(act)

        @block.vector
        def _(dve):
            dve.sem_inc(acc_done, FIRST)
            dve.sem_inc(ot_done, FIRST)
            own = Own(dve, own_dve)
            for i in range(QUADS):
                dve.wait_ge(wol_done, i + 1)
                at = slice(i * 4, i * 4 + 4)
                nc.vector.tensor_tensor(wot[:, at, :], A.raw[:, at, :], wol[:, at, :].bitcast(F32), ALU.subtract
                                        ).then_inc(wot_done, 1)
            own(nc.vector.scalar_tensor_tensor(kcol[:], kcol[:], DH1 ** -0.5, qcol[:], ALU.mult, ALU.mult))
            dve.wait_ge(rkb_done, G)
            dve.wait_ge(bias_done, G)

            def keys(it, j):
                dve.wait_ge(qk_ring[j], (it + 1) * 32)
                nc.vector.scalar_tensor_tensor(kn[:, j % 2, :], k[:, j, :], kcol[:, bass.ds(quad_of(it) * 4 + j, 1)],
                                               rkb[:, bass.ds(group(it) * N, N)], ALU.mult, ALU.mult).then_inc(kn_done, 1)

            def peak(it, j):
                n = it * 4 + j
                dve.wait_ge(scores, n + 1)
                r = row[:, j % 2]
                nc.vector.tensor_reduce(r[:, 0], ps[:, j % 2, :].rearrange("p (b s) -> p b s", b=GB), AX, ALU.max
                                        ).then_inc(row_done, 1)
                dve.wait_ge(row_done, n + 1)
                nc.vector.scalar_tensor_tensor(r[:, 1], r[:, 0], -1.0, rq[:, bass.ds(group(it) * GB, GB)], ALU.mult,
                                               ALU.mult).then_inc(max_done, 1)

            def divide(it, j):
                n = it * 4 + j
                dve.wait_ge(exp_done, FIRST + n + 1)
                r = row[:, j % 2]
                nc.vector.reciprocal(r[:, 3], r[:, 2]).then_inc(sum_done, 1)
                dve.wait_ge(sum_done, n + 1)
                nc.vector.tensor_tensor(prob[:, j % 2], prob[:, j % 2], r[:, 3].unsqueeze(2).broadcast_to([P, GB, S]),
                                        ALU.mult).then_inc(prob_done, 1)

            def rest(it, par, j):
                dve.wait_ge(ol_done, it * 4 + j + 1)
                nc.vector.scalar_tensor_tensor(ot[:, par, j, :], ps[:, 4 + j % 2, :], vbias[:, bass.ds(quad_of(it) * 4 + j, 1)],
                                               ol[:, par, j, :].bitcast(F32), ALU.add, ALU.subtract).then_inc(ot_done, 1)

            def add(it, b):
                dve.wait_ge(final, FIRST + it * GB + b + 1)
                dve.wait_ge(acc_done, FIRST + it * GB + b)
                xb = K.x[:, bass.ds(group(it) * GB + b, 1), :].rearrange("p a d -> p (a d)")
                nc.vector.tensor_tensor(xb, xb, ps[:, 6 + b % 2, :], ALU.add).then_inc(acc_done, 1)

            def body(it, par, first, last):
                for j in range(4):
                    if j == 0 and not first:
                        rest(it - 1, 1 - par, 2)
                        rest(it - 1, 1 - par, 3)
                    if j >= 2:
                        rest(it, par, j - 2)
                    if j < 3:
                        peak(it, j + 1)
                    elif not last:
                        peak(it + 1, 0)
                    if j < 2:
                        keys(it, j + 2)
                    elif not last:
                        keys(it + 1, j - 2)
                    if not first:
                        if j:
                            add(it - 1, j - 1)
                    if j < 3:
                        divide(it, j + 1)
                    elif not last:
                        divide(it + 1, 0)
                    if j == 3 and not first:
                        add(it - 1, 3)

            dve.wait_ge(wot_done, QUADS)
            keys(0, 0)
            keys(0, 1)
            peak(0, 0)
            divide(0, 0)
            blocks(dve, body)
            rest(IT - 1, 1, 2)
            rest(IT - 1, 1, 3)
            for b in range(GB):
                add(IT - 1, b)
                for n in range(3 * b, 3 * b + 3):
                    row_stats.batch(n)
                dve.wait_ge(acc_done, FIRST + (IT - 1) * GB + b + 1)
                row_stats.batch((G - 1) * GB + b)
            row_stats.deviations(dve)

        @block.tensor
        def _(pe):
            pe.sem_inc(final, FIRST)
            for g in range(G):
                for b in range(GB):
                    ins = nc.tensor.matmul(ps[:, g, b * S:(b + 1) * S],
                                           rk[:, g * GB + b:g * GB + b + 1].broadcast_to([P, P]), K.ident[:],
                                           start=True, stop=True)
                ins.then_inc(spread, 1)
            pe.wait_ge(rkb_done, G)

            def n_before(it, j):
                return not isinstance(it, int) or it * 4 + j >= 2

            def score(it, j):
                pe.wait_ge(kn_done, it * 4 + j + 1)
                if n_before(it, j):
                    pe.wait_ge(exp_done, FIRST + it * 4 + j - 1)
                for b in range(GB):
                    s = slice(b * S, (b + 1) * S)
                    ins = nc.tensor.matmul(ps[:, j % 2, s], q[:, j, s], kn[:, j % 2, s], start=True, stop=True)
                ins.then_inc(scores, 1)

            def turn_prob(it, j):
                pe.wait_ge(prob_done, it * 4 + j + 1)
                if n_before(it, j):
                    pe.wait_ge(probT_done, FIRST + it * 4 + j - 1)
                for b in range(GB):
                    ins = nc.tensor.transpose(ps[:, 2 + j % 2, b * S:(b + 1) * S], prob[:, j % 2, b, :], K.ident[:])
                ins.then_inc(prob_T, 1)

            def mix(it, j):
                pe.wait_ge(probT_done, FIRST + it * 4 + j + 1)
                pe.wait_ge(v_ring[j], (it + 1) * 16)
                if n_before(it, j):
                    pe.wait_ge(ot_done, FIRST + it * 4 + j - 1)
                for b in range(GB):
                    s = slice(b * S, (b + 1) * S)
                    ins = nc.tensor.matmul(ps[:, 4 + j % 2, s], v[:, j, b, :], probT[:, j % 2, s], start=True, stop=True)
                ins.then_inc(mixed, 1)

            def output(it, par, b):
                if b == 0:
                    pe.wait_ge(ot_done, FIRST + it * 4 + 4)
                    if isinstance(it, int) and it == 0:
                        pe.wait_ge(wot_done, QUADS)
                if not isinstance(it, int) or it * GB + b >= 2:
                    pe.wait_ge(acc_done, FIRST + it * GB + b - 1)
                rows = slice(b * S, (b + 1) * S)
                for j in range(4):
                    w = bass.ds(quad_of(it) * 4 + j, 1)
                    ins = three_passes(nc, ps[:, 6 + b % 2, :], ol[:, par, j, rows], ot[:, par, j, rows],
                                       wol[:, w, :].rearrange("p a d -> p (a d)"),
                                       wot[:, w, :].rearrange("p a d -> p (a d)"), j == 0, j == 3)
                ins.then_inc(final, 1)

            def body(it, par, first, last):
                for j in range(4):
                    if j < 3:
                        score(it, j + 1)
                    elif not last:
                        score(it + 1, 0)
                    turn_prob(it, j)
                    if not first:
                        output(it - 1, 1 - par, j)
                    if j:
                        mix(it, j - 1)
                mix(it, 3)

            score(0, 0)
            blocks(pe, body)
            for b in range(GB):
                output(IT - 1, 1, b)


class LastWeights:
    pass


def ternary(nc, K, L, b_dram, out):
    with Phase(nc, "ternary") as ph:
        sb, sem = ph.sb, ph.sem
        lead, trail = operands(ph)
        stage = sb("stage", [P, 2, GB, D])
        bias = sb("bias", [P, D])
        loaded = sem("loaded")
        bias_done, product, y_done, stored = sem("bias_done"), sem("product"), sem("y_done"), sem("stored")
        block = ph.block()
        ps = K.ps
        all_turned = turn(nc, K, ph, block, stage, lead, trail)

        @block.sync
        def _(sp):
            sp.dma_start(bias[:], b_dram.partition_broadcast(P)).then_inc(loaded, 16)
            with sp.Fori(0, G - 1) as g:
                sp.wait_ge(y_done, (g + 1) * GB)
                at = bass.ds(g * GB, GB)
                sp.dma_start(out[at].rearrange("b s d -> s b d"), K.x[:, at, :]).then_inc(stored, 16)
            for b in range(B - GB, B):
                sp.wait_ge(y_done, b + 1)
                sp.dma_start(out[b], K.x[:, b, :]).then_inc(stored, 16)
            sp.wait_ge(stored, 16 * (G - 1 + GB))

        @block.gpsimd
        def _(pool):
            pool.wait_ge(loaded, 16)
            all_turned(pool)
            with pool.Fori(0, G) as g:
                xg = K.x[:, bass.ds(g * GB, GB), :]
                nc.gpsimd.tensor_tensor(xg, xg, bias[:].unsqueeze(1).broadcast_to([P, GB, D]), ALU.add
                                        ).then_inc(bias_done, 1)

        @block.vector
        def _(dve):
            with dve.Fori(0, G) as g:
                dve.wait_ge(bias_done, g + 1)
                for b in range(GB):
                    dve.wait_ge(product, g * GB + b + 1)
                    xb = K.x[:, bass.ds(g * GB + b, 1), :].rearrange("p a d -> p (a d)")
                    nc.vector.scalar_tensor_tensor(xb, ps[:, b, :], L.scale[:, 0:1], xb, ALU.mult, ALU.add
                                                   ).then_inc(y_done, 1)

        @block.tensor
        def _(pe):
            all_turned(pe)
            for b in range(B):
                if b >= GB:
                    pe.wait_ge(y_done, b - GB + 1)
                r = slice(b * S, (b + 1) * S)
                for c in range(C):
                    nc.tensor.matmul(ps[:, b % GB, :], lead[:, c, r], L.ternT[:, c, :], start=(c == 0), stop=False)
                    ins = nc.tensor.matmul(ps[:, b % GB, :], trail[:, c, r], L.ternT[:, c, :], start=False,
                                           stop=(c == C - 1))
                ins.then_inc(product, 1)


class Routing:
    pass


class Kept:
    pass


def operands(ph):
    return ph.sb("lead", [P, C, T], F32R), ph.sb("trail", [P, C, T], F32R)


def two_layers(nc, a, out):
    q_dram = nc.dram_tensor("q_heads", [H1, P, T], F32).ap()
    k_dram = nc.dram_tensor("k_heads", [H1, P, T], F32).ap()
    v_dram = nc.dram_tensor("v_heads", [H1, S, B, DH1], F32).ap()
    rows_dram = nc.dram_tensor("sorted_rows", [(TILES + 1) * P, D], F32).ap()
    y_dram = nc.dram_tensor("sorted_y", [TILES * P, D], F32).ap()
    with ExitStack() as stack:
        kept = lambda name, shape: stack.enter_context(nc.sbuf_tensor(name, shape, F32))
        K = Kept()
        K.x = kept("x_kept", [P, B, D])
        K.ident, K.ones = kept("ident", [P, P]), kept("ones", [P, P])
        K.eps5, K.eps6 = kept("eps5", [P, 1]), kept("eps6", [P, 1])
        K.scrap = kept("scrap", [P, 1])
        rq, rk = kept("rq", [P, B]), kept("rk", [P, B])
        K.ps = stack.enter_context(nc.psum_tensor("banks", [P, 8, 512], F32))
        R = Routing()
        R.weight = kept("weight", [P, 2, B])
        R.slot = stack.enter_context(nc.sbuf_tensor("slot", [P, 2, B], U32))
        R.expert = stack.enter_context(nc.sbuf_tensor("expert", [P, TILES + 1], U32))
        K.stats, K.mv, K.rstd = kept("stats", [P, B, 6]), kept("mv", [P, B, 2]), kept("rstd", [P, B])
        setup(nc, K)
        with Phase(nc, "of_ctx") as ph:
            lead, trail = operands(ph)
            project(nc, K, "keys", lead, trail, a["ctx_2048"], a["L1_xattn_ki_w"], a["L1_xattn_ki_b"], k_dram, rk,
                    [(K.x[:], a["x"].rearrange("b s d -> s b d"), False)])
            values(nc, K, lead, trail, a["L1_xattn_vi_w"], v_dram)
        mlstm(nc, K, a["ctx_2048"], a["L0_xattn_Wi"], a["L0_xattn_bi"], a["L0_xattn_Wf"], a["L0_xattn_bf"],
              a["L0_xattn_ln_scale"], rows_dram)
        with Phase(nc, "of_x1") as ph:
            lead, trail = operands(ph)
            normal, logits = ph.sb("normal", [P, B, D]), ph.sb("logits", [P, B, E])
            raw = ph.sb("raw", [P, SHARED])
            with Phase(nc, "turn_x1") as sub:
                block = sub.block()
                shared_weights(nc, sub, block, raw, [a[f"L0_ffn_sw_{n}"] for n in ("gate", "up", "down")])
                turn(nc, K, sub, block, sub.sb("stage", [P, 2, GB, D]), lead, trail, rms=a["L0_ffn_rms_weight"],
                     logits=logits, router=a["L0_ffn_router_w"], normal=normal)
            shared_expert(nc, K, R, lead, trail, normal, logits, rows_dram, raw)
        routed_experts(nc, K, R, rows_dram, y_dram, a["L0_ffn_rms_weight"],
                       [a[f"L0_ffn_w_{n}"] for n in ("gate", "up", "down")])
        L = LastWeights()
        L.ternT = stack.enter_context(nc.sbuf_tensor("ternT", [P, C, D], F32R))
        L.scale = kept("w_scale", [P, 1])
        combine(nc, K, R, y_dram, L, a["L1_ffn_weight"])
        with Phase(nc, "of_attend") as outer:
            A = attend_weights(outer, a["L1_xattn_o_w"], a["L1_xattn_o_b"], a["L1_xattn_vi_b"],
                               a["L1_xattn_nq_s"], a["L1_xattn_nki_s"])
            with Phase(nc, "of_x2") as ph:
                lead, trail = operands(ph)
                project(nc, K, "queries", lead, trail, None, a["L1_xattn_q_w"], a["L1_xattn_q_b"], q_dram, rq, A.loads)
            attend(nc, K, A, q_dram, k_dram, v_dram, rq, rk)
        ternary(nc, K, L, a["L1_ffn_bias"], out)


_INS = ['x', 'ctx_2048', 'L0_xattn_Wi', 'L0_xattn_bi', 'L0_xattn_Wf', 'L0_xattn_bf', 'L0_xattn_ln_scale',
        'L0_ffn_rms_weight', 'L0_ffn_router_w', 'L0_ffn_w_gate', 'L0_ffn_w_up', 'L0_ffn_w_down',
        'L0_ffn_sw_gate', 'L0_ffn_sw_up', 'L0_ffn_sw_down', 'L1_xattn_q_w', 'L1_xattn_q_b',
        'L1_xattn_ki_w', 'L1_xattn_ki_b', 'L1_xattn_vi_w', 'L1_xattn_vi_b', 'L1_xattn_o_w', 'L1_xattn_o_b',
        'L1_xattn_nq_s', 'L1_xattn_nki_s', 'L1_ffn_weight', 'L1_ffn_bias']


def kernel(**inputs):
    import concourse.bacc as bacc
    from concourse.bass_utils import run_bass_kernel_spmd

    nc = bacc.Bacc("TRN2", target_bir_lowering=False, num_devices=1)
    arrays, args = {}, {}
    for name in _INS:
        v = np.ascontiguousarray(inputs[name])
        arrays[f"in_{name}"] = v
        args[name] = nc.dram_tensor(f"in_{name}", v.shape, mybir.dt.from_np(v.dtype), kind="ExternalInput").ap()
    out = nc.dram_tensor("out", (B, S, D), F32, kind="ExternalOutput").ap()
    two_layers(nc, args, out)
    return run_bass_kernel_spmd(nc, [arrays], core_ids=[0]).results[0]["out"]
```
